# Optimizing a Trainium2 kernel written in Bass

```python
import numpy as np
import jax
import jax.numpy as jnp

def _softmax(x, axis=-1):
    return jax.nn.softmax(x, axis=axis)

def _gelu(x):
    return jax.nn.gelu(x, approximate=True)

def _silu(x):
    return jax.nn.silu(x)

def _sigmoid(x):
    return jax.nn.sigmoid(x)

def _layernorm(x, axis=-1, eps=1e-05):
    m = jnp.mean(x, axis=axis, keepdims=True)
    v = jnp.var(x, axis=axis, keepdims=True)
    return (x - m) / jnp.sqrt(v + eps)

def _scatter_add(tgt, idx, src, axis=0):
    return tgt.at[idx].add(src)

def _segment_sum(src, seg, n):
    return jax.ops.segment_sum(src, seg, n)
kernel_name = 'mk_prb_d1_jaxref_r8_c33f76'

def setup_inputs(seed: int=0):
    np.random.seed(seed)
    _w = jnp.asarray

    def _L0_attn_setup():
        import jax, jax.numpy as jnp
        import numpy as np
        import math
        N_HEAD = 16
        V_HEAD = 32
        NOPE = 32
        ROPE_D = 64
        KEEP = 32
        EPS = 1e-06

        def _freqs(T, dim=ROPE_D, theta=10000.0):
            f = 1.0 / theta ** (jnp.arange(0, dim, 2, dtype=jnp.float32) / dim)
            t = jnp.arange(T, dtype=jnp.float32)
            a = jnp.outer(t, f)
            return (jnp.cos(a), jnp.sin(a))

        def _rope(x, cos, sin):
            S = x.shape[-2]
            c = cos[:S][None, None]
            s = sin[:S][None, None]
            x1, x2 = jnp.split(x, 2, axis=-1)
            return jnp.concatenate([x1 * c - x2 * s, x1 * s + x2 * c], axis=-1)

        def _rms(x, g, eps=EPS):
            return x * jax.lax.rsqrt(jnp.mean(x * x, axis=-1, keepdims=True) + eps) * g

        def _attn(q, k, v, causal):
            scale = 1.0 / math.sqrt(q.shape[-1])
            s = jnp.einsum('bhqd,bhkd->bhqk', q, k) * scale
            if causal:
                Tq, Tk = (s.shape[-2], s.shape[-1])
                mask = jnp.tril(jnp.ones((Tq, Tk), dtype=bool))
                s = jnp.where(mask, s, jnp.finfo(s.dtype).min)
            return jnp.einsum('bhqk,bhkd->bhqd', jax.nn.softmax(s, axis=-1), v)

        def _forward(x, w_cq, g_qnorm, w_dq_nope, w_dq_rope, w_ckv, g_kvnorm, w_dk_nope, w_dv, w_krope, w_imp, w_selk, w_selv, w_wink, w_winv, w_gate, w_proj):
            B, T, C = x.shape
            cos, sin = _freqs(T)
            nq = _rms(x @ w_cq, g_qnorm)
            q_nope = (nq @ w_dq_nope).reshape(B, T, N_HEAD, NOPE).transpose(0, 2, 1, 3)
            q_rope = (nq @ w_dq_rope).reshape(B, T, N_HEAD, ROPE_D).transpose(0, 2, 1, 3)
            q_rope = _rope(q_rope, cos, sin)
            q = jnp.concatenate([q_nope, q_rope], axis=-1)
            gate = jax.nn.softmax((x @ w_gate).mean(axis=1), axis=-1)
            ckv = _rms(x @ w_ckv, g_kvnorm)
            k_nope = (ckv @ w_dk_nope).reshape(B, T, N_HEAD, NOPE).transpose(0, 2, 1, 3)
            v1 = (ckv @ w_dv).reshape(B, T, N_HEAD, V_HEAD).transpose(0, 2, 1, 3)
            k_rope = (x @ w_krope).reshape(B, T, 1, ROPE_D).transpose(0, 2, 1, 3) / N_HEAD
            k_rope = _rope(k_rope, cos, sin)
            k1 = jnp.concatenate([k_nope, jnp.broadcast_to(k_rope, (B, N_HEAD, T, ROPE_D))], axis=-1)
            scores = (x @ w_imp)[..., 0]
            _, idx = jax.lax.top_k(scores, KEEP)
            idx = jnp.sort(idx, axis=1)
            sel = jnp.take_along_axis(x, idx[:, :, None], axis=1)
            ks = (sel @ w_selk).reshape(B, KEEP, N_HEAD, NOPE + ROPE_D).transpose(0, 2, 1, 3)
            vs = (sel @ w_selv).reshape(B, KEEP, N_HEAD, V_HEAD).transpose(0, 2, 1, 3)
            ks = jnp.concatenate([ks[..., :NOPE], _rope(ks[..., NOPE:], cos, sin)], axis=-1)
            kw = (x @ w_wink).reshape(B, T, N_HEAD, NOPE + ROPE_D).transpose(0, 2, 1, 3)
            vw = (x @ w_winv).reshape(B, T, N_HEAD, V_HEAD).transpose(0, 2, 1, 3)
            kw = jnp.concatenate([kw[..., :NOPE], _rope(kw[..., NOPE:], cos, sin)], axis=-1)
            a1 = _attn(q, k1, v1, causal=True)
            a2 = _attn(q, ks, vs, causal=False)
            a3 = _attn(q, kw, vw, causal=True)
            g = gate[:, :, None, None, None]
            out = g[:, 0] * a1 + g[:, 1] * a2 + g[:, 2] * a3
            out = out.transpose(0, 2, 1, 3).reshape(B, T, N_HEAD * V_HEAD)
            return out @ w_proj
        key = jax.random.key(seed)
        ks = jax.random.split(key, 20)
        B, T, C = (2, 128, 128)
        q_lora, kv_lora = (96, 32)
        std = 0.02

        def w(k, shape):
            return jax.random.normal(k, shape, dtype=jnp.float32) * std
        return {'x': jax.random.normal(ks[0], (B, T, C), dtype=jnp.float32), 'w_cq': w(ks[1], (C, q_lora)), 'g_qnorm': jnp.ones((q_lora,), jnp.float32), 'w_dq_nope': w(ks[2], (q_lora, N_HEAD * NOPE)), 'w_dq_rope': w(ks[3], (q_lora, N_HEAD * ROPE_D)), 'w_ckv': w(ks[4], (C, kv_lora)), 'g_kvnorm': jnp.ones((kv_lora,), jnp.float32), 'w_dk_nope': w(ks[5], (kv_lora, N_HEAD * NOPE)), 'w_dv': w(ks[6], (kv_lora, N_HEAD * V_HEAD)), 'w_krope': w(ks[7], (C, ROPE_D)), 'w_imp': w(ks[8], (C, 1)), 'w_selk': w(ks[9], (C, N_HEAD * (NOPE + ROPE_D))), 'w_selv': w(ks[10], (C, N_HEAD * V_HEAD)), 'w_wink': w(ks[11], (C, N_HEAD * (NOPE + ROPE_D))), 'w_winv': w(ks[12], (C, N_HEAD * V_HEAD)), 'w_gate': w(ks[13], (C, 3)), 'w_proj': w(ks[14], (N_HEAD * V_HEAD, C))}
    _L0_attn_in = _L0_attn_setup()

    def _L0_ffn_setup():
        import jax, jax.numpy as jnp
        import numpy as np
        L, E, H, F, K = (4, 4, 128, 512, 2)
        B, S = (4, 256)
        EPS = 1e-05

        def _moe_layer(x, rw, rb, g, b, w1, b1, w2, b2):
            logits = jnp.einsum('bsh,he->bse', x, rw) + rb
            probs = jax.nn.softmax(logits, axis=-1)
            vals, idx = jax.lax.top_k(probs, K)
            vals = vals / vals.sum(axis=-1, keepdims=True)
            mu = x.mean(axis=-1, keepdims=True)
            xc = x - mu
            xhat = xc * jax.lax.rsqrt((xc * xc).mean(axis=-1, keepdims=True) + EPS)
            xe = xhat[None] * g[:, None, None, :] + b[:, None, None, :]
            h = jax.nn.gelu(jnp.einsum('ebsh,ehf->ebsf', xe, w1) + b1[:, None, None, :], approximate=False)
            y = jnp.einsum('ebsf,efh->ebsh', h, w2) + b2[:, None, None, :]
            expert_out = x[None] + y
            comb = jnp.einsum('bsk,bske->bse', vals, jax.nn.one_hot(idx, E, dtype=x.dtype))
            return jnp.einsum('bse,ebsh->bsh', comb, expert_out)
        key = jax.random.key(seed)
        ks = jax.random.split(key, 4)
        return {'hidden_states': jax.random.normal(ks[0], (B, S, H), jnp.float32), 'router_w': 0.02 * jax.random.normal(ks[1], (L, H, E), jnp.float32), 'router_b': jnp.zeros((L, E), jnp.float32), 'ln_g': jnp.ones((L, E, H), jnp.float32), 'ln_b': jnp.zeros((L, E, H), jnp.float32), 'w1': 0.02 * jax.random.normal(ks[2], (L, E, H, F), jnp.float32), 'b1': jnp.zeros((L, E, F), jnp.float32), 'w2': 0.02 * jax.random.normal(ks[3], (L, E, F, H), jnp.float32), 'b2': jnp.zeros((L, E, H), jnp.float32)}
    _L0_ffn_in = _L0_ffn_setup()
    _d = {'L0_attn_x': _L0_attn_in['x'], 'L0_attn_w_cq': _L0_attn_in['w_cq'], 'L0_attn_g_qnorm': _L0_attn_in['g_qnorm'], 'L0_attn_w_dq_nope': _L0_attn_in['w_dq_nope'], 'L0_attn_w_dq_rope': _L0_attn_in['w_dq_rope'], 'L0_attn_w_ckv': _L0_attn_in['w_ckv'], 'L0_attn_g_kvnorm': _L0_attn_in['g_kvnorm'], 'L0_attn_w_dk_nope': _L0_attn_in['w_dk_nope'], 'L0_attn_w_dv': _L0_attn_in['w_dv'], 'L0_attn_w_krope': _L0_attn_in['w_krope'], 'L0_attn_w_imp': _L0_attn_in['w_imp'], 'L0_attn_w_selk': _L0_attn_in['w_selk'], 'L0_attn_w_selv': _L0_attn_in['w_selv'], 'L0_attn_w_wink': _L0_attn_in['w_wink'], 'L0_attn_w_winv': _L0_attn_in['w_winv'], 'L0_attn_w_gate': _L0_attn_in['w_gate'], 'L0_attn_w_proj': _L0_attn_in['w_proj'], 'L0_ffn_router_w': _L0_ffn_in['router_w'], 'L0_ffn_router_b': _L0_ffn_in['router_b'], 'L0_ffn_ln_g': _L0_ffn_in['ln_g'], 'L0_ffn_ln_b': _L0_ffn_in['ln_b'], 'L0_ffn_w1': _L0_ffn_in['w1'], 'L0_ffn_b1': _L0_ffn_in['b1'], 'L0_ffn_w2': _L0_ffn_in['w2'], 'L0_ffn_b2': _L0_ffn_in['b2']}
    _x0 = _d['L0_attn_x']
    _d['L0_attn_x'] = jax.random.normal(jax.random.fold_in(jax.random.key(seed), 1), (32, 256, 128), dtype=_x0.dtype)
    del _x0
    return _d

def reference(L0_attn_x, L0_attn_w_cq, L0_attn_g_qnorm, L0_attn_w_dq_nope, L0_attn_w_dq_rope, L0_attn_w_ckv, L0_attn_g_kvnorm, L0_attn_w_dk_nope, L0_attn_w_dv, L0_attn_w_krope, L0_attn_w_imp, L0_attn_w_selk, L0_attn_w_selv, L0_attn_w_wink, L0_attn_w_winv, L0_attn_w_gate, L0_attn_w_proj, L0_ffn_router_w, L0_ffn_router_b, L0_ffn_ln_g, L0_ffn_ln_b, L0_ffn_w1, L0_ffn_b1, L0_ffn_w2, L0_ffn_b2):

    def _L0_attn_ref(x, w_cq, g_qnorm, w_dq_nope, w_dq_rope, w_ckv, g_kvnorm, w_dk_nope, w_dv, w_krope, w_imp, w_selk, w_selv, w_wink, w_winv, w_gate, w_proj):
        import jax, jax.numpy as jnp
        import numpy as np
        import math
        N_HEAD = 16
        V_HEAD = 32
        NOPE = 32
        ROPE_D = 64
        KEEP = 32
        EPS = 1e-06

        def _freqs(T, dim=ROPE_D, theta=10000.0):
            f = 1.0 / theta ** (jnp.arange(0, dim, 2, dtype=jnp.float32) / dim)
            t = jnp.arange(T, dtype=jnp.float32)
            a = jnp.outer(t, f)
            return (jnp.cos(a), jnp.sin(a))

        def _rope(x, cos, sin):
            S = x.shape[-2]
            c = cos[:S][None, None]
            s = sin[:S][None, None]
            x1, x2 = jnp.split(x, 2, axis=-1)
            return jnp.concatenate([x1 * c - x2 * s, x1 * s + x2 * c], axis=-1)

        def _rms(x, g, eps=EPS):
            return x * jax.lax.rsqrt(jnp.mean(x * x, axis=-1, keepdims=True) + eps) * g

        def _attn(q, k, v, causal):
            scale = 1.0 / math.sqrt(q.shape[-1])
            s = jnp.einsum('bhqd,bhkd->bhqk', q, k) * scale
            if causal:
                Tq, Tk = (s.shape[-2], s.shape[-1])
                mask = jnp.tril(jnp.ones((Tq, Tk), dtype=bool))
                s = jnp.where(mask, s, jnp.finfo(s.dtype).min)
            return jnp.einsum('bhqk,bhkd->bhqd', jax.nn.softmax(s, axis=-1), v)

        def _forward(x, w_cq, g_qnorm, w_dq_nope, w_dq_rope, w_ckv, g_kvnorm, w_dk_nope, w_dv, w_krope, w_imp, w_selk, w_selv, w_wink, w_winv, w_gate, w_proj):
            B, T, C = x.shape
            cos, sin = _freqs(T)
            nq = _rms(x @ w_cq, g_qnorm)
            q_nope = (nq @ w_dq_nope).reshape(B, T, N_HEAD, NOPE).transpose(0, 2, 1, 3)
            q_rope = (nq @ w_dq_rope).reshape(B, T, N_HEAD, ROPE_D).transpose(0, 2, 1, 3)
            q_rope = _rope(q_rope, cos, sin)
            q = jnp.concatenate([q_nope, q_rope], axis=-1)
            gate = jax.nn.softmax((x @ w_gate).mean(axis=1), axis=-1)
            ckv = _rms(x @ w_ckv, g_kvnorm)
            k_nope = (ckv @ w_dk_nope).reshape(B, T, N_HEAD, NOPE).transpose(0, 2, 1, 3)
            v1 = (ckv @ w_dv).reshape(B, T, N_HEAD, V_HEAD).transpose(0, 2, 1, 3)
            k_rope = (x @ w_krope).reshape(B, T, 1, ROPE_D).transpose(0, 2, 1, 3) / N_HEAD
            k_rope = _rope(k_rope, cos, sin)
            k1 = jnp.concatenate([k_nope, jnp.broadcast_to(k_rope, (B, N_HEAD, T, ROPE_D))], axis=-1)
            scores = (x @ w_imp)[..., 0]
            _, idx = jax.lax.top_k(scores, KEEP)
            idx = jnp.sort(idx, axis=1)
            sel = jnp.take_along_axis(x, idx[:, :, None], axis=1)
            ks = (sel @ w_selk).reshape(B, KEEP, N_HEAD, NOPE + ROPE_D).transpose(0, 2, 1, 3)
            vs = (sel @ w_selv).reshape(B, KEEP, N_HEAD, V_HEAD).transpose(0, 2, 1, 3)
            ks = jnp.concatenate([ks[..., :NOPE], _rope(ks[..., NOPE:], cos, sin)], axis=-1)
            kw = (x @ w_wink).reshape(B, T, N_HEAD, NOPE + ROPE_D).transpose(0, 2, 1, 3)
            vw = (x @ w_winv).reshape(B, T, N_HEAD, V_HEAD).transpose(0, 2, 1, 3)
            kw = jnp.concatenate([kw[..., :NOPE], _rope(kw[..., NOPE:], cos, sin)], axis=-1)
            a1 = _attn(q, k1, v1, causal=True)
            a2 = _attn(q, ks, vs, causal=False)
            a3 = _attn(q, kw, vw, causal=True)
            g = gate[:, :, None, None, None]
            out = g[:, 0] * a1 + g[:, 1] * a2 + g[:, 2] * a3
            out = out.transpose(0, 2, 1, 3).reshape(B, T, N_HEAD * V_HEAD)
            return out @ w_proj
        return _forward(x, w_cq, g_qnorm, w_dq_nope, w_dq_rope, w_ckv, g_kvnorm, w_dk_nope, w_dv, w_krope, w_imp, w_selk, w_selv, w_wink, w_winv, w_gate, w_proj)

    def _L0_ffn_ref(hidden_states, router_w, router_b, ln_g, ln_b, w1, b1, w2, b2):
        import jax, jax.numpy as jnp
        import numpy as np
        L, E, H, F, K = (4, 4, 128, 512, 2)
        B, S = (4, 256)
        EPS = 1e-05

        def _moe_layer(x, rw, rb, g, b, w1, b1, w2, b2):
            logits = jnp.einsum('bsh,he->bse', x, rw) + rb
            probs = jax.nn.softmax(logits, axis=-1)
            vals, idx = jax.lax.top_k(probs, K)
            vals = vals / vals.sum(axis=-1, keepdims=True)
            mu = x.mean(axis=-1, keepdims=True)
            xc = x - mu
            xhat = xc * jax.lax.rsqrt((xc * xc).mean(axis=-1, keepdims=True) + EPS)
            xe = xhat[None] * g[:, None, None, :] + b[:, None, None, :]
            h = jax.nn.gelu(jnp.einsum('ebsh,ehf->ebsf', xe, w1) + b1[:, None, None, :], approximate=False)
            y = jnp.einsum('ebsf,efh->ebsh', h, w2) + b2[:, None, None, :]
            expert_out = x[None] + y
            comb = jnp.einsum('bsk,bske->bse', vals, jax.nn.one_hot(idx, E, dtype=x.dtype))
            return jnp.einsum('bse,ebsh->bsh', comb, expert_out)
        x = hidden_states
        for l in range(L):
            x = _moe_layer(x, router_w[l], router_b[l], ln_g[l], ln_b[l], w1[l], b1[l], w2[l], b2[l])
        return x
    x = L0_attn_x
    xn = _layernorm(x, axis=-1)
    x = x + _L0_attn_ref(xn, L0_attn_w_cq, L0_attn_g_qnorm, L0_attn_w_dq_nope, L0_attn_w_dq_rope, L0_attn_w_ckv, L0_attn_g_kvnorm, L0_attn_w_dk_nope, L0_attn_w_dv, L0_attn_w_krope, L0_attn_w_imp, L0_attn_w_selk, L0_attn_w_selv, L0_attn_w_wink, L0_attn_w_winv, L0_attn_w_gate, L0_attn_w_proj) + _L0_ffn_ref(xn, L0_ffn_router_w, L0_ffn_router_b, L0_ffn_ln_g, L0_ffn_ln_b, L0_ffn_w1, L0_ffn_b1, L0_ffn_w2, L0_ffn_b2)
    return x

_drawn_inputs = setup_inputs


def setup_inputs(seed=0):
    import zlib

    import numpy as np

    out = dict(_drawn_inputs(seed))
    spreads = {'L0_attn_g_qnorm': (1.0, 0.6),
     'L0_attn_g_kvnorm': (1.0, 0.6),
     'L0_ffn_router_b': (0.0, 0.1),
     'L0_ffn_ln_g': (1.0, 0.6),
     'L0_ffn_ln_b': (0.0, 2.0),
     'L0_ffn_b1': (0.0, 0.431),
     'L0_ffn_b2': (0.0, 0.1)}
    factors = {'L0_attn_w_cq': 8.0,
     'L0_attn_w_dq_nope': 8.0,
     'L0_attn_w_dq_rope': 8.0,
     'L0_attn_w_ckv': 8.0,
     'L0_attn_w_dk_nope': 8.0,
     'L0_attn_w_dv': 8.0,
     'L0_attn_w_krope': 24.08,
     'L0_attn_w_imp': 8.0,
     'L0_attn_w_selk': 8.0,
     'L0_attn_w_selv': 8.0,
     'L0_attn_w_wink': 8.0,
     'L0_attn_w_winv': 8.0,
     'L0_attn_w_gate': 8.0,
     'L0_attn_w_proj': 8.0}
    for name, (base, spread) in spreads.items():
        noise = np.random.default_rng([zlib.crc32(name.encode()), seed]).standard_normal(out[name].shape)
        drawn = base * np.exp(spread * noise) if base else spread * noise
        out[name] = jnp.asarray(drawn.astype(out[name].dtype))
    for name, factor in factors.items():
        out[name] = (out[name] * factor).astype(out[name].dtype)
    return out
```

```python
from contextlib import ExitStack

import numpy as np
import concourse.bass as bass
from concourse import mybir

F32 = mybir.dt.float32
BF16 = mybir.dt.bfloat16
ALU = mybir.AluOpType
ACT = mybir.ActivationFunctionType
AX = mybir.AxisListType
ds = bass.ds

P = 128
B, T, C = 32, 256, 128
TILES = B * T // P
HALVES = T // P
HEADS, NOPE, ROPE, VD = 16, 32, 64, 32
HD = NOPE + ROPE
QL, KL = 96, 32
KEEP = 32
QUAD = 4
QUADS = HEADS // QUAD
NQ = B * QUADS
QW = HD + KL
SCALE = float(HD) ** -0.5
LN_EPS, RMS_EPS, MOE_EPS = 1e-5, 1e-6, 1e-5
CQ, CKV, CKR, CIMP, CGATE = 0, 96, 128, 192, 193
CROUT = 196
CALL = 200
GRP = 4
GT = GRP * HALVES
NGRP = B // GRP
LAYERS, EXPERTS, FF = 4, 4, 512
FT = FF // P
CHUNK = 4
NCH = TILES // CHUNK
GONE = -3.0e38


def shape_constants():
    f = (1.0 / np.float32(10000.0) ** (np.arange(0, ROPE, 2, dtype=np.float32) / np.float32(ROPE))).astype(np.float32)
    a = np.outer(np.arange(T, dtype=np.float32), f).astype(np.float32)
    cos, sin = np.cos(a).astype(np.float32), np.sin(a).astype(np.float32)
    return {
        "c_eye": np.eye(P, dtype=np.float32),
        "c_causal": np.triu(np.full((P, P), -1e30, np.float32), 1),
        "c_cos": np.concatenate([cos, cos], 1),
        "c_sin": np.concatenate([-sin, sin], 1),
        "c_iota": np.tile(np.arange(KEEP, dtype=np.float32), (P, 1)),
    }


def bcast(ap, n):
    return ap.unsqueeze(len(ap.shape)).to_broadcast(list(ap.shape) + [n])


class Store:
    pass


def setup(nc, a, st, ctx):
    def sem(name):
        return ctx.enter_context(nc.semaphore(name))

    tmp = ExitStack()

    def sb(name, shape, dt=F32):
        return tmp.enter_context(nc.sbuf_tensor(name, shape, dt))

    raw_rope = sb("raw_rope", [QL, HEADS * ROPE])
    raw_nope = sb("raw_nope", [QL, HEADS * NOPE])
    raw_dk = sb("raw_dk", [KL, HEADS * NOPE])
    dk_gained = sb("dk_gained", [KL, HEADS * NOPE])
    gq = sb("gq", [QL, 1])
    gq_scaled = sb("gq_scaled", [QL, 1])
    gkv = sb("gkv", [KL, 1])
    gkv_high = sb("gkv_high", [P, 1])
    nope_T = sb("nope_T", [P, QUADS, QL])
    dk_T = sb("dk_T", [P, QUADS, KL])
    causal32 = sb("causal32", [P, P])

    loaded = sem("su_loaded")
    dv_zeroed = sem("su_dv_zeroed")
    gq_ready = sem("su_gq_ready")
    dk_ready = sem("su_dk_ready")
    flipped = sem("su_flipped")
    flip_out = sem("su_flip_out")
    absorbed = sem("su_absorbed")
    wq_parts = sem("su_wq_parts")
    done = sem("su_done")
    NLOAD = 33

    with nc.Block() as block:

        @block.sync
        def _(sp):
            n = 0
            wq_, wn_ = a["w_wink"], a["w_selk"]

            def load(dst, src):
                nonlocal n
                n += 1
                sp.dma_start(dst, src).then_inc(loaded, 16)

            load(raw_rope[:], a["w_dq_rope"])
            load(raw_nope[:], a["w_dq_nope"])
            load(raw_dk[:], a["w_dk_nope"])
            load(gq[:], a["g_qnorm"].rearrange("(k o) -> k o", o=1))
            load(gkv[:], a["g_kvnorm"].rearrange("(k o) -> k o", o=1))
            load(gkv_high[P - KL:P, :], a["g_kvnorm"].rearrange("(k o) -> k o", o=1))
            load(st.eye[:], a["c_eye"])
            load(causal32[:], a["c_causal"])
            load(st.cos[:], a["c_cos"].rearrange("(h p) d -> p h d", p=P))
            load(st.sin[:], a["c_sin"].rearrange("(h p) d -> p h d", p=P))
            for j in range(GRP):
                load(st.cos_sel[KEEP * j:KEEP * (j + 1), :], a["c_cos"][0:KEEP, :])
                load(st.sin_sel[KEEP * j:KEEP * (j + 1), :], a["c_sin"][0:KEEP, :])
            load(st.iota[:], a["c_iota"])
            load(st.w_all[:, CQ:CQ + QL], a["w_cq"])
            load(st.w_all[:, CKV:CKV + KL], a["w_ckv"])
            load(st.w_all[:, CKR:CKR + ROPE], a["w_krope"])
            load(st.w_all[:, CIMP:CIMP + 1], a["w_imp"])
            load(st.w_all[:, CGATE:CGATE + 3], a["w_gate"])
            load(st.w_all[:, CROUT:CROUT + EXPERTS], a["router_w"][0])
            load(st.rb0[:], a["router_b"][0:1, :].to_broadcast([P, EXPERTS]))
            for dst, src in ((st.w_kw, a["w_wink"]), (st.w_ks, a["w_selk"])):
                v = src.rearrange("c (h d) -> c h d", d=HD)
                load(dst[:, 0:HEADS, 0:ROPE], v[:, :, NOPE:HD])
                load(dst[:, 0:HEADS, ROPE:HD], v[:, :, 0:NOPE])
            load(st.w_vw[:], a["w_winv"])
            load(st.w_vs[:], a["w_selv"])
            sp.wait_ge(dv_zeroed, 1)
            load(st.w_v1[P - KL:P, :], a["w_dv"])
            assert n == NLOAD, n

        @block.vector
        def _(dve):
            nc.vector.memset(st.w_v1[:], 0.0).then_inc(dv_zeroed, 1)
            dve.wait_ge(loaded, 16 * NLOAD)
            nc.vector.tensor_scalar(gq_scaled[:], gq[:], SCALE, None, ALU.mult).then_inc(gq_ready, 1)
            nc.vector.tensor_scalar(dk_gained[:], raw_dk[:], gkv[:], None, ALU.mult).then_inc(dk_ready, 1)
            nc.vector.tensor_copy(st.causal[:], causal32[:]).then_inc(done, 1)
            nc.vector.tensor_copy(st.eye16[:], st.eye[:]).then_inc(done, 1)
            nc.vector.tensor_scalar(st.w_all[:, CKR:CKR + ROPE], st.w_all[:, CKR:CKR + ROPE], 1.0 / HEADS, None,
                                    ALU.mult).then_inc(done, 1)
            nc.vector.tensor_scalar(st.w_v1[P - KL:P, :], st.w_v1[P - KL:P, :], gkv_high[P - KL:P, :], None,
                                    ALU.mult).then_inc(done, 1)
            dve.wait_ge(gq_ready, 1)
            nc.vector.tensor_scalar(st.w_q[:, :, 0:ROPE], raw_rope[:].rearrange("p (h d) -> p h d", d=ROPE),
                                    gq_scaled[:], None, ALU.mult).then_inc(wq_parts, 1)
            nc.vector.tensor_scalar(st.w_q[:, :, ROPE:HD], raw_nope[:].rearrange("p (h d) -> p h d", d=NOPE),
                                    gq_scaled[:], None, ALU.mult).then_inc(wq_parts, 1)
            for j in range(QUAD):
                dve.wait_ge(absorbed, j + 1)
                nc.vector.tensor_scalar(st.w_q[:, j:HEADS:QUAD, HD:QW],
                                        st.bank[2 + j][0:QL, 0:QUADS * KL].rearrange("p (g d) -> p g d", d=KL),
                                        gq_scaled[:], None, ALU.mult).then_inc(wq_parts, 1)
            dve.wait_ge(wq_parts, 2 + QUAD)

        @block.scalar
        def _(act):
            act.wait_ge(flipped, 1)
            nc.scalar.activation(nope_T[:], st.bank[0][:, 0:QUADS * QL].rearrange("p (g d) -> p g d", d=QL),
                                 ACT.Copy).then_inc(flip_out, 1)
            act.wait_ge(flipped, 2)
            nc.scalar.activation(dk_T[:], st.bank[1][:, 0:QUADS * KL].rearrange("p (g d) -> p g d", d=KL),
                                 ACT.Copy).then_inc(flip_out, 1)

        @block.tensor
        def _(pe):
            pe.wait_ge(loaded, 16 * NLOAD)
            for g in range(QUADS):
                last = nc.tensor.transpose(st.bank[0][:, g * QL:(g + 1) * QL], raw_nope[:, g * P:(g + 1) * P],
                                           st.eye[0:QL, 0:QL])
            last.then_inc(flipped, 1)
            pe.wait_ge(dk_ready, 1)
            for g in range(QUADS):
                last = nc.tensor.transpose(st.bank[1][:, g * KL:(g + 1) * KL], dk_gained[:, g * P:(g + 1) * P],
                                           st.eye[0:KL, 0:KL])
            last.then_inc(flipped, 1)
            pe.wait_ge(flip_out, 2)
            for j in range(QUAD):
                rows = slice(NOPE * j, NOPE * (j + 1))
                for g in range(QUADS):
                    last = nc.tensor.matmul(st.bank[2 + j][0:QL, g * KL:(g + 1) * KL], nope_T[rows, g, :],
                                            dk_T[rows, g, :], start=True, stop=True)
                last.then_inc(absorbed, 1)

    tmp.close()


def tokens(nc, a, st, ctx):
    def sem(name):
        return ctx.enter_context(nc.semaphore(name))

    tmp = ExitStack()

    def sb(name, shape, dt=F32):
        return tmp.enter_context(nc.sbuf_tensor(name, shape, dt))

    x = sb("tk_x", [P, GT, C])
    xc = sb("tk_xc", [P, GT, C])
    sq = sb("tk_sq", [P, GT, C])
    xn = sb("tk_xn", [P, GT, C])
    xnT = sb("tk_xnT", [P, GT, P])
    mean = sb("tk_mean", [P, GT])
    nmean = sb("tk_nmean", [P, GT])
    vsum = sb("tk_vsum", [P, GT])
    var = sb("tk_var", [P, GT])
    rstd = sb("tk_rstd", [P, GT])
    proj = sb("tk_proj", [P, GT, CALL])
    psq = sb("tk_psq", [P, GT, QL + KL])
    ssum = sb("tk_ssum", [P, 2, GT])
    smean = sb("tk_smean", [P, 2, GT])
    rrms = sb("tk_rrms", [P, 2, GT])
    rot = sb("tk_rot", [P, GT, ROPE])
    key = sb("tk_key", [P, GT, P])
    nq = sb("tk_nq", [P, GT, QL])
    keyT = sb("tk_keyT", [P, GT, P])
    nqT = sb("tk_nqT", [QL, GT, P])
    minus_half = sb("tk_minus_half", [P, 2 * GT])
    mom = sb("tk_mom", [P, 2, GT])
    msq = sb("tk_msq", [P, GT])
    vsq = sb("tk_vsq", [P, GT])

    x_in = sem("tk_x_in")
    summed = sem("tk_summed")
    mean_ready = sem("tk_mean_ready")
    centered = sem("tk_centered")
    squared = sem("tk_squared")
    vsummed = sem("tk_vsummed")
    var_ready = sem("tk_var_ready")
    half_ready = sem("tk_half_ready")
    rstd_ready = sem("tk_rstd_ready")
    xn_ready = sem("tk_xn_ready")
    xt_ps = sem("tk_xt_ps")
    xnT_ready = sem("tk_xnT_ready")
    proj_ps = sem("tk_proj_ps")
    proj_ready = sem("tk_proj_ready")
    psq_ready = sem("tk_psq_ready")
    ssummed = sem("tk_ssummed")
    smean_ready = sem("tk_smean_ready")
    rrms_ready = sem("tk_rrms_ready")
    kept = sem("tk_kept")
    rotated = sem("tk_rotated")
    key_zeroed = sem("tk_key_zeroed")
    lat_ready = sem("tk_lat_ready")
    lat_ps = sem("tk_lat_ps")
    latT_ready = sem("tk_latT_ready")
    xsq_ready = sem("tk_xsq_ready")
    mom_ready = sem("tk_mom_ready")
    mean1_ready = sem("tk_mean1_ready")
    vsq_ready = sem("tk_vsq_ready")
    xn_out = sem("tk_xn_out")
    xt_out = sem("tk_xt_out")
    lat_out = sem("tk_lat_out")

    x_dram = a["x"].rearrange("b (h p) c -> p (b h) c", p=P)
    xn_dram = st.d_xn.rearrange("t p c -> p t c")
    bk = st.bank

    def two(ap):
        return ap.rearrange("p t n -> p (t n)")

    with nc.Block() as block:

        @block.sync
        def _(sp):
            def load(i):
                sp.dma_start(x[:], x_dram[:, ds(i * GT, GT), :]).then_inc(x_in, 16)

            def store(i):
                sp.wait_ge(xn_ready, i + 1)
                sp.dma_start(xn_dram[:, ds(i * GT, GT), :], xn[:]).then_inc(xn_out, 16)
                sp.wait_ge(xnT_ready, 2 * i + 2)
                sp.dma_start(st.d_xnT[ds(i * GRP, GRP)].rearrange("b c n -> c b n"),
                             xnT[:].rearrange("p (b h) n -> p b (h n)", h=HALVES)).then_inc(xt_out, 16)
                sp.wait_ge(latT_ready, 4 * i + 4)
                sp.dma_start(st.d_kvT[ds(i * GRP, GRP)].rearrange("b c n -> c b n"),
                             keyT[:].rearrange("p (b h) n -> p b (h n)", h=HALVES)).then_inc(lat_out, 16)
                sp.dma_start(st.d_nqT[ds(i * GRP, GRP)].rearrange("b c n -> c b n"),
                             nqT[:].rearrange("p (b h) n -> p b (h n)", h=HALVES)).then_inc(lat_out, 16)

            sp.sem_inc(xn_out, 16)
            sp.sem_inc(xt_out, 16)
            sp.sem_inc(lat_out, 32)
            load(0)
            with sp.Fori(0, NGRP - 1) as i:
                sp.wait_ge(centered, i + 1)
                load(i + 1)
                store(i)
            store(NGRP - 1)
            sp.wait_ge(xn_out, 16 * NGRP + 16)
            sp.wait_ge(xt_out, 16 * NGRP + 16)
            sp.wait_ge(lat_out, 32 * NGRP + 32)

        @block.gpsimd
        def _(pool):
            nc.gpsimd.memset(minus_half[:], -0.5).then_inc(half_ready, 1)
            pool.wait_ge(half_ready, 1)
            with pool.Fori(0, NGRP) as i:
                pool.wait_ge(var_ready, i + 1)
                nc.gpsimd.tensor_tensor(rstd[:], var[:], minus_half[:, 0:GT], ALU.pow).then_inc(rstd_ready, 1)
                pool.wait_ge(smean_ready, 2 * i + 2)
                nc.gpsimd.tensor_tensor(rrms[:].rearrange("p k t -> p (k t)"), smean[:].rearrange("p k t -> p (k t)"),
                                        minus_half[:], ALU.pow).then_inc(rrms_ready, 1)

        @block.scalar
        def _(act):
            with act.Fori(0, NGRP) as i:
                act.wait_ge(centered, i + 1)
                nc.scalar.activation(sq[:], xc[:], ACT.Square).then_inc(squared, 1)
                for k in range(2):
                    act.wait_ge(xt_ps, 2 * i + k + 1)
                    if k == 0:
                        act.wait_ge(xt_out, 16 * i + 16)
                    nc.scalar.activation(two(xnT[:, 4 * k:4 * k + 4, :]), bk[k][:, :], ACT.Copy).then_inc(xnT_ready, 1)
                act.wait_ge(vsummed, i + 1)
                nc.scalar.activation(sq[:], xn[:], ACT.Square).then_inc(xsq_ready, 1)
                for k in range(4):
                    act.wait_ge(proj_ps, 4 * i + k + 1)
                    nc.scalar.activation(two(proj[:, 2 * k:2 * k + 2, :]), bk[2 + k][:, 0:2 * CALL],
                                         ACT.Copy).then_inc(proj_ready, 1)
                act.wait_ge(proj_ready, 4 * i + 4)
                nc.scalar.activation(psq[:], proj[:, :, 0:QL + KL], ACT.Square).then_inc(psq_ready, 1)
                for k in range(4):
                    act.wait_ge(lat_ps, 4 * i + k + 1)
                    if k == 0:
                        act.wait_ge(lat_out, 32 * i + 32)
                    if k < 2:
                        nc.scalar.activation(two(keyT[:, 4 * k:4 * k + 4, :]), bk[k][:, :],
                                             ACT.Copy).then_inc(latT_ready, 1)
                    else:
                        nc.scalar.activation(two(nqT[:, 4 * k - 8:4 * k - 4, :]), bk[k][0:QL, :],
                                             ACT.Copy).then_inc(latT_ready, 1)

        @block.vector
        def _(dve):
            nc.vector.memset(key[:], 0.0).then_inc(key_zeroed, 1)
            dve.wait_ge(key_zeroed, 1)
            with dve.Fori(0, NGRP) as i:
                dve.wait_ge(x_in, 16 * i + 16)
                nc.vector.reduce_sum(mean[:], x[:], axis=AX.X).then_inc(summed, 1)
                dve.wait_ge(summed, i + 1)
                nc.vector.tensor_scalar(nmean[:], mean[:], 1.0 / C, None, ALU.mult).then_inc(mean_ready, 1)
                dve.wait_ge(mean_ready, i + 1)
                nc.vector.tensor_tensor(xc[:], x[:], bcast(nmean[:], C), ALU.subtract).then_inc(centered, 1)
                dve.wait_ge(squared, i + 1)
                nc.vector.reduce_sum(vsum[:], sq[:], axis=AX.X).then_inc(vsummed, 1)
                dve.wait_ge(vsummed, i + 1)
                nc.vector.tensor_scalar(var[:], vsum[:], 1.0 / C, LN_EPS, ALU.mult, ALU.add).then_inc(var_ready, 1)
                dve.wait_ge(rstd_ready, i + 1)
                dve.wait_ge(xn_out, 16 * i + 16)
                nc.vector.tensor_tensor(xn[:], xc[:], bcast(rstd[:], C), ALU.mult).then_inc(xn_ready, 1)
                dve.wait_ge(proj_ready, 4 * i + 4)
                nc.vector.tensor_copy(st.imp[:, :, ds(i * GRP, GRP)],
                                      proj[:, :, CIMP].rearrange("p (b h) -> p h b", h=HALVES)).then_inc(kept, 1)
                for h in range(HALVES):
                    nc.vector.tensor_copy(st.gl[:, h, ds(i * GRP, GRP), :],
                                          proj[:, h:GT:HALVES, CGATE:CGATE + 3]).then_inc(kept, 1)
                nc.vector.tensor_tensor(st.logits[:, ds(i * GT, GT), :], proj[:, :, CROUT:CROUT + EXPERTS],
                                        st.rb0[:].unsqueeze(1).to_broadcast([P, GT, EXPERTS]), ALU.add)\
                    .then_inc(kept, 1)
                nc.vector.reduce_sum(mom[:, 0, :], xn[:], axis=AX.X).then_inc(mom_ready, 1)
                dve.wait_ge(xsq_ready, i + 1)
                nc.vector.reduce_sum(mom[:, 1, :], sq[:], axis=AX.X).then_inc(mom_ready, 1)
                dve.wait_ge(mom_ready, 2 * i + 2)
                nc.vector.tensor_scalar(st.mv[:, ds(i * GT, GT), 0], mom[:, 0, :], 1.0 / C, None,
                                        ALU.mult).then_inc(mean1_ready, 1)
                nc.vector.tensor_tensor(msq[:], mom[:, 0, :], mom[:, 0, :], ALU.mult).then_inc(mean1_ready, 1)
                dve.wait_ge(mean1_ready, 2 * i + 2)
                nc.vector.scalar_tensor_tensor(vsq[:], msq[:], -1.0 / C, mom[:, 1, :], ALU.mult,
                                               ALU.add).then_inc(vsq_ready, 1)
                dve.wait_ge(vsq_ready, i + 1)
                nc.vector.tensor_scalar(st.mv[:, ds(i * GT, GT), 1], vsq[:], 1.0 / C, None, ALU.mult).then_inc(kept, 1)
                dve.wait_ge(psq_ready, i + 1)
                nc.vector.reduce_sum(ssum[:, 0, :], psq[:, :, 0:QL], axis=AX.X).then_inc(ssummed, 1)
                nc.vector.reduce_sum(ssum[:, 1, :], psq[:, :, QL:QL + KL], axis=AX.X).then_inc(ssummed, 1)
                dve.wait_ge(ssummed, 2 * i + 1)
                nc.vector.tensor_scalar(smean[:, 0, :], ssum[:, 0, :], 1.0 / QL, RMS_EPS, ALU.mult,
                                        ALU.add).then_inc(smean_ready, 1)
                dve.wait_ge(ssummed, 2 * i + 2)
                nc.vector.tensor_scalar(smean[:, 1, :], ssum[:, 1, :], 1.0 / KL, RMS_EPS, ALU.mult,
                                        ALU.add).then_inc(smean_ready, 1)
                halves = proj[:, :, CKR:CKR + ROPE].rearrange("p (b h) d -> p b h d", h=HALVES)
                rk = rot[:].rearrange("p (b h) d -> p b h d", h=HALVES)
                hr = ROPE // 2
                for h in range(HALVES):
                    def tab(t, lo, hi):
                        return t[:, h:h + 1, lo:hi].to_broadcast([P, GRP, hi - lo])
                    nc.vector.tensor_tensor(rk[:, :, h, 0:hr], halves[:, :, h, hr:ROPE], tab(st.sin, 0, hr),
                                            ALU.mult).then_inc(rotated, 1)
                    nc.vector.tensor_tensor(rk[:, :, h, hr:ROPE], halves[:, :, h, 0:hr], tab(st.sin, hr, ROPE),
                                            ALU.mult).then_inc(rotated, 1)
                    nc.vector.tensor_tensor(key[:, h:GT:HALVES, 0:ROPE], halves[:, :, h, :], tab(st.cos, 0, ROPE),
                                            ALU.mult).then_inc(rotated, 1)
                dve.wait_ge(rotated, 6 * i + 6)
                nc.vector.tensor_tensor(key[:, :, 0:ROPE], key[:, :, 0:ROPE], rot[:], ALU.add).then_inc(lat_ready, 1)
                dve.wait_ge(rrms_ready, i + 1)
                nc.vector.tensor_tensor(key[:, :, P - KL:P], proj[:, :, CKV:CKV + KL], bcast(rrms[:, 1, :], KL),
                                        ALU.mult).then_inc(lat_ready, 1)
                nc.vector.tensor_tensor(nq[:], proj[:, :, CQ:CQ + QL], bcast(rrms[:, 0, :], QL),
                                        ALU.mult).then_inc(lat_ready, 1)

        @block.tensor
        def _(pe):
            with pe.Fori(0, NGRP) as i:
                pe.wait_ge(xn_ready, i + 1)
                for t in range(GT):
                    last = nc.tensor.transpose(bk[t // 4][:, (t % 4) * P:(t % 4 + 1) * P], xn[:, t, :], st.eye[:])
                    if t % 4 == 3:
                        last.then_inc(xt_ps, 1)
                for t in range(GT):
                    if t % 4 == 0:
                        pe.wait_ge(xnT_ready, 2 * i + t // 4 + 1)
                    last = nc.tensor.matmul(bk[2 + t // 2][:, (t % 2) * CALL:(t % 2 + 1) * CALL], xnT[:, t, :],
                                            st.w_all[:], start=True, stop=True)
                    if t % 2 == 1:
                        last.then_inc(proj_ps, 1)
                pe.wait_ge(lat_ready, 3 * i + 3)
                for t in range(GT):
                    last = nc.tensor.transpose(bk[t // 4][:, (t % 4) * P:(t % 4 + 1) * P], key[:, t, :], st.eye[:])
                    if t % 4 == 3:
                        last.then_inc(lat_ps, 1)
                for t in range(GT):
                    last = nc.tensor.transpose(bk[2 + t // 4][0:QL, (t % 4) * P:(t % 4 + 1) * P], nq[:, t, :],
                                               st.eye[:])
                    if t % 4 == 3:
                        last.then_inc(lat_ps, 1)

    tmp.close()


def choose(nc, a, st, ctx):
    def sem(name):
        return ctx.enter_context(nc.semaphore(name))

    tmp = ExitStack()

    def sb(name, shape, dt=F32):
        return tmp.enter_context(nc.sbuf_tensor(name, shape, dt))

    left = sb("ch_left", [B, 2, T])
    top = sb("ch_top", [B, 8])
    taken = sb("ch_taken", [B, T])
    rank = sb("ch_rank", [B, T])
    place = sb("ch_place", [B, T])
    place1 = sb("ch_place1", [B, T])
    ones = sb("ch_ones", [B, T])
    mean_w = sb("ch_mean_w", [P, P])
    gm = sb("ch_gm", [P, B])
    gd = sb("ch_gd", [P, B, 3])
    ge = sb("ch_ge", [P, B, 3])
    gs = sb("ch_gs", [P, B])
    gr = sb("ch_gr", [P, B])
    bk = st.bank

    imp_T = sem("ch_imp_T")
    step = sem("ch_vector_step")
    mean_ready = sem("ch_mean_ready")
    place_ready = sem("ch_place_ready")
    place_T = sem("ch_place_T")
    gate_ps = sem("ch_gate_ps")
    gate_off = sem("ch_gate_off")
    gate_exp = sem("ch_gate_exp")

    with nc.Block() as block:

        @block.tensor
        def _(pe):
            for h in range(HALVES):
                last = nc.tensor.transpose(bk[0][0:B, h * P:(h + 1) * P], st.imp[:, h, :], st.eye[:])
            last.then_inc(imp_T, 1)
            pe.wait_ge(mean_ready, 1)
            for h in range(HALVES):
                last = nc.tensor.matmul(bk[1][:, 0:B * 3], mean_w[:], st.gl[:, h].rearrange("p b k -> p (b k)"),
                                        start=(h == 0), stop=(h == HALVES - 1))
            last.then_inc(gate_ps, 1)
            pe.wait_ge(place_ready, 1)
            for h in range(HALVES):
                last = nc.tensor.transpose(bk[2][:, h * B:(h + 1) * B], place1[:, h * P:(h + 1) * P],
                                           st.eye[0:B, 0:B])
            last.then_inc(place_T, 1)

        @block.vector
        def _(dve):
            n = 0

            def after(ins):
                nonlocal n
                n += 1
                ins.then_inc(step, 1)
                dve.wait_ge(step, n)

            nc.vector.memset(mean_w[:], 1.0 / T).then_inc(mean_ready, 1)
            after(nc.vector.memset(ones[:], 1.0))
            dve.wait_ge(imp_T, 1)
            after(nc.vector.tensor_copy(left[:, 0, :], bk[0][0:B, 0:T]))
            for r in range(KEEP // 8):
                after(nc.vector.max(top[:], left[:, r % 2, :]))
                after(nc.vector.match_replace(left[:, (r + 1) % 2, :], top[:], left[:, r % 2, :], GONE))
            after(nc.vector.tensor_scalar(taken[:], left[:, 0, :], GONE, None, ALU.is_equal))
            after(nc.vector.tensor_tensor_scan(rank[:], ones[:], taken[:], 0.0, ALU.mult, ALU.add))
            after(nc.vector.tensor_tensor(place[:], rank[:], taken[:], ALU.mult))
            nc.vector.tensor_scalar(place1[:], place[:], -1.0, None, ALU.add).then_inc(place_ready, 1)
            dve.wait_ge(gate_ps, 1)
            gl = bk[1][:, 0:B * 3].rearrange("p (b k) -> p b k", k=3)
            after(nc.vector.reduce_max(gm[:], gl, axis=AX.X))
            nc.vector.tensor_tensor(gd[:], gl, bcast(gm[:], 3), ALU.subtract).then_inc(gate_off, 1)
            dve.wait_ge(gate_exp, 1)
            after(nc.vector.reduce_sum(gs[:], ge[:], axis=AX.X))
            after(nc.vector.reciprocal(gr[:], gs[:]))
            after(nc.vector.tensor_tensor(st.gates[:], ge[:], bcast(gr[:], 3), ALU.mult))
            dve.wait_ge(place_T, 1)
            after(nc.vector.tensor_copy(st.place[:].rearrange("p b h -> p h b"),
                                        bk[2][:, 0:HALVES * B].rearrange("p (h b) -> p h b", b=B)))

        @block.scalar
        def _(act):
            act.wait_ge(gate_off, 1)
            nc.scalar.activation(ge[:], gd[:], ACT.Exp).then_inc(gate_exp, 1)

    tmp.close()


def selected(nc, a, st, ctx):
    def sem(name):
        return ctx.enter_context(nc.semaphore(name))

    tmp = ExitStack()

    def sb(name, shape, dt=F32):
        return tmp.enter_context(nc.sbuf_tensor(name, shape, dt))

    xn = sb("se_xn", [P, GT, C])
    pick = sb("se_pick", [P, GT, KEEP])
    selT = sb("se_selT", [P, P])
    keys = sb("se_keys", [P, HEADS, HD])
    rot = sb("se_rot", [P, HEADS, ROPE])
    keysT = sb("se_keysT", [HD, GRP, HEADS, KEEP])
    vals = sb("se_vals", [P, GRP, QUADS, QUAD * (VD + 1)])
    bk = st.bank

    xn_in = sem("se_xn_in")
    picked = sem("se_picked")
    sel_ps = sem("se_sel_ps")
    selT_ready = sem("se_selT_ready")
    keys_ps = sem("se_keys_ps")
    roped = sem("se_roped")
    rot_ready = sem("se_rot_ready")
    keys_ready = sem("se_keys_ready")
    keysT_ps = sem("se_keysT_ps")
    keysT_ready = sem("se_keysT_ready")
    vals_ps = sem("se_vals_ps")
    vals_init = sem("se_vals_init")
    vals_ready = sem("se_vals_ready")
    keys_out = sem("se_keys_out")
    vals_out = sem("se_vals_out")
    xn_dram = st.d_xn.rearrange("t p c -> p t c")
    hr = ROPE // 2

    with nc.Block() as block:

        @block.sync
        def _(sp):
            def load(i):
                sp.dma_start(xn[:], xn_dram[:, ds(i * GT, GT), :]).then_inc(xn_in, 16)

            def store(i):
                sp.wait_ge(vals_ready, QUAD * GRP * (i + 2))
                quads = ds(i * GRP * QUADS, GRP * QUADS)
                sp.dma_start(st.d_vs[quads].rearrange("q p n -> p q n"),
                             vals[:].rearrange("p b g n -> p (b g) n")).then_inc(vals_out, 16)
                sp.wait_ge(keysT_ready, QUADS * (i + 2))
                sp.dma_start(st.d_ks[quads].rearrange("q p n -> p q n"),
                             keysT[:].rearrange("p b (g h) n -> p (b g) (h n)", g=QUADS)).then_inc(keys_out, 16)

            sp.sem_inc(keys_out, 16)
            sp.sem_inc(vals_out, 16)
            load(0)
            with sp.Fori(0, NGRP - 1) as i:
                sp.wait_ge(sel_ps, i + 1)
                load(i + 1)
                store(i)
            store(NGRP - 1)
            sp.wait_ge(keys_out, 16 * NGRP + 16)
            sp.wait_ge(vals_out, 16 * NGRP + 16)

        @block.vector
        def _(dve):
            nc.vector.memset(vals[:], 0.0).then_inc(vals_init, 1)
            dve.wait_ge(vals_init, 1)
            for j in range(QUAD):
                nc.vector.memset(vals[KEEP * j:KEEP * (j + 1), :, :, j * (VD + 1) + VD:(j + 1) * (VD + 1)],
                                 1.0).then_inc(vals_init, 1)
            dve.wait_ge(vals_init, 1 + QUAD)
            with dve.Fori(0, NGRP) as i:
                nc.vector.tensor_tensor(pick[:], st.iota[:].unsqueeze(1).to_broadcast([P, GT, KEEP]),
                                        bcast(st.place[:, ds(i * GRP, GRP), :].rearrange("p b h -> p (b h)"), KEEP),
                                        ALU.is_equal).then_inc(picked, 1)
                dve.wait_ge(sel_ps, i + 1)
                nc.vector.tensor_copy(selT[:], bk[0][:, 0:P]).then_inc(selT_ready, 1)
                for g in range(QUADS):
                    dve.wait_ge(keys_ps, QUADS * i + g + 1)
                    k = bk[1 + g][:, 0:QUAD * HD].rearrange("p (h d) -> p h d", d=HD)
                    hs = slice(QUAD * g, QUAD * (g + 1))

                    def tab(t, lo, hi):
                        return t[:, lo:hi].unsqueeze(1).to_broadcast([P, QUAD, hi - lo])
                    nc.vector.tensor_tensor(rot[:, hs, 0:hr], k[:, :, hr:ROPE], tab(st.sin_sel, 0, hr),
                                            ALU.mult).then_inc(rot_ready, 1)
                    nc.vector.tensor_tensor(rot[:, hs, hr:ROPE], k[:, :, 0:hr], tab(st.sin_sel, hr, ROPE),
                                            ALU.mult).then_inc(rot_ready, 1)
                    nc.vector.tensor_tensor(keys[:, hs, 0:ROPE], k[:, :, 0:ROPE], tab(st.cos_sel, 0, ROPE),
                                            ALU.mult).then_inc(rot_ready, 1)
                    nc.vector.tensor_copy(keys[:, hs, ROPE:HD], k[:, :, ROPE:HD]).then_inc(roped, 1)
                    dve.wait_ge(rot_ready, 3 * (QUADS * i + g + 1))
                    nc.vector.tensor_tensor(keys[:, hs, 0:ROPE], keys[:, hs, 0:ROPE], rot[:, hs, :],
                                            ALU.add).then_inc(keys_ready, 1)

        @block.scalar
        def _(act):
            act.sem_inc(vals_ready, QUAD * GRP)
            act.sem_inc(keysT_ready, QUADS)
            act.wait_ge(vals_init, 1 + QUAD)
            with act.Fori(0, NGRP) as i:
                act.wait_ge(vals_ps, i + 1)
                act.wait_ge(vals_out, 16 * i + 16)
                pv = bk[5][:, :].rearrange("p (g h d) -> p g h d", g=QUADS, h=QUAD)
                for b in range(GRP):
                    for j in range(QUAD):
                        nc.scalar.activation(vals[KEEP * j:KEEP * (j + 1), b, :, j * (VD + 1):j * (VD + 1) + VD],
                                             pv[KEEP * b:KEEP * (b + 1), :, j, :], ACT.Copy).then_inc(vals_ready, 1)
                act.wait_ge(keys_out, 16 * i + 16)
                for g in range(QUADS):
                    act.wait_ge(keysT_ps, QUADS * i + g + 1)
                    nc.scalar.activation(keysT[:, :, QUAD * g:QUAD * (g + 1), :].rearrange("p b h j -> p h b j"),
                                         bk[1 + g][0:HD, :].rearrange("p (h b j) -> p h b j", h=QUAD, b=GRP),
                                         ACT.Copy).then_inc(keysT_ready, 1)

        @block.tensor
        def _(pe):
            with pe.Fori(0, NGRP) as i:
                pe.wait_ge(xn_in, 16 * i + 16)
                pe.wait_ge(picked, i + 1)
                for b in range(GRP):
                    for h in range(HALVES):
                        last = nc.tensor.matmul(bk[0][:, b * KEEP:(b + 1) * KEEP], xn[:, b * HALVES + h, :],
                                                pick[:, b * HALVES + h, :], start=(h == 0), stop=(h == HALVES - 1))
                last.then_inc(sel_ps, 1)
                pe.wait_ge(selT_ready, i + 1)
                pe.wait_ge(vals_ready, QUAD * GRP * (i + 1))
                nc.tensor.matmul(bk[5][:, :], selT[:], st.w_vs[:], start=True, stop=True).then_inc(vals_ps, 1)
                for g in range(QUADS):
                    pe.wait_ge(keysT_ready, QUADS * i + g + 1)
                    nc.tensor.matmul(bk[1 + g][:, 0:QUAD * HD], selT[:],
                                     st.w_ks[:, QUAD * g:QUAD * (g + 1), :].rearrange("p h d -> p (h d)"),
                                     start=True, stop=True).then_inc(keys_ps, 1)
                for g in range(QUADS):
                    pe.wait_ge(keys_ready, QUADS * i + g + 1)
                    for j in range(QUAD):
                        last = nc.tensor.transpose(bk[1 + g][0:HD, j * P:(j + 1) * P], keys[:, QUAD * g + j, :],
                                                   st.eye[:])
                    last.then_inc(keysT_ps, 1)

    tmp.close()


def attention(nc, a, st, ctx):
    def sem(name):
        return ctx.enter_context(nc.semaphore(name))

    tmp = ExitStack()

    def sb(name, shape, dt=F32):
        return tmp.enter_context(nc.sbuf_tensor(name, shape, dt))

    UNITS = QUAD * HALVES
    VW = VD + 1
    hr = ROPE // 2
    nqT = sb("at_nqT", [QL, T])
    xnT = sb("at_xnT", [P, T])
    latT = sb("at_latT", [P, T])
    keys = sb("at_keys", [P, 1 + QUAD, T])
    qT = sb("at_qT", [P, QUAD, T])
    ksel = sb("at_ksel", [HD, QUAD * KEEP])
    vsel = sb("at_vsel", [P, QUAD * VW])
    vals = sb("at_vals", [P, HALVES, 2, QUAD, VW])
    q_tok = sb("at_q_tok", [P, HALVES, QUAD, QW])
    k_tok = sb("at_k_tok", [P, HALVES, QUAD, HD])
    q_rot = sb("at_q_rot", [P, HALVES, QUAD, ROPE])
    k_rot = sb("at_k_rot", [P, HALVES, QUAD, ROPE])
    prob = sb("at_prob", [P, 2, 2 * T])
    probT = sb("at_probT", [P, 2, 2 * T])
    nmax = sb("at_nmax", [P, UNITS, 2])
    max2 = sb("at_max2", [P, HALVES * QUAD])
    off2 = sb("at_off2", [P, HALVES * QUAD, KEEP])
    prob2 = sb("at_prob2", [P, HALVES, QUAD * KEEP])
    prob2T = sb("at_prob2T", [P, HALVES, P])
    inv = sb("at_inv", [P, HALVES, 3, QUAD])
    share = sb("at_share", [P, HALVES, 3, QUAD])
    part = sb("at_part", [P, HALVES, 3, QUAD * VD])
    part12 = sb("at_part12", [P, HALVES, QUAD * VD])
    o = sb("at_o", [P, HALVES, QUAD * VD])

    S = st.bank[0:2]
    PT = st.bank[2:4]
    O = st.bank[4:6]
    M = st.bank[6:8]

    nq_in = sem("at_nq_in")
    tok_in = sem("at_tok_in")
    shared_in = sem("at_shared_in")
    ksel_in = sem("at_ksel_in")
    vsel_in = sem("at_vsel_in")
    s_ps = sem("at_s_ps")
    s2_ps = sem("at_s2_ps")
    q_ps = sem("at_q_ps")
    k_ps = sem("at_k_ps")
    heads_ps = sem("at_heads_ps")
    v_ps = sem("at_v_ps")
    pT_ps = sem("at_pT_ps")
    p2T_ps = sem("at_p2T_ps")
    av2_done = sem("at_av2_done")
    av_done = sem("at_av_done")
    q_taken = sem("at_q_taken")
    k_taken = sem("at_k_taken")
    q_roped = sem("at_q_roped")
    k_roped = sem("at_k_roped")
    heads_ready = sem("at_heads_ready")
    v_ready = sem("at_v_ready")
    nmax_ready = sem("at_nmax_ready")
    max2_ready = sem("at_max2_ready")
    s2_taken = sem("at_s2_taken")
    p_ready = sem("at_p_ready")
    p2_ready = sem("at_p2_ready")
    pT_ready = sem("at_pT_ready")
    p2T_ready = sem("at_p2T_ready")
    inv_ready = sem("at_inv_ready")
    share_ready = sem("at_share_ready")
    o_taken = sem("at_o_taken")
    o_sum12 = sem("at_o_sum12")
    o_ready = sem("at_o_ready")
    o_out = sem("at_o_out")
    init = sem("at_init")

    def unit_keys(u):
        return P * (u % HALVES + 1)

    with nc.Block() as block:

        @block.sync
        def _(sp):
            def batch(q):
                return (q % NQ) // QUADS

            def load_nq(q):
                sp.dma_start(nqT[:], st.d_nqT[ds(batch(q), 1)].rearrange("b c n -> c (b n)")).then_inc(nq_in, 16)

            def load_tok(q):
                sp.dma_start(xnT[:], st.d_xnT[ds(batch(q), 1)].rearrange("b c n -> c (b n)")).then_inc(tok_in, 16)
                sp.dma_start(latT[:], st.d_kvT[ds(batch(q), 1)].rearrange("b c n -> c (b n)")).then_inc(tok_in, 16)

            def load_shared(q):
                sp.dma_start(keys[:, 0, :],
                             st.d_kvT[ds(batch(q), 1)].rearrange("b c n -> c (b n)")).then_inc(shared_in, 16)

            def load_ksel(q):
                sp.dma_start(ksel[:], st.d_ks[ds(q % NQ, 1)].rearrange("o p n -> p (o n)")).then_inc(ksel_in, 16)

            def load_vsel(q):
                sp.dma_start(vsel[:], st.d_vs[ds(q % NQ, 1)].rearrange("o p n -> p (o n)")).then_inc(vsel_in, 16)

            sp.sem_inc(o_out, 16)
            load_nq(0)
            load_tok(0)
            load_shared(0)
            load_ksel(0)
            load_vsel(0)
            sp.wait_ge(q_ps, HALVES)
            load_nq(1)
            sp.wait_ge(v_ps, HALVES)
            load_tok(1)
            with sp.Fori(0, NQ) as i:
                sp.wait_ge(s2_ps, i + 1)
                load_ksel(i + 1)
                sp.wait_ge(av2_done, i + 1)
                load_vsel(i + 1)
                sp.wait_ge(q_ps, HALVES * (i + 2))
                load_nq(i + 2)
                sp.wait_ge(s_ps, UNITS * (i + 1))
                load_shared(i + 1)
                sp.wait_ge(v_ps, HALVES * (i + 2))
                load_tok(i + 2)
                sp.wait_ge(o_ready, i + 1)
                sp.dma_start(st.d_o[ds((i // QUADS) * HALVES, HALVES), :, ds((i % QUADS) * QUAD * VD, QUAD * VD)]
                             .rearrange("h p n -> p h n"), o[:]).then_inc(o_out, 16)
            sp.wait_ge(o_out, 16 * (NQ + 1))
            sp.wait_ge(nq_in, 16 * (NQ + 2))
            sp.wait_ge(tok_in, 32 * (NQ + 2))
            sp.wait_ge(shared_in, 16 * (NQ + 1))
            sp.wait_ge(ksel_in, 16 * (NQ + 1))
            sp.wait_ge(vsel_in, 16 * (NQ + 1))

        @block.gpsimd
        def _(pool):
            def rope(q):
                for t in range(HALVES):
                    pool.wait_ge(q_taken, HALVES * q + t + 1)
                    nc.gpsimd.tensor_tensor(q_tok[:, t, :, 0:ROPE], q_tok[:, t, :, 0:ROPE], q_rot[:, t],
                                            ALU.add).then_inc(q_roped, 1)
                    pool.wait_ge(k_taken, HALVES * q + t + 1)
                    nc.gpsimd.tensor_tensor(k_tok[:, t, :, 0:ROPE], k_tok[:, t, :, 0:ROPE], k_rot[:, t],
                                            ALU.add).then_inc(k_roped, 1)

            rope(0)
            with pool.Fori(0, NQ) as i:
                rope(i + 1)
                pool.wait_ge(o_taken, i + 2)
                nc.gpsimd.tensor_tensor(part12[:], part[:, :, 0, :], part[:, :, 1, :], ALU.add).then_inc(o_sum12, 1)
                pool.wait_ge(o_sum12, i + 1)
                pool.wait_ge(o_out, 16 * (i + 1))
                nc.gpsimd.tensor_tensor(o[:], part12[:], part[:, :, 2, :], ALU.add).then_inc(o_ready, 1)

        @block.vector
        def _(dve):
            def rope_of(ps, tok, rot, t, width, taken):
                v = ps.rearrange("p (h d) -> p h d", d=width)

                def tab(x, lo, hi):
                    return x[:, t, lo:hi].unsqueeze(1).to_broadcast([P, QUAD, hi - lo])
                nc.vector.tensor_tensor(rot[:, t, :, 0:hr], v[:, :, hr:ROPE], tab(st.sin, 0, hr), ALU.mult)
                nc.vector.tensor_tensor(rot[:, t, :, hr:ROPE], v[:, :, 0:hr], tab(st.sin, hr, ROPE), ALU.mult)
                nc.vector.tensor_copy(tok[:, t, :, ROPE:width], v[:, :, ROPE:width])
                nc.vector.tensor_tensor(tok[:, t, :, 0:ROPE], v[:, :, 0:ROPE], tab(st.cos, 0, ROPE),
                                        ALU.mult).then_inc(taken, 1)

            def rope_q(q, t):
                dve.wait_ge(q_ps, HALVES * q + t + 1)
                rope_of(M[1 - t][:, 0:QUAD * QW], q_tok, q_rot, t, QW, q_taken)

            def rope_k(q, t):
                dve.wait_ge(k_ps, HALVES * q + t + 1)
                rope_of(M[t][:, 0:QUAD * HD], k_tok, k_rot, t, HD, k_taken)

            def unit_max(i, u):
                dve.wait_ge(s_ps, UNITS * i + u + 1)
                nc.vector.tensor_reduce(nmax[:, u, :],
                                        S[u % 2][:, 0:2 * unit_keys(u)].rearrange("p (a k) -> p a k", a=2),
                                        AX.X, ALU.max, negate=True).then_inc(nmax_ready, 1)

            nc.vector.memset(keys[:, 1:1 + QUAD, :], 0.0).then_inc(init, 1)
            nc.vector.memset(vals[:], 1.0).then_inc(init, 1)
            dve.sem_inc(o_taken, 1)
            for t in range(HALVES):
                rope_q(0, t)
                rope_k(0, t)
            with dve.Fori(0, NQ) as i:
                unit_max(i, 0)
                dve.wait_ge(s2_ps, i + 1)
                s2 = M[0][:, 0:HALVES * QUAD * KEEP].rearrange("p (n k) -> p n k", k=KEEP)
                nc.vector.reduce_max(max2[:], s2, axis=AX.X).then_inc(max2_ready, 1)
                dve.wait_ge(max2_ready, i + 1)
                nc.vector.tensor_tensor(off2[:], s2, bcast(max2[:], KEEP), ALU.subtract).then_inc(s2_taken, 1)
                rope_q(i + 1, 0)
                unit_max(i, 1)
                rope_k(i + 1, 0)
                unit_max(i, 2)
                rope_q(i + 1, 1)
                unit_max(i, 3)
                rope_k(i + 1, 1)
                for u in range(4, UNITS):
                    unit_max(i, u)
                dve.wait_ge(av_done, UNITS * (i + 1))
                ov = st.psum[:, 4:6, 0:3 * QUAD * VW].rearrange("p q (n d) -> p q n d", d=VW)
                nc.vector.reciprocal(inv[:].rearrange("p q k h -> p q (k h)"), ov[:, :, :, VD]).then_inc(inv_ready, 1)
                dve.wait_ge(inv_ready, i + 1)
                gate = st.gates[:, ds(i // QUADS, 1), :]
                for t in range(HALVES):
                    nc.vector.tensor_tensor(share[:, t], inv[:, t],
                                            gate.rearrange("p o k -> p (o k)").unsqueeze(2).to_broadcast([P, 3, QUAD]),
                                            ALU.mult).then_inc(share_ready, 1)
                dve.wait_ge(share_ready, HALVES * (i + 1))
                nc.vector.tensor_tensor(part[:].rearrange("p q k (h d) -> p q (k h) d", d=VD), ov[:, :, :, 0:VD],
                                        bcast(share[:].rearrange("p q k h -> p q (k h)"), VD),
                                        ALU.mult).then_inc(o_taken, 1)

        @block.scalar
        def _(act):
            def unit_exp(i, u):
                act.wait_ge(nmax_ready, UNITS * i + u + 1)
                n = unit_keys(u)
                for k in range(2):
                    last = nc.scalar.activation(prob[:, u % 2, k * n:(k + 1) * n], S[u % 2][:, k * n:(k + 1) * n],
                                                ACT.Exp, bias=nmax[:, u, k:k + 1])
                last.then_inc(p_ready, 1)

            def unit_probT(i, u):
                act.wait_ge(pT_ps, UNITS * i + u + 1)
                n = 2 * unit_keys(u)
                nc.scalar.activation(probT[:, u % 2, 0:n], PT[u % 2][:, 0:n], ACT.Copy).then_inc(pT_ready, 1)

            def head(q, h):
                act.wait_ge(heads_ps, QUAD * q + h + 1)
                nc.scalar.activation(qT[:, h, :], M[h % 2][:, 0:T], ACT.Copy)
                nc.scalar.activation(keys[0:HD, 1 + h, :], M[h % 2][0:HD, T:2 * T], ACT.Copy).then_inc(heads_ready, 1)

            def values(q, t):
                act.wait_ge(v_ps, HALVES * q + t + 1)
                nc.scalar.activation(vals[:, t, :, :, 0:VD],
                                     M[t][:, 0:2 * QUAD * VD].rearrange("p (k h d) -> p k h d", k=2, h=QUAD),
                                     ACT.Copy).then_inc(v_ready, 1)

            act.wait_ge(init, 2)
            for h in range(QUAD):
                head(0, h)
            for t in range(HALVES):
                values(0, t)
            with act.Fori(0, NQ) as i:
                unit_exp(i, 0)
                act.wait_ge(s2_taken, i + 1)
                nc.scalar.activation(prob2[:].rearrange("p q n -> p (q n)"), off2[:].rearrange("p n k -> p (n k)"),
                                     ACT.Exp).then_inc(p2_ready, 1)
                unit_exp(i, 1)
                act.wait_ge(p2T_ps, i + 1)
                nc.scalar.activation(prob2T[:].rearrange("p q n -> p (q n)"), M[1][:, 0:HALVES * P],
                                     ACT.Copy).then_inc(p2T_ready, 1)
                unit_probT(i, 0)
                unit_exp(i, 2)
                unit_probT(i, 1)
                unit_exp(i, 3)
                unit_probT(i, 2)
                unit_exp(i, 4)
                unit_probT(i, 3)
                unit_exp(i, 5)
                head(i + 1, 0)
                unit_probT(i, 4)
                unit_exp(i, 6)
                head(i + 1, 1)
                unit_probT(i, 5)
                unit_exp(i, 7)
                head(i + 1, 2)
                unit_probT(i, 6)
                head(i + 1, 3)
                unit_probT(i, 7)
                act.wait_ge(av_done, UNITS * (i + 1))
                values(i + 1, 0)
                values(i + 1, 1)

        @block.tensor
        def _(pe):
            def wq(q):
                return st.w_q[:, ds((q % QUADS) * QUAD, QUAD), :].rearrange("p h d -> p (h d)")

            def wk(q):
                return st.w_kw[:, ds((q % QUADS) * QUAD, QUAD), :].rearrange("p h d -> p (h d)")

            def wv(w, q):
                return w[:, ds((q % QUADS) * QUAD * VD, QUAD * VD)]

            def queries(q, t):
                nc.tensor.matmul(M[1 - t][:, 0:QUAD * QW], nqT[:, t * P:(t + 1) * P], wq(q), start=True,
                                 stop=True).then_inc(q_ps, 1)

            def window_keys(q, t):
                nc.tensor.matmul(M[t][:, 0:QUAD * HD], xnT[:, t * P:(t + 1) * P], wk(q), start=True,
                                 stop=True).then_inc(k_ps, 1)

            def head(q, h):
                if h == 0:
                    pe.wait_ge(q_roped, HALVES * (q + 1))
                    pe.wait_ge(k_roped, HALVES * (q + 1))
                elif h >= 2:
                    pe.wait_ge(heads_ready, QUAD * q + h - 1)
                for t in range(HALVES):
                    nc.tensor.transpose(M[h % 2][:, t * P:(t + 1) * P], q_tok[:, t, h, :], st.eye[:])
                    last = nc.tensor.transpose(M[h % 2][0:HD, T + t * P:T + (t + 1) * P], k_tok[:, t, h, :],
                                               st.eye[:])
                last.then_inc(heads_ps, 1)

            def values(q, t):
                pe.wait_ge(heads_ready, QUAD * q + QUAD - 1 + t)
                nc.tensor.matmul(M[t][:, 0:QUAD * VD], latT[:, t * P:(t + 1) * P], wv(st.w_v1, q), start=True,
                                 stop=True)
                nc.tensor.matmul(M[t][:, QUAD * VD:2 * QUAD * VD], xnT[:, t * P:(t + 1) * P], wv(st.w_vw, q),
                                 start=True, stop=True).then_inc(v_ps, 1)

            def scores(i, u):
                h, t = divmod(u, HALVES)
                n = unit_keys(u)
                if u >= 2:
                    pe.wait_ge(p_ready, UNITS * i + u - 1)
                out = S[u % 2][:, 0:2 * n].rearrange("p (a k) -> p a k", a=2)
                nc.tensor.matmul(out, qT[:, h, t * P:(t + 1) * P], keys[:, 0:h + 2:h + 1, 0:n], start=True, stop=False)
                nc.tensor.matmul(out[:, :, n - P:n], st.eye16[:],
                                 st.causal[:].unsqueeze(1).to_broadcast([P, 2, P]), start=False,
                                 stop=True).then_inc(s_ps, 1)

            def turn(i, u):
                pe.wait_ge(p_ready, UNITS * i + u + 1)
                for k in range(2 * (u % HALVES + 1)):
                    last = nc.tensor.transpose(PT[u % 2][:, k * P:(k + 1) * P], prob[:, u % 2, k * P:(k + 1) * P],
                                               st.eye[:])
                last.then_inc(pT_ps, 1)

            def weigh(i, u):
                h, t = divmod(u, HALVES)
                pe.wait_ge(pT_ready, UNITS * i + u + 1)
                for k in range(2):
                    o0 = 2 * k * QUAD * VW + h * VW
                    for kt in range(t + 1):
                        blk = k * (t + 1) + kt
                        last = nc.tensor.matmul(O[t][:, o0:o0 + VW], probT[:, u % 2, blk * P:(blk + 1) * P],
                                                vals[:, kt, k, h, :], start=(kt == 0), stop=(kt == t))
                last.then_inc(av_done, 1)

            pe.wait_ge(nq_in, 16)
            pe.wait_ge(tok_in, 32)
            queries(0, 0)
            window_keys(0, 0)
            pe.wait_ge(k_taken, 1)
            queries(0, 1)
            pe.wait_ge(q_taken, 1)
            window_keys(0, 1)
            for h in range(QUAD):
                head(0, h)
            for t in range(HALVES):
                values(0, t)
            with pe.Fori(0, NQ) as i:
                pe.wait_ge(shared_in, 16 * (i + 1))
                pe.wait_ge(heads_ready, QUAD * (i + 1))
                scores(i, 0)
                pe.wait_ge(ksel_in, 16 * (i + 1))
                pe.wait_ge(v_ready, HALVES * (i + 1))
                for t in range(HALVES):
                    for h in range(QUAD):
                        c = (t * QUAD + h) * KEEP
                        last = nc.tensor.matmul(M[0][:, c:c + KEEP], qT[0:HD, h, t * P:(t + 1) * P],
                                                ksel[:, h * KEEP:(h + 1) * KEEP], start=True, stop=True)
                last.then_inc(s2_ps, 1)
                pe.wait_ge(nq_in, 16 * (i + 2))
                queries(i + 1, 0)
                scores(i, 1)
                pe.wait_ge(s2_taken, i + 1)
                pe.wait_ge(tok_in, 32 * (i + 2))
                window_keys(i + 1, 0)
                pe.wait_ge(p2_ready, i + 1)
                pe.wait_ge(q_taken, HALVES * (i + 1) + 1)
                for t in range(HALVES):
                    last = nc.tensor.transpose(M[1][:, t * P:(t + 1) * P], prob2[:, t, :], st.eye[:])
                last.then_inc(p2T_ps, 1)
                turn(i, 0)
                scores(i, 2)
                pe.wait_ge(k_taken, HALVES * (i + 1) + 1)
                queries(i + 1, 1)
                pe.wait_ge(p2T_ready, i + 1)
                pe.wait_ge(vsel_in, 16 * (i + 1))
                pe.wait_ge(o_taken, i + 1)
                for t in range(HALVES):
                    last = nc.tensor.matmul(O[t][:, QUAD * VW:2 * QUAD * VW], prob2T[:, t, :], vsel[:], start=True,
                                            stop=True)
                last.then_inc(av2_done, 1)
                weigh(i, 0)
                turn(i, 1)
                scores(i, 3)
                window_keys(i + 1, 1)
                weigh(i, 1)
                turn(i, 2)
                scores(i, 4)
                weigh(i, 2)
                turn(i, 3)
                scores(i, 5)
                head(i + 1, 0)
                weigh(i, 3)
                turn(i, 4)
                scores(i, 6)
                head(i + 1, 1)
                weigh(i, 4)
                turn(i, 5)
                scores(i, 7)
                head(i + 1, 2)
                weigh(i, 5)
                turn(i, 6)
                head(i + 1, 3)
                values(i + 1, 0)
                weigh(i, 6)
                turn(i, 7)
                values(i + 1, 1)
                weigh(i, 7)

    tmp.close()


def experts(nc, a, st, ctx):
    def sem(name):
        return ctx.enter_context(nc.semaphore(name))

    tmp = ExitStack()

    def sb(name, shape, dt=F32):
        return tmp.enter_context(nc.sbuf_tensor(name, shape, dt))

    LE = LAYERS * EXPERTS
    W = CHUNK * P
    PER = EXPERTS * FT
    state, logits, mv = st.state, st.logits, st.mv
    w1_raw = sb("mo_w1_raw", [P, EXPERTS, FF])
    w1 = sb("mo_w1", [P, EXPERTS, FF])
    w2 = sb("mo_w2", [P, 2, EXPERTS, FT, C])
    b1_rows = sb("mo_b1_rows", [LE * FT, P])
    gb_rows = sb("mo_gb_rows", [2 * LE, C])
    b1T = sb("mo_b1T", [P, LE * FT])
    gbT = sb("mo_gbT", [P, 2 * LE])
    bias = sb("mo_bias", [P, PER])
    rw = sb("mo_rw", [C, LAYERS, EXPERTS])
    rb = sb("mo_rb", [P, LE])
    b2_in = sb("mo_b2_in", [3 * 32, LE * C])
    b2_rest = sb("mo_b2_rest", [3 * 32, LE * C])
    b2_part = sb("mo_b2_part", [3 * 32, LE * C], BF16)
    ones = sb("mo_ones", [3 * 32, P], BF16)
    xh = sb("mo_xh", [P, CHUNK, C])
    xhT = sb("mo_xhT", [P, W])
    h = sb("mo_h", [P, 2, FT, W])
    fresh = sb("mo_fresh", [P, CHUNK, C])
    freshT = sb("mo_freshT", [P, CHUNK, P])
    stats = sb("mo_stats", [P, CHUNK, 6])
    fresh_mv = sb("mo_fresh_mv", [P, CHUNK, 2])
    vareps = sb("mo_vareps", [P, TILES])
    minus_half = sb("mo_minus_half", [P, TILES])
    rstd = sb("mo_rstd", [P, TILES])
    comb = sb("mo_comb", [P, TILES, EXPERTS])
    lmax = sb("mo_lmax", [P, TILES])
    loff = sb("mo_loff", [P, TILES, EXPERTS])
    lexp = sb("mo_lexp", [P, TILES, EXPERTS])
    lsum = sb("mo_lsum", [P, TILES])
    linv = sb("mo_linv", [P, TILES])
    pr = sb("mo_pr", [P, TILES, EXPERTS])
    ge = sb("mo_ge", [P, 6, TILES])
    ra = sb("mo_ra", [P, EXPERTS, TILES])
    rc = sb("mo_rc", [P, EXPERTS, TILES])
    kept = sb("mo_kept", [P, TILES, EXPERTS])
    ksum = sb("mo_ksum", [P, TILES])
    kinv = sb("mo_kinv", [P, TILES])

    U = st.bank[0:4]
    Y = st.bank[4:6]
    TR = st.bank[6]
    RT = st.bank[7]

    small_in = sem("mo_small_in")
    w_in = sem("mo_w_in")
    b2_cleared = sem("mo_b2_cleared")
    b2_loaded = sem("mo_b2_loaded")
    half_ready = sem("mo_half_ready")
    b2_step = sem("mo_b2_step")
    rows_ps = sem("mo_rows_ps")
    rows_turned = sem("mo_rows_turned")
    w1_ready = sem("mo_w1_ready")
    bias_ps = sem("mo_bias_ps")
    bias_ready = sem("mo_bias_ready")
    step = sem("mo_router_step")
    var_ready = sem("mo_var_ready")
    rstd_ready = sem("mo_rstd_ready")
    loff_ready = sem("mo_loff_ready")
    lexp_ready = sem("mo_lexp_ready")
    xh_ready = sem("mo_xh_ready")
    xh_ps = sem("mo_xh_ps")
    xhT_ready = sem("mo_xhT_ready")
    up_ps = sem("mo_up_ps")
    h_ready = sem("mo_h_ready")
    y_ps = sem("mo_y_ps")
    y_taken = sem("mo_y_taken")
    fresh_kept = sem("mo_fresh_kept")
    fresh_ps = sem("mo_fresh_ps")
    freshT_ready = sem("mo_freshT_ready")
    stats_ready = sem("mo_stats_ready")
    aggr_ready = sem("mo_aggr_ready")
    mv_ready = sem("mo_mv_ready")
    logits_ps = sem("mo_logits_ps")
    logits_ready = sem("mo_logits_ready")
    NSMALL = 6

    def fresh_at(n):
        return EXPERTS * (n + 1) + 2


    with nc.Block() as block:

        @block.sync
        def _(sp):
            sp.dma_start(state[:], st.d_xn.rearrange("t p c -> p t c")).then_inc(small_in, 16)
            sp.dma_start(b1_rows[:], a["b1"].rearrange("l e (f p) -> (l e f) p", p=P)).then_inc(small_in, 16)
            sp.dma_start(gb_rows[0:LE, :], a["ln_g"].rearrange("l e c -> (l e) c")).then_inc(small_in, 16)
            sp.dma_start(gb_rows[LE:2 * LE, :], a["ln_b"].rearrange("l e c -> (l e) c")).then_inc(small_in, 16)
            sp.dma_start(rw[:], a["router_w"].rearrange("l h e -> h l e")).then_inc(small_in, 16)
            sp.dma_start(rb[:], a["router_b"].rearrange("(o l) e -> o (l e)", o=1).to_broadcast([P, LE]))\
                .then_inc(small_in, 16)

            def load_w(l):
                sp.dma_start(w1_raw[:], a["w1"][ds(l, 1)].rearrange("o e h f -> h (o e) f")).then_inc(w_in, 16)
                for e in range(EXPERTS):
                    sp.dma_start(w2[:, ds(l % 2, 1), e].rearrange("p o f c -> p (o f) c"),
                                 a["w2"][ds(l, 1), e].rearrange("o (f p) c -> p (o f) c", p=P))\
                        .then_inc(w_in, 16)

            load_w(0)
            sp.wait_ge(b2_cleared, 1)
            for k in range(3):
                sp.dma_start(b2_in[32 * k:32 * k + 1, :],
                             a["b2"].rearrange("(o l) e c -> o (l e c)", o=1)).then_inc(b2_loaded, 16)
            with sp.Fori(0, LAYERS - 1) as l:
                sp.wait_ge(w1_ready, l + 1)
                sp.wait_ge(bias_ready, l + 1)
                load_w(l + 1)

        @block.gpsimd
        def _(pool):
            nc.gpsimd.memset(minus_half[:], -0.5).then_inc(half_ready, 1)
            pool.wait_ge(half_ready, 1)
            with pool.Fori(0, LAYERS) as l:
                pool.wait_ge(var_ready, l + 1)
                nc.gpsimd.tensor_tensor(rstd[:], vareps[:], minus_half[:], ALU.pow).then_inc(rstd_ready, 1)

        @block.scalar
        def _(act):
            act.sem_inc(fresh_kept, 1)
            act.wait_ge(rows_ps, 1)
            nc.scalar.activation(b1T[:], TR[:, 0:LE * FT], ACT.Copy).then_inc(rows_turned, 1)
            nc.scalar.activation(gbT[:], TR[:, LE * FT:LE * FT + 2 * LE], ACT.Copy).then_inc(rows_turned, 1)

            def turned(n):
                act.wait_ge(xh_ps, n + 1)
                nc.scalar.activation(xhT[:], TR, ACT.Copy).then_inc(xhT_ready, 1)

            def keep(n, c):
                act.wait_ge(y_taken, fresh_at(n))
                nc.scalar.activation(state[:, ds(c * CHUNK, CHUNK), :], fresh[:], ACT.Copy).then_inc(fresh_kept, 1)

            def gelus(n, c, first):
                for e in range(EXPERTS):
                    if e == 1 and not first:
                        keep(n - 1, c - 1)
                    for f in range(FT):
                        act.wait_ge(up_ps, PER * n + e * FT + f + 1)
                        nc.scalar.activation(h[:, e % 2, f, :], U[f], ACT.Gelu,
                                             bias=bias[:, e * FT + f:e * FT + f + 1]).then_inc(h_ready, 1)

            with act.Fori(0, LAYERS) as l:
                act.wait_ge(loff_ready, l + 1)
                nc.scalar.activation(lexp[:], loff[:], ACT.Exp).then_inc(lexp_ready, 1)
                act.wait_ge(bias_ready, l + 1)
                turned(l * NCH)
                gelus(l * NCH, 0, True)
                turned(l * NCH + 1)
                with act.Fori(1, NCH - 1) as c:
                    gelus(l * NCH + c, c, False)
                    turned(l * NCH + c + 1)
                gelus(l * NCH + NCH - 1, NCH - 1, False)
                keep(l * NCH + NCH - 1, NCH - 1)

        @block.vector
        def _(dve):
            nc.vector.memset(b2_in[:], 0.0).then_inc(b2_cleared, 1)
            nc.vector.memset(ones[:], 1.0)
            dve.sem_inc(y_taken, 2)
            dve.wait_ge(b2_loaded, 16 * 3)
            dve.wait_ge(small_in, 16 * NSMALL)
            nc.vector.tensor_copy(b2_part[:], b2_in[:]).then_inc(b2_step, 1)
            dve.wait_ge(b2_step, 1)
            nc.vector.tensor_tensor(b2_rest[:], b2_in[:], b2_part[:], ALU.subtract).then_inc(b2_step, 1)
            dve.wait_ge(b2_step, 2)
            for row in (32, 64):
                nc.vector.tensor_copy(b2_part[row:row + 32, :], b2_rest[row:row + 32, :]).then_inc(b2_step, 1)
            dve.wait_ge(b2_step, 4)
            nc.vector.tensor_tensor(b2_rest[64:96, :], b2_rest[64:96, :], b2_part[64:96, :],
                                    ALU.subtract).then_inc(b2_step, 1)
            dve.wait_ge(b2_step, 5)
            nc.vector.tensor_copy(b2_part[64:96, :], b2_rest[64:96, :]).then_inc(b2_step, 1)

            def norm(n, c):
                for t in range(CHUNK):
                    tile = c * CHUNK + t
                    last = nc.vector.tensor_scalar(xh[:, t, :], state[:, ds(tile, 1), :].rearrange("p o c -> p (o c)"),
                                                   mv[:, ds(tile, 1), 0], rstd[:, ds(tile, 1)], ALU.subtract,
                                                   ALU.mult)
                last.then_inc(xh_ready, 1)

            def turned(n, c):
                dve.wait_ge(stats_ready, n + 1)
                dve.wait_ge(fresh_ps, n + 1)
                nc.vector.tensor_copy(freshT[:].rearrange("p t n -> p (t n)"), TR).then_inc(freshT_ready, 1)
                for t in range(CHUNK):
                    last = nc.vector.bn_aggr(fresh_mv[:, t, :], stats[:, t, :])
                last.then_inc(aggr_ready, 1)
                dve.wait_ge(aggr_ready, n + 1)
                nc.vector.tensor_copy(mv[:, ds(c * CHUNK, CHUNK), :], fresh_mv[:]).then_inc(mv_ready, 1)

            def route(n, c, l):
                dve.wait_ge(logits_ps, n + 1)
                nc.vector.tensor_tensor(logits[:, ds(c * CHUNK, CHUNK), :],
                                        RT[:, 0:CHUNK * EXPERTS].rearrange("p (t e) -> p t e", e=EXPERTS),
                                        rb[:, ds(((l + 1) % LAYERS) * EXPERTS, EXPERTS)].unsqueeze(1)
                                        .to_broadcast([P, CHUNK, EXPERTS]), ALU.add).then_inc(logits_ready, 1)

            def add_expert(n, c, e):
                dve.wait_ge(y_ps, EXPERTS * n + e + 1)
                dve.wait_ge(y_taken, EXPERTS * n + e + 2)
                if e == EXPERTS - 1:
                    dve.wait_ge(fresh_kept, n + 1)
                for t in range(CHUNK):
                    tile = c * CHUNK + t
                    s = state[:, ds(tile, 1), :].rearrange("p o c -> p (o c)")
                    last = nc.vector.scalar_tensor_tensor(
                        fresh[:, t, :] if e == EXPERTS - 1 else s, Y[e % 2][:, t * C:(t + 1) * C],
                        comb[:, ds(tile, 1), e], s, ALU.mult, ALU.add)
                last.then_inc(y_taken, 1)

            def moments(n):
                dve.wait_ge(y_taken, fresh_at(n))
                for t in range(CHUNK):
                    last = nc.vector.bn_stats(stats[:, t, :], fresh[:, t, :])
                last.then_inc(stats_ready, 1)

            def chunk(l, c, first, final):
                n = l * NCH + c
                if not final:
                    dve.wait_ge(xh_ps, n + 1)
                    norm(n + 1, c + 1)
                if not first:
                    turned(n - 1, c - 1)
                add_expert(n, c, 0)
                if not first:
                    route(n - 1, c - 1, l)
                for e in range(1, EXPERTS):
                    add_expert(n, c, e)
                moments(n)

            RSTEPS = 20
            with dve.Fori(0, LAYERS) as l:
                k = 0

                def after(ins):
                    nonlocal k
                    k += 1
                    ins.then_inc(step, 1)
                    dve.wait_ge(step, RSTEPS * l + k)

                dve.wait_ge(fresh_kept, NCH * l + 1)
                dve.wait_ge(rows_turned, 2)
                nc.vector.tensor_scalar(vareps[:], mv[:, :, 1], MOE_EPS, None, ALU.add).then_inc(var_ready, 1)
                after(nc.vector.reduce_max(lmax[:], logits[:], axis=AX.X))
                nc.vector.tensor_tensor(loff[:], logits[:], bcast(lmax[:], EXPERTS),
                                        ALU.subtract).then_inc(loff_ready, 1)
                dve.wait_ge(w_in, 16 * (1 + EXPERTS) * (l + 1))
                for e in range(EXPERTS):
                    last = nc.vector.tensor_scalar(w1[:, e, :], w1_raw[:, e, :], gbT[:, ds(l * EXPERTS + e, 1)],
                                                   None, ALU.mult)
                last.then_inc(w1_ready, 1)
                dve.wait_ge(bias_ps, l + 1)
                nc.vector.tensor_tensor(bias[:], RT[:, 0:PER], b1T[:, ds(l * PER, PER)],
                                        ALU.add).then_inc(bias_ready, 1)
                dve.wait_ge(rstd_ready, l + 1)
                norm(l * NCH, 0)
                dve.wait_ge(lexp_ready, l + 1)
                after(nc.vector.reduce_sum(lsum[:], lexp[:], axis=AX.X))
                after(nc.vector.reciprocal(linv[:], lsum[:]))
                after(nc.vector.tensor_tensor(pr[:], lexp[:], bcast(linv[:], EXPERTS), ALU.mult))
                pair = {}
                for j in range(EXPERTS):
                    for e in range(j + 1, EXPERTS):
                        pair[j, e] = len(pair)
                        last = nc.vector.tensor_tensor(ge[:, pair[j, e], :], pr[:, :, j], pr[:, :, e], ALU.is_ge)
                after(last)

                def g(j, e):
                    return ge[:, pair[j, e], :]
                plan = [(g(0, 1), ALU.add, g(0, 2), ALU.add, g(0, 3), ALU.is_ge, 1.5),
                        (g(0, 1), ALU.subtract, g(1, 2), ALU.subtract, g(1, 3), ALU.is_le, -0.5),
                        (g(0, 2), ALU.add, g(1, 2), ALU.subtract, g(2, 3), ALU.is_le, 0.5),
                        (g(0, 3), ALU.add, g(1, 3), ALU.add, g(2, 3), ALU.is_le, 1.5)]
                for e, (x0, op0, x1, op1, x2, cmp, at) in enumerate(plan):
                    after(nc.vector.tensor_tensor(ra[:, e, :], x0, x1, op0))
                    after(nc.vector.tensor_tensor(rc[:, e, :], ra[:, e, :], x2, op1))
                    after(nc.vector.scalar_tensor_tensor(kept[:, :, e], rc[:, e, :], at, pr[:, :, e], cmp, ALU.mult))
                after(nc.vector.reduce_sum(ksum[:], kept[:], axis=AX.X))
                after(nc.vector.reciprocal(kinv[:], ksum[:]))
                after(nc.vector.tensor_tensor(comb[:], kept[:], bcast(kinv[:], EXPERTS), ALU.mult))
                assert k == RSTEPS, k
                chunk(l, 0, True, False)
                with dve.Fori(1, NCH - 1) as c:
                    chunk(l, c, False, False)
                chunk(l, NCH - 1, False, True)
                turned(l * NCH + NCH - 1, NCH - 1)
                route(l * NCH + NCH - 1, NCH - 1, l)
                dve.wait_ge(logits_ready, NCH * (l + 1))
                dve.wait_ge(mv_ready, NCH * (l + 1))

        @block.tensor
        def _(pe):
            pe.wait_ge(small_in, 16 * NSMALL)
            nc.tensor.transpose(TR[:, 0:LE * FT], b1_rows[:], st.eye[0:LE * FT, 0:LE * FT])
            nc.tensor.transpose(TR[:, LE * FT:LE * FT + 2 * LE], gb_rows[:],
                                st.eye[0:2 * LE, 0:2 * LE]).then_inc(rows_ps, 1)
            pe.wait_ge(rows_turned, 2)
            pe.wait_ge(b2_step, 6)

            def turn(n):
                pe.wait_ge(xh_ready, n + 1)
                for t in range(CHUNK):
                    last = nc.tensor.transpose(TR[:, t * P:(t + 1) * P], xh[:, t, :], st.eye[:])
                last.then_inc(xh_ps, 1)

            def up(n, e):
                for f in range(FT):
                    if e > 0:
                        pe.wait_ge(h_ready, PER * n + (e - 1) * FT + f + 1)
                    nc.tensor.matmul(U[f], w1[:, e, f * P:(f + 1) * P], xhT[:], start=True,
                                     stop=True).then_inc(up_ps, 1)

            def down(n, l, e):
                pe.wait_ge(y_taken, EXPERTS * n + e + 1)
                y = Y[e % 2]
                b2 = b2_part[:, ds((l * EXPERTS + e) * C, C)].unsqueeze(1).to_broadcast([3 * 32, CHUNK, C])
                nc.tensor.matmul(y.rearrange("p (t c) -> p t c", c=C), ones[:], b2, start=True, stop=False,
                                 skip_group_check=True)
                for f in range(FT):
                    pe.wait_ge(h_ready, PER * n + e * FT + f + 1)
                    for t in range(CHUNK):
                        last = nc.tensor.matmul(y[:, t * C:(t + 1) * C], h[:, e % 2, f, t * P:(t + 1) * P],
                                                w2[:, ds(l % 2, 1), e, f, :].rearrange("p o c -> p (o c)"), start=False, stop=(f == FT - 1),
                                                skip_group_check=True)
                last.then_inc(y_ps, 1)

            def turn_fresh(n):
                pe.wait_ge(y_taken, fresh_at(n))
                for t in range(CHUNK):
                    last = nc.tensor.transpose(TR[:, t * P:(t + 1) * P], fresh[:, t, :], st.eye[:])
                last.then_inc(fresh_ps, 1)

            def route(n, l):
                pe.wait_ge(freshT_ready, n + 1)
                for t in range(CHUNK):
                    last = nc.tensor.matmul(RT[:, t * EXPERTS:(t + 1) * EXPERTS], freshT[:, t, :],
                                            rw[:, ds((l + 1) % LAYERS, 1), :].rearrange("p o e -> p (o e)"),
                                            start=True, stop=True)
                last.then_inc(logits_ps, 1)

            def chunk(l, c, first, final):
                n = l * NCH + c
                pe.wait_ge(xhT_ready, n + 1)
                up(n, 0)
                if not first:
                    turn_fresh(n - 1)
                up(n, 1)
                down(n, l, 0)
                if not first:
                    route(n - 1, l)
                up(n, 2)
                down(n, l, 1)
                up(n, 3)
                if not final:
                    turn(n + 1)
                down(n, l, 2)
                down(n, l, 3)

            with pe.Fori(0, LAYERS) as l:
                pe.wait_ge(w_in, 16 * (1 + EXPERTS) * (l + 1))
                pe.wait_ge(loff_ready, l + 1)
                for e in range(EXPERTS):
                    for f in range(FT):
                        last = nc.tensor.matmul(RT[:, e * FT + f:e * FT + f + 1], w1_raw[:, e, f * P:(f + 1) * P],
                                                gbT[:, ds(LE + l * EXPERTS + e, 1)], start=True, stop=True)
                last.then_inc(bias_ps, 1)
                turn(l * NCH)
                pe.wait_ge(w1_ready, l + 1)
                chunk(l, 0, True, False)
                with pe.Fori(1, NCH - 1) as c:
                    chunk(l, c, False, False)
                chunk(l, NCH - 1, False, True)
                turn_fresh(l * NCH + NCH - 1)
                route(l * NCH + NCH - 1, l)

    tmp.close()


def finish(nc, a, st, out, ctx):
    def sem(name):
        return ctx.enter_context(nc.semaphore(name))

    tmp = ExitStack()

    def sb(name, shape, dt=F32):
        return tmp.enter_context(nc.sbuf_tensor(name, shape, dt))

    D = HEADS * VD
    KT = D // P
    N = TILES // CHUNK
    w_p = sb("fi_w_p", [P, KT, C])
    o = sb("fi_o", [P, 2, CHUNK, D])
    oT = sb("fi_oT", [P, 2, KT, P])
    x = sb("fi_x", [P, 2, CHUNK, C])
    part = sb("fi_part", [P, 2, CHUNK, C])
    res = sb("fi_res", [P, 2, CHUNK, C])

    w_in = sem("fi_w_in")
    o_in = [sem(f"fi_o_in{s}") for s in range(2)]
    turned_ps = sem("fi_turned_ps")
    turned = sem("fi_turned")
    y_ps = sem("fi_y_ps")
    added = sem("fi_added")
    res_ready = sem("fi_res_ready")
    stored = [sem(f"fi_stored{s}") for s in range(2)]
    x_dram = a["x"].rearrange("b (h p) c -> p (b h) c", p=P)
    out_dram = out.rearrange("b (h p) c -> p (b h) c", p=P)
    o_dram = st.d_o.rearrange("t p n -> p t n")

    with nc.Block() as block:

        @block.sync
        def _(sp):
            def load(g, s):
                sp.dma_start(o[:, s], o_dram[:, ds(g * CHUNK, CHUNK), :]).then_inc(o_in[s], 16)
                sp.dma_start(x[:, s], x_dram[:, ds(g * CHUNK, CHUNK), :]).then_inc(o_in[s], 16)

            sp.dma_start(w_p[:], a["w_proj"].rearrange("(k p) c -> p k c", p=P)).then_inc(w_in, 16)
            for s in range(2):
                sp.sem_inc(stored[s], 16)
            load(0, 0)
            load(1, 1)
            with sp.Fori(0, N // 2 - 1) as i:
                for s in range(2):
                    g = 2 * i + s
                    sp.wait_ge(res_ready, g + 1)
                    load(g + 2, s)
                    sp.dma_start(out_dram[:, ds(g * CHUNK, CHUNK), :], res[:, s]).then_inc(stored[s], 16)
            for s in range(2):
                g = N - 2 + s
                sp.wait_ge(res_ready, g + 1)
                sp.dma_start(out_dram[:, ds(g * CHUNK, CHUNK), :], res[:, s]).then_inc(stored[s], 16)
            for s in range(2):
                sp.wait_ge(stored[s], 16 * (N // 2 + 1))

        @block.scalar
        def _(act):
            with act.Fori(0, N // 2) as i:
                for s in range(2):
                    for t in range(CHUNK):
                        m = (2 * i + s) * CHUNK + t
                        act.wait_ge(turned_ps, m + 1)
                        nc.scalar.activation(oT[:, t % 2].rearrange("p k n -> p (k n)"), st.bank[t % 2],
                                             ACT.Copy).then_inc(turned, 1)

        @block.vector
        def _(dve):
            with dve.Fori(0, N // 2) as i:
                for s in range(2):
                    g = 2 * i + s
                    dve.wait_ge(y_ps, g + 1)
                    nc.vector.tensor_tensor(part[:, s], st.bank[2 + s].rearrange("p (t c) -> p t c", c=C),
                                            st.state[:, ds(g * CHUNK, CHUNK), :], ALU.add).then_inc(added, 1)
                    dve.wait_ge(added, g + 1)
                    dve.wait_ge(stored[s], 16 * (i + 1))
                    nc.vector.tensor_tensor(res[:, s], part[:, s], x[:, s], ALU.add).then_inc(res_ready, 1)

        @block.tensor
        def _(pe):
            pe.wait_ge(w_in, 16)

            def turn(m, s, t):
                for k in range(KT):
                    last = nc.tensor.transpose(st.bank[t % 2][:, k * P:(k + 1) * P], o[:, s, t, k * P:(k + 1) * P],
                                               st.eye[:])
                last.then_inc(turned_ps, 1)

            with pe.Fori(0, N // 2) as i:
                for s in range(2):
                    g = 2 * i + s
                    pe.wait_ge(o_in[s], 32 * (i + 1))
                    turn(g * CHUNK, s, 0)
                    for t in range(CHUNK):
                        if t + 1 < CHUNK:
                            if t > 0:
                                pe.wait_ge(turned, g * CHUNK + t)
                            turn(g * CHUNK + t + 1, s, t + 1)
                        pe.wait_ge(turned, g * CHUNK + t + 1)
                        for k in range(KT):
                            last = nc.tensor.matmul(st.bank[2 + s][:, t * C:(t + 1) * C], oT[:, t % 2, k, :],
                                                    w_p[:, k, :], start=(k == 0), stop=(k == KT - 1))
                    last.then_inc(y_ps, 1)

    tmp.close()


def program(nc, a, out):
    st = Store()
    with ExitStack() as ctx:
        def sb(stack, name, shape, dt=F32):
            return stack.enter_context(nc.sbuf_tensor(name, shape, dt))

        def dram(name, shape):
            return nc.dram_tensor(f"d_{name}", shape, F32, kind="Internal").ap()

        st.psum = ctx.enter_context(nc.psum_tensor("psum", [P, 8, 512], F32))
        st.bank = [st.psum[:, k, :] for k in range(8)]
        st.eye = sb(ctx, "eye", [P, P])
        st.d_xn = dram("xn", [TILES, P, C])
        st.d_xnT = dram("xnT", [B, P, T])
        st.d_kvT = dram("kvT", [B, P, T])
        st.d_nqT = dram("nqT", [B, QL, T])
        st.d_ks = dram("ks", [NQ, HD, QUAD * KEEP])
        st.d_vs = dram("vs", [NQ, P, QUAD * (VD + 1)])
        st.d_o = dram("o", [TILES, P, HEADS * VD])

        st.logits = sb(ctx, "logits", [P, TILES, EXPERTS])
        st.mv = sb(ctx, "mv", [P, TILES, 2])

        with ExitStack() as att:
            st.eye16 = sb(att, "eye16", [P, P], BF16)
            st.causal = sb(att, "causal", [P, P], BF16)
            st.cos = sb(att, "cos", [P, HALVES, ROPE])
            st.sin = sb(att, "sin", [P, HALVES, ROPE])
            st.w_q = sb(att, "w_q", [QL, HEADS, QW])
            st.w_kw = sb(att, "w_kw", [P, HEADS, HD])
            st.w_vw = sb(att, "w_vw", [P, HEADS * VD])
            st.w_v1 = sb(att, "w_v1", [P, HEADS * VD])
            st.gates = sb(att, "gates", [P, B, 3])
            with ExitStack() as pre:
                st.rb0 = sb(pre, "rb0", [P, EXPERTS])
                st.w_all = sb(pre, "w_all", [P, CALL])
                st.w_ks = sb(pre, "w_ks", [P, HEADS, HD])
                st.w_vs = sb(pre, "w_vs", [P, HEADS * VD])
                st.cos_sel = sb(pre, "cos_sel", [P, ROPE])
                st.sin_sel = sb(pre, "sin_sel", [P, ROPE])
                st.iota = sb(pre, "iota", [P, KEEP])
                st.imp = sb(pre, "imp", [P, HALVES, B])
                st.gl = sb(pre, "gl", [P, HALVES, B, 3])
                st.place = sb(pre, "place", [P, B, HALVES])
                setup(nc, a, st, ctx)
                tokens(nc, a, st, ctx)
                choose(nc, a, st, ctx)
                selected(nc, a, st, ctx)
            attention(nc, a, st, ctx)
        with ExitStack() as late:
            st.state = sb(late, "state", [P, TILES, C])
            experts(nc, a, st, ctx)
            finish(nc, a, st, out, ctx)


_INS = ["x", "w_cq", "g_qnorm", "w_dq_nope", "w_dq_rope", "w_ckv", "g_kvnorm", "w_dk_nope", "w_dv", "w_krope",
        "w_imp", "w_selk", "w_selv", "w_wink", "w_winv", "w_gate", "w_proj"]
_MOE = ["router_w", "router_b", "ln_g", "ln_b", "w1", "b1", "w2", "b2"]


def kernel(**inputs):
    import concourse.bacc as bacc
    from concourse.bass_utils import run_bass_kernel_spmd

    nc = bacc.Bacc("TRN2", target_bir_lowering=False, num_devices=1)
    arrays = {n: np.ascontiguousarray(inputs[f"L0_attn_{n}"]) for n in _INS}
    arrays.update({n: np.ascontiguousarray(inputs[f"L0_ffn_{n}"]) for n in _MOE})
    arrays.update(shape_constants())
    a = {n: nc.dram_tensor(n, v.shape, mybir.dt.from_np(v.dtype), kind="ExternalInput").ap()
         for n, v in arrays.items()}
    out = nc.dram_tensor("out", (B, T, C), F32, kind="ExternalOutput").ap()
    program(nc, a, out)
    r = run_bass_kernel_spmd(nc, [arrays], core_ids=[0])
    return r.results[0]["out"]
```

```python
from contextlib import ExitStack

import numpy as np
import concourse.bass as bass
from concourse import mybir

F32 = mybir.dt.float32
BF16 = mybir.dt.bfloat16
F16 = mybir.dt.float16
ALU = mybir.AluOpType
ACT = mybir.ActivationFunctionType
AX = mybir.AxisListType
ds = bass.ds

P = 128
B, T, C = 32, 256, 128
TILES = B * T // P
HALVES = T // P
HEADS, NOPE, ROPE, VD = 16, 32, 64, 32
HD = NOPE + ROPE
QL, KL = 96, 32
KEEP = 32
QUAD = 4
QUADS = HEADS // QUAD
NQ = B * QUADS
QW = HD + KL
SCALE = float(HD) ** -0.5
LN_EPS, RMS_EPS, MOE_EPS = 1e-5, 1e-6, 1e-5
CQ, CKV, CKR, CIMP, CGATE = 0, 96, 128, 192, 193
CROUT = 196
CALL = 200
GRP = 4
GT = GRP * HALVES
NGRP = B // GRP
LAYERS, EXPERTS, FF = 4, 4, 512
FT = FF // P
CHUNK = 4
NCH = TILES // CHUNK
WEIGHT_SCALE = 2.0 ** 14
GONE = -3.0e38


def shape_constants():
    f = (1.0 / np.float32(10000.0) ** (np.arange(0, ROPE, 2, dtype=np.float32) / np.float32(ROPE))).astype(np.float32)
    a = np.outer(np.arange(T, dtype=np.float32), f).astype(np.float32)
    cos, sin = np.cos(a).astype(np.float32), np.sin(a).astype(np.float32)
    return {
        "c_eye": np.eye(P, dtype=np.float32),
        "c_causal": np.triu(np.full((P, P), -1e30, np.float32), 1),
        "c_cos": np.concatenate([cos, cos], 1),
        "c_sin": np.concatenate([-sin, sin], 1),
        "c_iota": np.tile(np.arange(KEEP, dtype=np.float32), (P, 1)),
    }


def bcast(ap, n):
    return ap.unsqueeze(len(ap.shape)).to_broadcast(list(ap.shape) + [n])


class Store:
    pass


def setup(nc, a, st, ctx):
    def sem(name):
        return ctx.enter_context(nc.semaphore(name))

    tmp = ExitStack()

    def sb(name, shape, dt=F32):
        return tmp.enter_context(nc.sbuf_tensor(name, shape, dt))

    raw_rope = sb("raw_rope", [QL, HEADS * ROPE])
    raw_nope = sb("raw_nope", [QL, HEADS * NOPE])
    raw_dk = sb("raw_dk", [KL, HEADS * NOPE])
    dk_gained = sb("dk_gained", [KL, HEADS * NOPE])
    gq = sb("gq", [QL, 1])
    gq_scaled = sb("gq_scaled", [QL, 1])
    gkv = sb("gkv", [KL, 1])
    gkv_high = sb("gkv_high", [P, 1])
    nope_T = sb("nope_T", [P, QUADS, QL])
    dk_T = sb("dk_T", [P, QUADS, KL])
    causal32 = sb("causal32", [P, P])

    loaded = sem("su_loaded")
    dv_zeroed = sem("su_dv_zeroed")
    gq_ready = sem("su_gq_ready")
    dk_ready = sem("su_dk_ready")
    flipped = sem("su_flipped")
    flip_out = sem("su_flip_out")
    absorbed = sem("su_absorbed")
    wq_parts = sem("su_wq_parts")
    done = sem("su_done")
    NLOAD = 33

    with nc.Block() as block:

        @block.sync
        def _(sp):
            n = 0
            wq_, wn_ = a["w_wink"], a["w_selk"]

            def load(dst, src):
                nonlocal n
                n += 1
                sp.dma_start(dst, src).then_inc(loaded, 16)

            load(raw_rope[:], a["w_dq_rope"])
            load(raw_nope[:], a["w_dq_nope"])
            load(raw_dk[:], a["w_dk_nope"])
            load(gq[:], a["g_qnorm"].rearrange("(k o) -> k o", o=1))
            load(gkv[:], a["g_kvnorm"].rearrange("(k o) -> k o", o=1))
            load(gkv_high[P - KL:P, :], a["g_kvnorm"].rearrange("(k o) -> k o", o=1))
            load(st.eye[:], a["c_eye"])
            load(causal32[:], a["c_causal"])
            load(st.cos[:], a["c_cos"].rearrange("(h p) d -> p h d", p=P))
            load(st.sin[:], a["c_sin"].rearrange("(h p) d -> p h d", p=P))
            for j in range(GRP):
                load(st.cos_sel[KEEP * j:KEEP * (j + 1), :], a["c_cos"][0:KEEP, :])
                load(st.sin_sel[KEEP * j:KEEP * (j + 1), :], a["c_sin"][0:KEEP, :])
            load(st.iota[:], a["c_iota"])
            load(st.w_all[:, CQ:CQ + QL], a["w_cq"])
            load(st.w_all[:, CKV:CKV + KL], a["w_ckv"])
            load(st.w_all[:, CKR:CKR + ROPE], a["w_krope"])
            load(st.w_all[:, CIMP:CIMP + 1], a["w_imp"])
            load(st.w_all[:, CGATE:CGATE + 3], a["w_gate"])
            load(st.w_all[:, CROUT:CROUT + EXPERTS], a["router_w"][0])
            load(st.rb0[:], a["router_b"][0:1, :].to_broadcast([P, EXPERTS]))
            for dst, src in ((st.w_kw, a["w_wink"]), (st.w_ks, a["w_selk"])):
                v = src.rearrange("c (h d) -> c h d", d=HD)
                load(dst[:, 0:HEADS, 0:ROPE], v[:, :, NOPE:HD])
                load(dst[:, 0:HEADS, ROPE:HD], v[:, :, 0:NOPE])
            load(st.w_vw[:], a["w_winv"])
            load(st.w_vs[:], a["w_selv"])
            sp.wait_ge(dv_zeroed, 1)
            load(st.w_v1[P - KL:P, :], a["w_dv"])
            assert n == NLOAD, n

        @block.vector
        def _(dve):
            nc.vector.memset(st.w_v1[:], 0.0).then_inc(dv_zeroed, 1)
            dve.wait_ge(loaded, 16 * NLOAD)
            nc.vector.tensor_scalar(gq_scaled[:], gq[:], SCALE, None, ALU.mult).then_inc(gq_ready, 1)
            nc.vector.tensor_scalar(dk_gained[:], raw_dk[:], gkv[:], None, ALU.mult).then_inc(dk_ready, 1)
            nc.vector.tensor_copy(st.causal[:], causal32[:]).then_inc(done, 1)
            nc.vector.tensor_copy(st.eye16[:], st.eye[:]).then_inc(done, 1)
            nc.vector.tensor_scalar(st.w_all[:, CKR:CKR + ROPE], st.w_all[:, CKR:CKR + ROPE], 1.0 / HEADS, None,
                                    ALU.mult).then_inc(done, 1)
            nc.vector.tensor_scalar(st.w_v1[P - KL:P, :], st.w_v1[P - KL:P, :], gkv_high[P - KL:P, :], None,
                                    ALU.mult).then_inc(done, 1)
            dve.wait_ge(gq_ready, 1)
            nc.vector.tensor_scalar(st.w_q[:, :, 0:ROPE], raw_rope[:].rearrange("p (h d) -> p h d", d=ROPE),
                                    gq_scaled[:], None, ALU.mult).then_inc(wq_parts, 1)
            nc.vector.tensor_scalar(st.w_q[:, :, ROPE:HD], raw_nope[:].rearrange("p (h d) -> p h d", d=NOPE),
                                    gq_scaled[:], None, ALU.mult).then_inc(wq_parts, 1)
            for j in range(QUAD):
                dve.wait_ge(absorbed, j + 1)
                nc.vector.tensor_scalar(st.w_q[:, j:HEADS:QUAD, HD:QW],
                                        st.bank[2 + j][0:QL, 0:QUADS * KL].rearrange("p (g d) -> p g d", d=KL),
                                        gq_scaled[:], None, ALU.mult).then_inc(wq_parts, 1)
            dve.wait_ge(wq_parts, 2 + QUAD)

        @block.scalar
        def _(act):
            act.wait_ge(flipped, 1)
            nc.scalar.activation(nope_T[:], st.bank[0][:, 0:QUADS * QL].rearrange("p (g d) -> p g d", d=QL),
                                 ACT.Copy).then_inc(flip_out, 1)
            act.wait_ge(flipped, 2)
            nc.scalar.activation(dk_T[:], st.bank[1][:, 0:QUADS * KL].rearrange("p (g d) -> p g d", d=KL),
                                 ACT.Copy).then_inc(flip_out, 1)

        @block.tensor
        def _(pe):
            pe.wait_ge(loaded, 16 * NLOAD)
            for g in range(QUADS):
                last = nc.tensor.transpose(st.bank[0][:, g * QL:(g + 1) * QL], raw_nope[:, g * P:(g + 1) * P],
                                           st.eye[0:QL, 0:QL])
            last.then_inc(flipped, 1)
            pe.wait_ge(dk_ready, 1)
            for g in range(QUADS):
                last = nc.tensor.transpose(st.bank[1][:, g * KL:(g + 1) * KL], dk_gained[:, g * P:(g + 1) * P],
                                           st.eye[0:KL, 0:KL])
            last.then_inc(flipped, 1)
            pe.wait_ge(flip_out, 2)
            for j in range(QUAD):
                rows = slice(NOPE * j, NOPE * (j + 1))
                for g in range(QUADS):
                    last = nc.tensor.matmul(st.bank[2 + j][0:QL, g * KL:(g + 1) * KL], nope_T[rows, g, :],
                                            dk_T[rows, g, :], start=True, stop=True)
                last.then_inc(absorbed, 1)

    tmp.close()


def tokens(nc, a, st, ctx):
    def sem(name):
        return ctx.enter_context(nc.semaphore(name))

    tmp = ExitStack()

    def sb(name, shape, dt=F32):
        return tmp.enter_context(nc.sbuf_tensor(name, shape, dt))

    x = sb("tk_x", [P, GT, C])
    xc = sb("tk_xc", [P, GT, C])
    sq = sb("tk_sq", [P, GT, C])
    xn = sb("tk_xn", [P, GT, C])
    xnT = sb("tk_xnT", [P, GT, P])
    mean = sb("tk_mean", [P, GT])
    nmean = sb("tk_nmean", [P, GT])
    vsum = sb("tk_vsum", [P, GT])
    var = sb("tk_var", [P, GT])
    rstd = sb("tk_rstd", [P, GT])
    proj = sb("tk_proj", [P, GT, CALL])
    psq = sb("tk_psq", [P, GT, QL + KL])
    ssum = sb("tk_ssum", [P, 2, GT])
    smean = sb("tk_smean", [P, 2, GT])
    rrms = sb("tk_rrms", [P, 2, GT])
    rot = sb("tk_rot", [P, GT, ROPE])
    key = sb("tk_key", [P, GT, P])
    nq = sb("tk_nq", [P, GT, QL])
    keyT = sb("tk_keyT", [P, GT, P])
    nqT = sb("tk_nqT", [QL, GT, P])
    minus_half = sb("tk_minus_half", [P, 2 * GT])
    mom = sb("tk_mom", [P, 2, GT])
    msq = sb("tk_msq", [P, GT])
    vsq = sb("tk_vsq", [P, GT])

    x_in = sem("tk_x_in")
    summed = sem("tk_summed")
    mean_ready = sem("tk_mean_ready")
    centered = sem("tk_centered")
    squared = sem("tk_squared")
    vsummed = sem("tk_vsummed")
    var_ready = sem("tk_var_ready")
    half_ready = sem("tk_half_ready")
    rstd_ready = sem("tk_rstd_ready")
    xn_ready = sem("tk_xn_ready")
    xt_ps = sem("tk_xt_ps")
    xnT_ready = sem("tk_xnT_ready")
    proj_ps = sem("tk_proj_ps")
    proj_ready = sem("tk_proj_ready")
    psq_ready = sem("tk_psq_ready")
    ssummed = sem("tk_ssummed")
    smean_ready = sem("tk_smean_ready")
    rrms_ready = sem("tk_rrms_ready")
    kept = sem("tk_kept")
    rotated = sem("tk_rotated")
    key_zeroed = sem("tk_key_zeroed")
    lat_ready = sem("tk_lat_ready")
    lat_ps = sem("tk_lat_ps")
    latT_ready = sem("tk_latT_ready")
    xsq_ready = sem("tk_xsq_ready")
    mom_ready = sem("tk_mom_ready")
    mean1_ready = sem("tk_mean1_ready")
    vsq_ready = sem("tk_vsq_ready")
    xn_out = sem("tk_xn_out")
    xt_out = sem("tk_xt_out")
    lat_out = sem("tk_lat_out")

    x_dram = a["x"].rearrange("b (h p) c -> p (b h) c", p=P)
    xn_dram = st.d_xn.rearrange("t p c -> p t c")
    bk = st.bank

    def two(ap):
        return ap.rearrange("p t n -> p (t n)")

    with nc.Block() as block:

        @block.sync
        def _(sp):
            def load(i):
                sp.dma_start(x[:], x_dram[:, ds(i * GT, GT), :]).then_inc(x_in, 16)

            def store(i):
                sp.wait_ge(xn_ready, i + 1)
                sp.dma_start(xn_dram[:, ds(i * GT, GT), :], xn[:]).then_inc(xn_out, 16)
                sp.wait_ge(xnT_ready, 2 * i + 2)
                sp.dma_start(st.d_xnT[ds(i * GRP, GRP)].rearrange("b c n -> c b n"),
                             xnT[:].rearrange("p (b h) n -> p b (h n)", h=HALVES)).then_inc(xt_out, 16)
                sp.wait_ge(latT_ready, 4 * i + 4)
                sp.dma_start(st.d_kvT[ds(i * GRP, GRP)].rearrange("b c n -> c b n"),
                             keyT[:].rearrange("p (b h) n -> p b (h n)", h=HALVES)).then_inc(lat_out, 16)
                sp.dma_start(st.d_nqT[ds(i * GRP, GRP)].rearrange("b c n -> c b n"),
                             nqT[:].rearrange("p (b h) n -> p b (h n)", h=HALVES)).then_inc(lat_out, 16)

            sp.sem_inc(xn_out, 16)
            sp.sem_inc(xt_out, 16)
            sp.sem_inc(lat_out, 32)
            load(0)
            with sp.Fori(0, NGRP - 1) as i:
                sp.wait_ge(centered, i + 1)
                load(i + 1)
                store(i)
            store(NGRP - 1)
            sp.wait_ge(xn_out, 16 * NGRP + 16)
            sp.wait_ge(xt_out, 16 * NGRP + 16)
            sp.wait_ge(lat_out, 32 * NGRP + 32)

        @block.gpsimd
        def _(pool):
            nc.gpsimd.memset(minus_half[:], -0.5).then_inc(half_ready, 1)
            pool.wait_ge(half_ready, 1)
            with pool.Fori(0, NGRP) as i:
                pool.wait_ge(var_ready, i + 1)
                nc.gpsimd.tensor_tensor(rstd[:], var[:], minus_half[:, 0:GT], ALU.pow).then_inc(rstd_ready, 1)
                pool.wait_ge(smean_ready, 2 * i + 2)
                nc.gpsimd.tensor_tensor(rrms[:].rearrange("p k t -> p (k t)"), smean[:].rearrange("p k t -> p (k t)"),
                                        minus_half[:], ALU.pow).then_inc(rrms_ready, 1)

        @block.scalar
        def _(act):
            with act.Fori(0, NGRP) as i:
                act.wait_ge(centered, i + 1)
                nc.scalar.activation(sq[:], xc[:], ACT.Square).then_inc(squared, 1)
                for k in range(2):
                    act.wait_ge(xt_ps, 2 * i + k + 1)
                    if k == 0:
                        act.wait_ge(xt_out, 16 * i + 16)
                    nc.scalar.activation(two(xnT[:, 4 * k:4 * k + 4, :]), bk[k][:, :], ACT.Copy).then_inc(xnT_ready, 1)
                act.wait_ge(vsummed, i + 1)
                nc.scalar.activation(sq[:], xn[:], ACT.Square).then_inc(xsq_ready, 1)
                for k in range(4):
                    act.wait_ge(proj_ps, 4 * i + k + 1)
                    nc.scalar.activation(two(proj[:, 2 * k:2 * k + 2, :]), bk[2 + k][:, 0:2 * CALL],
                                         ACT.Copy).then_inc(proj_ready, 1)
                act.wait_ge(proj_ready, 4 * i + 4)
                nc.scalar.activation(psq[:], proj[:, :, 0:QL + KL], ACT.Square).then_inc(psq_ready, 1)
                for k in range(4):
                    act.wait_ge(lat_ps, 4 * i + k + 1)
                    if k == 0:
                        act.wait_ge(lat_out, 32 * i + 32)
                    if k < 2:
                        nc.scalar.activation(two(keyT[:, 4 * k:4 * k + 4, :]), bk[k][:, :],
                                             ACT.Copy).then_inc(latT_ready, 1)
                    else:
                        nc.scalar.activation(two(nqT[:, 4 * k - 8:4 * k - 4, :]), bk[k][0:QL, :],
                                             ACT.Copy).then_inc(latT_ready, 1)

        @block.vector
        def _(dve):
            nc.vector.memset(key[:], 0.0).then_inc(key_zeroed, 1)
            dve.wait_ge(key_zeroed, 1)
            with dve.Fori(0, NGRP) as i:
                dve.wait_ge(x_in, 16 * i + 16)
                nc.vector.reduce_sum(mean[:], x[:], axis=AX.X).then_inc(summed, 1)
                dve.wait_ge(summed, i + 1)
                nc.vector.tensor_scalar(nmean[:], mean[:], 1.0 / C, None, ALU.mult).then_inc(mean_ready, 1)
                dve.wait_ge(mean_ready, i + 1)
                nc.vector.tensor_tensor(xc[:], x[:], bcast(nmean[:], C), ALU.subtract).then_inc(centered, 1)
                dve.wait_ge(squared, i + 1)
                nc.vector.reduce_sum(vsum[:], sq[:], axis=AX.X).then_inc(vsummed, 1)
                dve.wait_ge(vsummed, i + 1)
                nc.vector.tensor_scalar(var[:], vsum[:], 1.0 / C, LN_EPS, ALU.mult, ALU.add).then_inc(var_ready, 1)
                dve.wait_ge(rstd_ready, i + 1)
                dve.wait_ge(xn_out, 16 * i + 16)
                nc.vector.tensor_tensor(xn[:], xc[:], bcast(rstd[:], C), ALU.mult).then_inc(xn_ready, 1)
                dve.wait_ge(proj_ready, 4 * i + 4)
                nc.vector.tensor_copy(st.imp[:, :, ds(i * GRP, GRP)],
                                      proj[:, :, CIMP].rearrange("p (b h) -> p h b", h=HALVES)).then_inc(kept, 1)
                for h in range(HALVES):
                    nc.vector.tensor_copy(st.gl[:, h, ds(i * GRP, GRP), :],
                                          proj[:, h:GT:HALVES, CGATE:CGATE + 3]).then_inc(kept, 1)
                nc.vector.tensor_tensor(st.logits[:, ds(i * GT, GT), :], proj[:, :, CROUT:CROUT + EXPERTS],
                                        st.rb0[:].unsqueeze(1).to_broadcast([P, GT, EXPERTS]), ALU.add)\
                    .then_inc(kept, 1)
                nc.vector.reduce_sum(mom[:, 0, :], xn[:], axis=AX.X).then_inc(mom_ready, 1)
                dve.wait_ge(xsq_ready, i + 1)
                nc.vector.reduce_sum(mom[:, 1, :], sq[:], axis=AX.X).then_inc(mom_ready, 1)
                dve.wait_ge(mom_ready, 2 * i + 2)
                nc.vector.tensor_scalar(st.mv[:, ds(i * GT, GT), 0], mom[:, 0, :], 1.0 / C, None,
                                        ALU.mult).then_inc(mean1_ready, 1)
                nc.vector.tensor_tensor(msq[:], mom[:, 0, :], mom[:, 0, :], ALU.mult).then_inc(mean1_ready, 1)
                dve.wait_ge(mean1_ready, 2 * i + 2)
                nc.vector.scalar_tensor_tensor(vsq[:], msq[:], -1.0 / C, mom[:, 1, :], ALU.mult,
                                               ALU.add).then_inc(vsq_ready, 1)
                dve.wait_ge(vsq_ready, i + 1)
                nc.vector.tensor_scalar(st.mv[:, ds(i * GT, GT), 1], vsq[:], 1.0 / C, None, ALU.mult).then_inc(kept, 1)
                dve.wait_ge(psq_ready, i + 1)
                nc.vector.reduce_sum(ssum[:, 0, :], psq[:, :, 0:QL], axis=AX.X).then_inc(ssummed, 1)
                nc.vector.reduce_sum(ssum[:, 1, :], psq[:, :, QL:QL + KL], axis=AX.X).then_inc(ssummed, 1)
                dve.wait_ge(ssummed, 2 * i + 1)
                nc.vector.tensor_scalar(smean[:, 0, :], ssum[:, 0, :], 1.0 / QL, RMS_EPS, ALU.mult,
                                        ALU.add).then_inc(smean_ready, 1)
                dve.wait_ge(ssummed, 2 * i + 2)
                nc.vector.tensor_scalar(smean[:, 1, :], ssum[:, 1, :], 1.0 / KL, RMS_EPS, ALU.mult,
                                        ALU.add).then_inc(smean_ready, 1)
                halves = proj[:, :, CKR:CKR + ROPE].rearrange("p (b h) d -> p b h d", h=HALVES)
                rk = rot[:].rearrange("p (b h) d -> p b h d", h=HALVES)
                hr = ROPE // 2
                for h in range(HALVES):
                    def tab(t, lo, hi):
                        return t[:, h:h + 1, lo:hi].to_broadcast([P, GRP, hi - lo])
                    nc.vector.tensor_tensor(rk[:, :, h, 0:hr], halves[:, :, h, hr:ROPE], tab(st.sin, 0, hr),
                                            ALU.mult).then_inc(rotated, 1)
                    nc.vector.tensor_tensor(rk[:, :, h, hr:ROPE], halves[:, :, h, 0:hr], tab(st.sin, hr, ROPE),
                                            ALU.mult).then_inc(rotated, 1)
                    nc.vector.tensor_tensor(key[:, h:GT:HALVES, 0:ROPE], halves[:, :, h, :], tab(st.cos, 0, ROPE),
                                            ALU.mult).then_inc(rotated, 1)
                dve.wait_ge(rotated, 6 * i + 6)
                nc.vector.tensor_tensor(key[:, :, 0:ROPE], key[:, :, 0:ROPE], rot[:], ALU.add).then_inc(lat_ready, 1)
                dve.wait_ge(rrms_ready, i + 1)
                nc.vector.tensor_tensor(key[:, :, P - KL:P], proj[:, :, CKV:CKV + KL], bcast(rrms[:, 1, :], KL),
                                        ALU.mult).then_inc(lat_ready, 1)
                nc.vector.tensor_tensor(nq[:], proj[:, :, CQ:CQ + QL], bcast(rrms[:, 0, :], QL),
                                        ALU.mult).then_inc(lat_ready, 1)

        @block.tensor
        def _(pe):
            with pe.Fori(0, NGRP) as i:
                pe.wait_ge(xn_ready, i + 1)
                for t in range(GT):
                    last = nc.tensor.transpose(bk[t // 4][:, (t % 4) * P:(t % 4 + 1) * P], xn[:, t, :], st.eye[:])
                    if t % 4 == 3:
                        last.then_inc(xt_ps, 1)
                for t in range(GT):
                    if t % 4 == 0:
                        pe.wait_ge(xnT_ready, 2 * i + t // 4 + 1)
                    last = nc.tensor.matmul(bk[2 + t // 2][:, (t % 2) * CALL:(t % 2 + 1) * CALL], xnT[:, t, :],
                                            st.w_all[:], start=True, stop=True)
                    if t % 2 == 1:
                        last.then_inc(proj_ps, 1)
                pe.wait_ge(lat_ready, 3 * i + 3)
                for t in range(GT):
                    last = nc.tensor.transpose(bk[t // 4][:, (t % 4) * P:(t % 4 + 1) * P], key[:, t, :], st.eye[:])
                    if t % 4 == 3:
                        last.then_inc(lat_ps, 1)
                for t in range(GT):
                    last = nc.tensor.transpose(bk[2 + t // 4][0:QL, (t % 4) * P:(t % 4 + 1) * P], nq[:, t, :],
                                               st.eye[:])
                    if t % 4 == 3:
                        last.then_inc(lat_ps, 1)

    tmp.close()


def choose(nc, a, st, ctx):
    def sem(name):
        return ctx.enter_context(nc.semaphore(name))

    tmp = ExitStack()

    def sb(name, shape, dt=F32):
        return tmp.enter_context(nc.sbuf_tensor(name, shape, dt))

    left = sb("ch_left", [B, 2, T])
    top = sb("ch_top", [B, 8])
    taken = sb("ch_taken", [B, T])
    rank = sb("ch_rank", [B, T])
    place = sb("ch_place", [B, T])
    place1 = sb("ch_place1", [B, T])
    ones = sb("ch_ones", [B, T])
    mean_w = sb("ch_mean_w", [P, P])
    gm = sb("ch_gm", [P, B])
    gd = sb("ch_gd", [P, B, 3])
    ge = sb("ch_ge", [P, B, 3])
    gs = sb("ch_gs", [P, B])
    gr = sb("ch_gr", [P, B])
    bk = st.bank

    imp_T = sem("ch_imp_T")
    step = sem("ch_vector_step")
    mean_ready = sem("ch_mean_ready")
    place_ready = sem("ch_place_ready")
    place_T = sem("ch_place_T")
    gate_ps = sem("ch_gate_ps")
    gate_off = sem("ch_gate_off")
    gate_exp = sem("ch_gate_exp")

    with nc.Block() as block:

        @block.tensor
        def _(pe):
            for h in range(HALVES):
                last = nc.tensor.transpose(bk[0][0:B, h * P:(h + 1) * P], st.imp[:, h, :], st.eye[:])
            last.then_inc(imp_T, 1)
            pe.wait_ge(mean_ready, 1)
            for h in range(HALVES):
                last = nc.tensor.matmul(bk[1][:, 0:B * 3], mean_w[:], st.gl[:, h].rearrange("p b k -> p (b k)"),
                                        start=(h == 0), stop=(h == HALVES - 1))
            last.then_inc(gate_ps, 1)
            pe.wait_ge(place_ready, 1)
            for h in range(HALVES):
                last = nc.tensor.transpose(bk[2][:, h * B:(h + 1) * B], place1[:, h * P:(h + 1) * P],
                                           st.eye[0:B, 0:B])
            last.then_inc(place_T, 1)

        @block.vector
        def _(dve):
            n = 0

            def after(ins):
                nonlocal n
                n += 1
                ins.then_inc(step, 1)
                dve.wait_ge(step, n)

            nc.vector.memset(mean_w[:], 1.0 / T).then_inc(mean_ready, 1)
            after(nc.vector.memset(ones[:], 1.0))
            dve.wait_ge(imp_T, 1)
            after(nc.vector.tensor_copy(left[:, 0, :], bk[0][0:B, 0:T]))
            for r in range(KEEP // 8):
                after(nc.vector.max(top[:], left[:, r % 2, :]))
                after(nc.vector.match_replace(left[:, (r + 1) % 2, :], top[:], left[:, r % 2, :], GONE))
            after(nc.vector.tensor_scalar(taken[:], left[:, 0, :], GONE, None, ALU.is_equal))
            after(nc.vector.tensor_tensor_scan(rank[:], ones[:], taken[:], 0.0, ALU.mult, ALU.add))
            after(nc.vector.tensor_tensor(place[:], rank[:], taken[:], ALU.mult))
            nc.vector.tensor_scalar(place1[:], place[:], -1.0, None, ALU.add).then_inc(place_ready, 1)
            dve.wait_ge(gate_ps, 1)
            gl = bk[1][:, 0:B * 3].rearrange("p (b k) -> p b k", k=3)
            after(nc.vector.reduce_max(gm[:], gl, axis=AX.X))
            nc.vector.tensor_tensor(gd[:], gl, bcast(gm[:], 3), ALU.subtract).then_inc(gate_off, 1)
            dve.wait_ge(gate_exp, 1)
            after(nc.vector.reduce_sum(gs[:], ge[:], axis=AX.X))
            after(nc.vector.reciprocal(gr[:], gs[:]))
            after(nc.vector.tensor_tensor(gd[:], ge[:], bcast(gr[:], 3), ALU.mult))
            after(nc.vector.tensor_scalar(st.gates[:, :, 0:3:2], gd[:, :, 0:3:2], 1.0 / WEIGHT_SCALE, None, ALU.mult))
            after(nc.vector.tensor_copy(st.gates[:, :, 1:2], gd[:, :, 1:2]))
            dve.wait_ge(place_T, 1)
            after(nc.vector.tensor_copy(st.place[:].rearrange("p b h -> p h b"),
                                        bk[2][:, 0:HALVES * B].rearrange("p (h b) -> p h b", b=B)))

        @block.scalar
        def _(act):
            act.wait_ge(gate_off, 1)
            nc.scalar.activation(ge[:], gd[:], ACT.Exp).then_inc(gate_exp, 1)

    tmp.close()


def selected(nc, a, st, ctx):
    def sem(name):
        return ctx.enter_context(nc.semaphore(name))

    tmp = ExitStack()

    def sb(name, shape, dt=F32):
        return tmp.enter_context(nc.sbuf_tensor(name, shape, dt))

    xn = sb("se_xn", [P, GT, C])
    pick = sb("se_pick", [P, GT, KEEP])
    selT = sb("se_selT", [P, P])
    keys = sb("se_keys", [P, HEADS, HD])
    rot = sb("se_rot", [P, HEADS, ROPE])
    keysT = sb("se_keysT", [HD, GRP, HEADS, KEEP])
    vals = sb("se_vals", [P, GRP, QUADS, QUAD * (VD + 1)])
    bk = st.bank

    xn_in = sem("se_xn_in")
    picked = sem("se_picked")
    sel_ps = sem("se_sel_ps")
    selT_ready = sem("se_selT_ready")
    keys_ps = sem("se_keys_ps")
    roped = sem("se_roped")
    rot_ready = sem("se_rot_ready")
    keys_ready = sem("se_keys_ready")
    keysT_ps = sem("se_keysT_ps")
    keysT_ready = sem("se_keysT_ready")
    vals_ps = sem("se_vals_ps")
    vals_init = sem("se_vals_init")
    vals_ready = sem("se_vals_ready")
    keys_out = sem("se_keys_out")
    vals_out = sem("se_vals_out")
    xn_dram = st.d_xn.rearrange("t p c -> p t c")
    hr = ROPE // 2

    with nc.Block() as block:

        @block.sync
        def _(sp):
            def load(i):
                sp.dma_start(xn[:], xn_dram[:, ds(i * GT, GT), :]).then_inc(xn_in, 16)

            def store(i):
                sp.wait_ge(vals_ready, QUAD * GRP * (i + 2))
                quads = ds(i * GRP * QUADS, GRP * QUADS)
                sp.dma_start(st.d_vs[quads].rearrange("q p n -> p q n"),
                             vals[:].rearrange("p b g n -> p (b g) n")).then_inc(vals_out, 16)
                sp.wait_ge(keysT_ready, QUADS * (i + 2))
                sp.dma_start(st.d_ks[quads].rearrange("q p n -> p q n"),
                             keysT[:].rearrange("p b (g h) n -> p (b g) (h n)", g=QUADS)).then_inc(keys_out, 16)

            sp.sem_inc(keys_out, 16)
            sp.sem_inc(vals_out, 16)
            load(0)
            with sp.Fori(0, NGRP - 1) as i:
                sp.wait_ge(sel_ps, i + 1)
                load(i + 1)
                store(i)
            store(NGRP - 1)
            sp.wait_ge(keys_out, 16 * NGRP + 16)
            sp.wait_ge(vals_out, 16 * NGRP + 16)

        @block.vector
        def _(dve):
            nc.vector.memset(vals[:], 0.0).then_inc(vals_init, 1)
            dve.wait_ge(vals_init, 1)
            for j in range(QUAD):
                nc.vector.memset(vals[KEEP * j:KEEP * (j + 1), :, :, j * (VD + 1) + VD:(j + 1) * (VD + 1)],
                                 1.0).then_inc(vals_init, 1)
            dve.wait_ge(vals_init, 1 + QUAD)
            with dve.Fori(0, NGRP) as i:
                nc.vector.tensor_tensor(pick[:], st.iota[:].unsqueeze(1).to_broadcast([P, GT, KEEP]),
                                        bcast(st.place[:, ds(i * GRP, GRP), :].rearrange("p b h -> p (b h)"), KEEP),
                                        ALU.is_equal).then_inc(picked, 1)
                dve.wait_ge(sel_ps, i + 1)
                nc.vector.tensor_copy(selT[:], bk[0][:, 0:P]).then_inc(selT_ready, 1)
                for g in range(QUADS):
                    dve.wait_ge(keys_ps, QUADS * i + g + 1)
                    k = bk[1 + g][:, 0:QUAD * HD].rearrange("p (h d) -> p h d", d=HD)
                    hs = slice(QUAD * g, QUAD * (g + 1))

                    def tab(t, lo, hi):
                        return t[:, lo:hi].unsqueeze(1).to_broadcast([P, QUAD, hi - lo])
                    nc.vector.tensor_tensor(rot[:, hs, 0:hr], k[:, :, hr:ROPE], tab(st.sin_sel, 0, hr),
                                            ALU.mult).then_inc(rot_ready, 1)
                    nc.vector.tensor_tensor(rot[:, hs, hr:ROPE], k[:, :, 0:hr], tab(st.sin_sel, hr, ROPE),
                                            ALU.mult).then_inc(rot_ready, 1)
                    nc.vector.tensor_tensor(keys[:, hs, 0:ROPE], k[:, :, 0:ROPE], tab(st.cos_sel, 0, ROPE),
                                            ALU.mult).then_inc(rot_ready, 1)
                    nc.vector.tensor_copy(keys[:, hs, ROPE:HD], k[:, :, ROPE:HD]).then_inc(roped, 1)
                    dve.wait_ge(rot_ready, 3 * (QUADS * i + g + 1))
                    nc.vector.tensor_tensor(keys[:, hs, 0:ROPE], keys[:, hs, 0:ROPE], rot[:, hs, :],
                                            ALU.add).then_inc(keys_ready, 1)

        @block.scalar
        def _(act):
            act.sem_inc(vals_ready, QUAD * GRP)
            act.sem_inc(keysT_ready, QUADS)
            act.wait_ge(vals_init, 1 + QUAD)
            with act.Fori(0, NGRP) as i:
                act.wait_ge(vals_ps, i + 1)
                act.wait_ge(vals_out, 16 * i + 16)
                pv = bk[5][:, :].rearrange("p (g h d) -> p g h d", g=QUADS, h=QUAD)
                for b in range(GRP):
                    for j in range(QUAD):
                        nc.scalar.activation(vals[KEEP * j:KEEP * (j + 1), b, :, j * (VD + 1):j * (VD + 1) + VD],
                                             pv[KEEP * b:KEEP * (b + 1), :, j, :], ACT.Copy).then_inc(vals_ready, 1)
                act.wait_ge(keys_out, 16 * i + 16)
                for g in range(QUADS):
                    act.wait_ge(keysT_ps, QUADS * i + g + 1)
                    nc.scalar.activation(keysT[:, :, QUAD * g:QUAD * (g + 1), :].rearrange("p b h j -> p h b j"),
                                         bk[1 + g][0:HD, :].rearrange("p (h b j) -> p h b j", h=QUAD, b=GRP),
                                         ACT.Copy).then_inc(keysT_ready, 1)

        @block.tensor
        def _(pe):
            with pe.Fori(0, NGRP) as i:
                pe.wait_ge(xn_in, 16 * i + 16)
                pe.wait_ge(picked, i + 1)
                for b in range(GRP):
                    for h in range(HALVES):
                        last = nc.tensor.matmul(bk[0][:, b * KEEP:(b + 1) * KEEP], xn[:, b * HALVES + h, :],
                                                pick[:, b * HALVES + h, :], start=(h == 0), stop=(h == HALVES - 1))
                last.then_inc(sel_ps, 1)
                pe.wait_ge(selT_ready, i + 1)
                pe.wait_ge(vals_ready, QUAD * GRP * (i + 1))
                nc.tensor.matmul(bk[5][:, :], selT[:], st.w_vs[:], start=True, stop=True).then_inc(vals_ps, 1)
                for g in range(QUADS):
                    pe.wait_ge(keysT_ready, QUADS * i + g + 1)
                    nc.tensor.matmul(bk[1 + g][:, 0:QUAD * HD], selT[:],
                                     st.w_ks[:, QUAD * g:QUAD * (g + 1), :].rearrange("p h d -> p (h d)"),
                                     start=True, stop=True).then_inc(keys_ps, 1)
                for g in range(QUADS):
                    pe.wait_ge(keys_ready, QUADS * i + g + 1)
                    for j in range(QUAD):
                        last = nc.tensor.transpose(bk[1 + g][0:HD, j * P:(j + 1) * P], keys[:, QUAD * g + j, :],
                                                   st.eye[:])
                    last.then_inc(keysT_ps, 1)

    tmp.close()


def attention(nc, a, st, ctx):
    def sem(name):
        return ctx.enter_context(nc.semaphore(name))

    tmp = ExitStack()

    def sb(name, shape, dt=F32):
        return tmp.enter_context(nc.sbuf_tensor(name, shape, dt))

    UNITS = QUAD * HALVES
    VW = VD + 1
    UW = 2 * 3 * VD
    hr = ROPE // 2
    nqT = sb("at_nqT", [QL, T])
    xnT = sb("at_xnT", [P, T])
    latT = sb("at_latT", [P, T])
    keys = sb("at_keys", [P, 2, 1 + QUAD, T])
    qT = sb("at_qT", [P, QUAD, T])
    ksel = sb("at_ksel", [HD, QUAD * KEEP])
    vsel = sb("at_vsel", [P, QUAD * VW])
    vals = sb("at_vals", [P, 2, HALVES * 2 * QUAD, 3, VD], BF16)
    v_rest = sb("at_v_rest", [P, HALVES * 2 * QUAD, VD])
    q_tok = sb("at_q_tok", [P, HALVES, QUAD, QW])
    k_tok = sb("at_k_tok", [P, HALVES, QUAD, HD])
    q_sin = sb("at_q_sin", [P, HALVES, QUAD, ROPE])
    q_cos = sb("at_q_cos", [P, HALVES, QUAD, ROPE])
    k_sin = sb("at_k_sin", [P, HALVES, QUAD, ROPE])
    k_cos = sb("at_k_cos", [P, HALVES, QUAD, ROPE])
    prob = sb("at_prob", [P, 2, 2 * T])
    high = sb("at_high", [P, 2, 2 * T], F16)
    low = sb("at_low", [P, 2, 2 * T], F16)
    nmax = sb("at_nmax", [P, UNITS, 2])
    max2 = sb("at_max2", [P, HALVES * QUAD])
    off2 = sb("at_off2", [P, HALVES * QUAD, KEEP])
    prob2 = sb("at_prob2", [P, HALVES, QUAD * KEEP])
    prob2T = sb("at_prob2T", [P, HALVES, P])
    sums = sb("at_sums", [P, 2, HALVES, 3, QUAD])
    inv = sb("at_inv", [P, HALVES, 3, QUAD])
    share = sb("at_share", [P, 2, HALVES, 3, QUAD])
    osum = sb("at_osum", [P, 2, HALVES, 3, QUAD, VD])
    part = sb("at_part", [P, HALVES, 3, QUAD, VD])
    part13 = sb("at_part13", [P, HALVES, QUAD * VD])
    o = sb("at_o", [P, HALVES, QUAD * VD])

    S = st.bank[0:2]
    PT = st.bank[2:4]
    O = st.bank[4:6]
    M = st.bank[6:8]
    HM = [M[0], M[0], M[0], M[1]]

    nq_in = sem("at_nq_in")
    tok_in = sem("at_tok_in")
    shared_in = [sem(f"at_shared_in{s}") for s in range(2)]
    ksel_in = sem("at_ksel_in")
    vsel_in = sem("at_vsel_in")
    s_ps = sem("at_s_ps")
    s2_ps = sem("at_s2_ps")
    q_ps = sem("at_q_ps")
    k_ps = sem("at_k_ps")
    heads_ps = sem("at_heads_ps")
    v_ps = sem("at_v_ps")
    pT_ps = sem("at_pT_ps")
    p2T_ps = sem("at_p2T_ps")
    av2_done = sem("at_av2_done")
    av_done = sem("at_av_done")
    q_taken = sem("at_q_taken")
    k_taken = sem("at_k_taken")
    q_turned = sem("at_q_rotated")
    k_turned = sem("at_k_rotated")
    q_roped = sem("at_q_roped")
    k_roped = sem("at_k_roped")
    heads_ready = sem("at_heads_ready")
    v_high = sem("at_v_high")
    v_rested = sem("at_v_rested")
    v_mid = sem("at_v_mid")
    v_ready = sem("at_v_ready")
    nmax_ready = sem("at_nmax_ready")
    max2_ready = sem("at_max2_ready")
    s2_taken = sem("at_s2_taken")
    p_ready = sem("at_p_ready")
    p2_ready = sem("at_p2_ready")
    high_ready = sem("at_high_ready")
    low_ready = sem("at_low_ready")
    p2T_ready = sem("at_p2T_ready")
    sum2_ready = sem("at_sum2_ready")
    inv_ready = sem("at_inv_ready")
    share_ready = sem("at_share_ready")
    osum_ready = sem("at_osum_ready")
    o2_taken = sem("at_o2_taken")
    weighed = sem("at_weighed")
    o_sum13 = sem("at_o_sum13")
    o_ready = sem("at_o_ready")
    o_out = sem("at_o_out")
    init = sem("at_init")

    def unit_keys(u):
        return P * (u % HALVES + 1)

    def wait(eng, s, n):
        if not isinstance(n, int) or n > 0:
            eng.wait_ge(s, n)

    def more(i):
        return not (isinstance(i, int) and i >= NQ - 2)

    def quads(eng, body):
        body(0, 0, False)
        body(1, 1, False)
        with eng.Fori(1, NQ // 2 - 1) as j:
            body(2 * j, 0, False)
            body(2 * j + 1, 1, False)
        body(NQ - 2, 0, False)
        body(NQ - 1, 1, True)

    def ahead(i, s, u, last):
        if u < UNITS:
            return i, s, u
        return None if last else (i + 1, 1 - s, u - UNITS)

    with nc.Block() as block:

        @block.sync
        def _(sp):
            def load_nq(q):
                sp.dma_start(nqT[:], st.d_nqT[ds(q // QUADS, 1)].rearrange("b c n -> c (b n)")).then_inc(nq_in, 16)

            def load_tok(q):
                sp.dma_start(xnT[:], st.d_xnT[ds(q // QUADS, 1)].rearrange("b c n -> c (b n)")).then_inc(tok_in, 16)
                sp.dma_start(latT[:], st.d_kvT[ds(q // QUADS, 1)].rearrange("b c n -> c (b n)")).then_inc(tok_in, 16)

            def load_shared(q, s):
                sp.dma_start(keys[:, s, 0, :],
                             st.d_kvT[ds(q // QUADS, 1)].rearrange("b c n -> c (b n)")).then_inc(shared_in[s], 16)

            def load_ksel(q):
                sp.dma_start(ksel[:], st.d_ks[ds(q, 1)].rearrange("o p n -> p (o n)")).then_inc(ksel_in, 16)

            def load_vsel(q):
                sp.dma_start(vsel[:], st.d_vs[ds(q, 1)].rearrange("o p n -> p (o n)")).then_inc(vsel_in, 16)

            def store(q):
                sp.wait_ge(o_ready, q + 1)
                sp.dma_start(st.d_o[ds((q // QUADS) * HALVES, HALVES), :, ds((q % QUADS) * QUAD * VD, QUAD * VD)]
                             .rearrange("h p n -> p h n"), o[:]).then_inc(o_out, 16)

            def body(i, s, last):
                if more(i):
                    sp.wait_ge(q_ps, HALVES * (i + 2))
                    load_nq(i + 2)
                if not last:
                    sp.wait_ge(s2_ps, i + 1)
                    load_ksel(i + 1)
                if more(i):
                    sp.wait_ge(v_ps, i + 2)
                    load_tok(i + 2)
                if not last:
                    sp.wait_ge(av2_done, i + 1)
                    load_vsel(i + 1)
                if more(i):
                    sp.wait_ge(s_ps, UNITS * (i + 1))
                    load_shared(i + 2, s)
                if not (isinstance(i, int) and i == 0):
                    store(i - 1)

            load_nq(0)
            load_tok(0)
            load_shared(0, 0)
            load_shared(1, 1)
            load_ksel(0)
            load_vsel(0)
            sp.wait_ge(q_ps, HALVES)
            load_nq(1)
            sp.wait_ge(v_ps, 1)
            load_tok(1)
            quads(sp, body)
            store(NQ - 1)
            sp.wait_ge(o_out, 16 * NQ)

        @block.gpsimd
        def _(pool):
            def rope(q, t, tok, sin, cos, taken, turned, roped):
                def tab(x, lo, hi):
                    return x[:, t, lo:hi].unsqueeze(1).to_broadcast([P, QUAD, hi - lo])
                pool.wait_ge(taken, HALVES * q + t + 1)
                nc.gpsimd.tensor_tensor(sin[:, t, :, 0:hr], tok[:, t, :, hr:ROPE], tab(st.sin, 0, hr), ALU.mult)
                nc.gpsimd.tensor_tensor(sin[:, t, :, hr:ROPE], tok[:, t, :, 0:hr], tab(st.sin, hr, ROPE), ALU.mult)
                nc.gpsimd.tensor_tensor(cos[:, t], tok[:, t, :, 0:ROPE], tab(st.cos, 0, ROPE),
                                        ALU.mult).then_inc(turned, 1)
                pool.wait_ge(turned, HALVES * q + t + 1)
                nc.gpsimd.tensor_tensor(tok[:, t, :, 0:ROPE], cos[:, t], sin[:, t], ALU.add).then_inc(roped, 1)

            def rope_k(q, t):
                rope(q, t, k_tok, k_sin, k_cos, k_taken, k_turned, k_roped)

            def rope_q(q, t):
                rope(q, t, q_tok, q_sin, q_cos, q_taken, q_turned, q_roped)

            def values(q, s):
                pool.wait_ge(v_mid, q + 1)
                nc.gpsimd.tensor_tensor(vals[:, s, :, 2, :], v_rest[:], vals[:, s, :, 1, :],
                                        ALU.subtract).then_inc(v_ready, 1)

            def combine(q, s):
                pool.wait_ge(share_ready, HALVES * (q + 1))
                pool.wait_ge(osum_ready, UNITS * (q + 1))
                pool.wait_ge(o2_taken, q + 1)
                wait(pool, o_ready, q)
                for t in range(HALVES):
                    nc.gpsimd.tensor_tensor(part[:, t], osum[:, s, t], bcast(share[:, s, t], VD),
                                            ALU.mult).then_inc(weighed, 1)
                pool.wait_ge(weighed, HALVES * (q + 1))
                pv = part[:].rearrange("p t k h d -> p t k (h d)")
                nc.gpsimd.tensor_tensor(part13[:], pv[:, :, 0, :], pv[:, :, 2, :], ALU.add).then_inc(o_sum13, 1)
                wait(pool, o_out, 16 * q)
                pool.wait_ge(o_sum13, q + 1)
                nc.gpsimd.tensor_tensor(o[:], part13[:], pv[:, :, 1, :], ALU.add).then_inc(o_ready, 1)

            def body(i, s, last):
                if not last:
                    rope_k(i + 1, 1)
                    rope_q(i + 1, 0)
                    rope_q(i + 1, 1)
                if not (isinstance(i, int) and i == 0):
                    combine(i - 1, 1 - s)
                if not last:
                    values(i + 1, 1 - s)
                if more(i):
                    rope_k(i + 2, 0)

            for t in range(HALVES):
                rope_k(0, t)
                rope_q(0, t)
            values(0, 0)
            rope_k(1, 0)
            quads(pool, body)
            combine(NQ - 1, 1)

        @block.vector
        def _(dve):
            def unit_max(i, s, u):
                dve.wait_ge(s_ps, UNITS * i + u + 1)
                nc.vector.tensor_reduce(nmax[:, u, :],
                                        S[u % 2][:, 0:2 * unit_keys(u)].rearrange("p (a k) -> p a k", a=2),
                                        AX.X, ALU.max, negate=True).then_inc(nmax_ready, 1)

            def unit_low(i, u):
                dve.wait_ge(high_ready, UNITS * i + u + 1)
                n = 2 * unit_keys(u)
                nc.vector.scalar_tensor_tensor(low[:, u % 2, 0:n], PT[u % 2][:, 0:n], WEIGHT_SCALE,
                                               high[:, u % 2, 0:n], ALU.mult, ALU.subtract).then_inc(low_ready, 1)

            def unit_sum(i, s, u):
                h, t = divmod(u, HALVES)
                dve.wait_ge(av_done, UNITS * i + u + 1)
                if u < HALVES:
                    wait(dve, weighed, HALVES * (i - 1))
                nc.vector.reduce_sum(osum[:, s, t, 0:3:2, h, :],
                                     O[t][:, 0:UW].rearrange("p (k j d) -> p k d j", k=2, j=3), axis=AX.X).then_inc(osum_ready, 1)

            def rest(q, s):
                dve.wait_ge(v_high, q + 1)
                wait(dve, v_ready, q)
                nc.vector.tensor_tensor(v_rest[:], M[0].rearrange("p (n d) -> p n d", d=VD), vals[:, s, :, 0, :],
                                        ALU.subtract).then_inc(v_rested, 1)

            def chosen_off(i):
                dve.wait_ge(s2_ps, i + 1)
                s2 = M[1][:, 0:HALVES * QUAD * KEEP].rearrange("p (n k) -> p n k", k=KEEP)
                nc.vector.reduce_max(max2[:], s2, axis=AX.X).then_inc(max2_ready, 1)
                dve.wait_ge(max2_ready, i + 1)
                nc.vector.tensor_tensor(off2[:], s2, bcast(max2[:], KEEP), ALU.subtract).then_inc(s2_taken, 1)

            def body(i, s, last):
                for u in range(UNITS):
                    if n := ahead(i, s, u + 2, last):
                        unit_max(*n)
                    if u >= 2:
                        unit_sum(i, s, u - 2)
                    elif not (isinstance(i, int) and i == 0):
                        unit_sum(i - 1, 1 - s, UNITS - 2 + u)
                    unit_low(i, u)
                    if u == 3:
                        chosen_off(i)
                    if u == 2 and not last:
                        rest(i + 1, 1 - s)
                    if u == 5:
                        dve.wait_ge(p2_ready, i + 1)
                        nc.vector.reduce_sum(sums[:, s, :, 1, :], prob2[:].rearrange("p t (h k) -> p t h k", h=QUAD),
                                             axis=AX.X).then_inc(sum2_ready, 1)
                    if u == 7:
                        dve.wait_ge(p_ready, UNITS * (i + 1))
                        dve.wait_ge(sum2_ready, i + 1)
                        nc.vector.reciprocal(inv[:], sums[:, s]).then_inc(inv_ready, 1)
                        dve.wait_ge(inv_ready, i + 1)
                        gate = st.gates[:, ds(i // QUADS, 1), :]
                        for t in range(HALVES):
                            nc.vector.tensor_tensor(share[:, s, t], inv[:, t],
                                                    gate.rearrange("p o k -> p (o k)").unsqueeze(2)
                                                    .to_broadcast([P, 3, QUAD]), ALU.mult).then_inc(share_ready, 1)

            for s in range(2):
                nc.vector.memset(keys[:, s, 1:1 + QUAD, :], 0.0).then_inc(init, 1)
            rest(0, 0)
            unit_max(0, 0, 0)
            unit_max(0, 0, 1)
            quads(dve, body)
            for u in (UNITS - 2, UNITS - 1):
                unit_sum(NQ - 1, 1, u)

        @block.scalar
        def _(act):
            def unit_exp(i, s, u):
                act.wait_ge(nmax_ready, UNITS * i + u + 1)
                if u == 0:
                    wait(act, inv_ready, i - 1)
                h, t = divmod(u, HALVES)
                n = unit_keys(u)
                for k in range(2):
                    last = nc.scalar.activation(prob[:, u % 2, k * n:(k + 1) * n], S[u % 2][:, k * n:(k + 1) * n],
                                                ACT.Exp, bias=nmax[:, u, k:k + 1],
                                                accum_out=sums[:, s, t, 2 * k, h:h + 1])
                last.then_inc(p_ready, 1)

            def unit_high(i, u):
                act.wait_ge(pT_ps, UNITS * i + u + 1)
                wait(act, av_done, UNITS * i + u - 1)
                n = 2 * unit_keys(u)
                nc.scalar.activation(high[:, u % 2, 0:n], PT[u % 2][:, 0:n], ACT.Copy,
                                     scale=WEIGHT_SCALE).then_inc(high_ready, 1)

            def take_k(q, t):
                act.wait_ge(k_ps, HALVES * q + t + 1)
                nc.scalar.activation(k_tok[:, t].rearrange("p h d -> p (h d)"), M[0][:, 0:QUAD * HD],
                                     ACT.Copy).then_inc(k_taken, 1)

            def take_q(q, t):
                act.wait_ge(q_ps, HALVES * q + t + 1)
                nc.scalar.activation(q_tok[:, t].rearrange("p h d -> p (h d)"), M[1][:, 0:QUAD * QW],
                                     ACT.Copy).then_inc(q_taken, 1)

            def head(q, s, h):
                act.wait_ge(heads_ps, QUAD * q + h + 1)
                nc.scalar.activation(qT[:, h, :], HM[h][:, 0:T], ACT.Copy)
                nc.scalar.activation(keys[0:HD, s, 1 + h, :], HM[h][0:HD, T:2 * T],
                                     ACT.Copy).then_inc(heads_ready, 1)

            def values(q, s):
                act.wait_ge(v_ps, q + 1)
                wait(act, av_done, UNITS * (q - 1))
                nc.scalar.activation(vals[:, s, :, 0, :], M[0].rearrange("p (n d) -> p n d", d=VD),
                                     ACT.Copy).then_inc(v_high, 1)

            def middle(q, s):
                act.wait_ge(v_rested, q + 1)
                nc.scalar.activation(vals[:, s, :, 1, :], v_rest[:], ACT.Copy).then_inc(v_mid, 1)

            def body(i, s, last):
                q, r = i + 1, 1 - s
                for u in range(UNITS):
                    if n := ahead(i, s, u + 1, last):
                        unit_exp(*n)
                    unit_high(i, u)
                    if u == 4:
                        act.wait_ge(s2_taken, i + 1)
                        wait(act, sum2_ready, i)
                        nc.scalar.activation(prob2[:].rearrange("p q n -> p (q n)"),
                                             off2[:].rearrange("p n k -> p (n k)"), ACT.Exp).then_inc(p2_ready, 1)
                    if u >= 4 and not last and u < 7:
                        head(q, r, u - 4)
                    if u == 5:
                        act.wait_ge(p2T_ps, i + 1)
                        nc.scalar.activation(prob2T[:].rearrange("p q n -> p (q n)"), M[1][:, 0:HALVES * P],
                                             ACT.Copy).then_inc(p2T_ready, 1)
                    if u == 6:
                        act.wait_ge(av2_done, i + 1)
                        nc.scalar.activation(osum[:, s, :, 1].rearrange("p t h d -> p t (h d)"),
                                             M[1][:, 0:HALVES * QUAD * VD].rearrange("p (t n) -> p t n", t=HALVES),
                                             ACT.Copy).then_inc(o2_taken, 1)
                    if last:
                        continue
                    if u == 0:
                        take_k(q, 1)
                        take_q(q, 0)
                    if u == 1:
                        take_q(q, 1)
                        values(q, r)
                    if u == 3:
                        middle(q, r)
                    if u == 7:
                        head(q, r, QUAD - 1)
                        if more(i):
                            take_k(q + 1, 0)

            act.wait_ge(init, 2)
            for t in range(HALVES):
                take_k(0, t)
                take_q(0, t)
            values(0, 0)
            middle(0, 0)
            for h in range(QUAD):
                head(0, 0, h)
            take_k(1, 0)
            unit_exp(0, 0, 0)
            quads(act, body)

        @block.tensor
        def _(pe):
            def queries(q, t):
                if t == 0:
                    wait(pe, heads_ready, QUAD * q)
                    pe.wait_ge(nq_in, 16 * (q + 1))
                else:
                    pe.wait_ge(q_taken, HALVES * q + 1)
                w = st.w_q[:, ds((q % QUADS) * QUAD, QUAD), :].rearrange("p h d -> p (h d)")
                nc.tensor.matmul(M[1][:, 0:QUAD * QW], nqT[:, t * P:(t + 1) * P], w, start=True,
                                 stop=True).then_inc(q_ps, 1)

            def window_keys(q, t):
                if t == 0:
                    wait(pe, heads_ready, QUAD * q - 1)
                    pe.wait_ge(tok_in, 32 * (q + 1))
                else:
                    pe.wait_ge(k_taken, HALVES * q + 1)
                w = st.w_kw[:, ds((q % QUADS) * QUAD, QUAD), :].rearrange("p h d -> p (h d)")
                nc.tensor.matmul(M[0][:, 0:QUAD * HD], xnT[:, t * P:(t + 1) * P], w, start=True,
                                 stop=True).then_inc(k_ps, 1)

            def values(q):
                pe.wait_ge(k_taken, HALVES * (q + 1))
                cols = ds((q % QUADS) * QUAD * VD, QUAD * VD)
                n = QUAD * VD
                for t in range(HALVES):
                    nc.tensor.matmul(M[0][:, 2 * t * n:(2 * t + 1) * n], latT[:, t * P:(t + 1) * P],
                                     st.w_v1[:, cols], start=True, stop=True)
                    last = nc.tensor.matmul(M[0][:, (2 * t + 1) * n:(2 * t + 2) * n], xnT[:, t * P:(t + 1) * P],
                                            st.w_vw[:, cols], start=True, stop=True)
                last.then_inc(v_ps, 1)

            def head(q, h):
                if h == 0:
                    pe.wait_ge(q_roped, HALVES * (q + 1))
                    pe.wait_ge(k_roped, HALVES * (q + 1))
                    pe.wait_ge(v_rested, q + 1)
                elif h == QUAD - 1:
                    wait(pe, o2_taken, q)
                else:
                    pe.wait_ge(heads_ready, QUAD * q + h)
                for t in range(HALVES):
                    nc.tensor.transpose(HM[h][:, t * P:(t + 1) * P], q_tok[:, t, h, :], st.eye[:])
                    last = nc.tensor.transpose(HM[h][0:HD, T + t * P:T + (t + 1) * P], k_tok[:, t, h, :],
                                               st.eye[:])
                last.then_inc(heads_ps, 1)

            def scores(i, s, u):
                h, t = divmod(u, HALVES)
                n = unit_keys(u)
                if t == 0:
                    pe.wait_ge(heads_ready, QUAD * i + h + 1)
                if u == 0:
                    pe.wait_ge(shared_in[s], 16 * (i // 2 + 1))
                wait(pe, p_ready, UNITS * i + u - 1)
                out = S[u % 2][:, 0:2 * n].rearrange("p (a k) -> p a k", a=2)
                nc.tensor.matmul(out, qT[:, h, t * P:(t + 1) * P], keys[:, s, 0:h + 2:h + 1, 0:n], start=True,
                                 stop=False)
                nc.tensor.matmul(out[:, :, n - P:n], st.eye16[:],
                                 st.causal[:].unsqueeze(1).to_broadcast([P, 2, P]), start=False,
                                 stop=True).then_inc(s_ps, 1)

            def chosen(t):
                for h in range(QUAD):
                    c = (t * QUAD + h) * KEEP
                    last = nc.tensor.matmul(M[1][:, c:c + KEEP], qT[0:HD, h, t * P:(t + 1) * P],
                                            ksel[:, h * KEEP:(h + 1) * KEEP], start=True, stop=True)
                return last

            def turn(i, u):
                pe.wait_ge(p_ready, UNITS * i + u + 1)
                wait(pe, low_ready, UNITS * i + u - 1)
                for k in range(2 * (u % HALVES + 1)):
                    last = nc.tensor.transpose(PT[u % 2][:, k * P:(k + 1) * P], prob[:, u % 2, k * P:(k + 1) * P],
                                               st.eye[:])
                last.then_inc(pT_ps, 1)

            def weigh(i, s, u):
                h, t = divmod(u, HALVES)
                pe.wait_ge(low_ready, UNITS * i + u + 1)
                if u == 0:
                    pe.wait_ge(v_ready, i + 1)
                wait(pe, osum_ready, UNITS * i + u - 1)
                for k in range(2):
                    o0 = k * 3 * VD
                    for kt in range(t + 1):
                        blk = slice((k * (t + 1) + kt) * P, (k * (t + 1) + kt + 1) * P)
                        v = vals[:, s, (kt * 2 + k) * QUAD + h].rearrange("p j d -> p (j d)")
                        nc.tensor.matmul(O[t][:, o0:o0 + 3 * VD], high[:, u % 2, blk], v, start=(kt == 0),
                                         stop=False, skip_group_check=True)
                        last = nc.tensor.matmul(O[t][:, o0:o0 + 2 * VD], low[:, u % 2, blk], v[:, 0:2 * VD],
                                                start=False, stop=(kt == t), skip_group_check=True)
                last.then_inc(av_done, 1)

            def body(i, s, last):
                q = i + 1
                for u in range(UNITS):
                    if n := ahead(i, s, u + 2, last):
                        scores(*n)
                    turn(i, u)
                    if u == 0 and not last:
                        window_keys(q, 1)
                        queries(q, 0)
                    if u == 1 and not last:
                        queries(q, 1)
                        values(q)
                    if u == 2:
                        pe.wait_ge(ksel_in, 16 * (i + 1))
                        if last:
                            pe.wait_ge(heads_ready, QUAD * (i + 1))
                        else:
                            pe.wait_ge(q_taken, HALVES * (q + 1))
                        chosen(0)
                        chosen(1).then_inc(s2_ps, 1)
                    if 4 <= u <= 6 and not last:
                        head(q, u - 4)
                    if u == 5:
                        pe.wait_ge(p2_ready, i + 1)
                        for t in range(HALVES):
                            l = nc.tensor.transpose(M[1][:, t * P:(t + 1) * P], prob2[:, t, :], st.eye[:])
                        l.then_inc(p2T_ps, 1)
                    if u == 6:
                        pe.wait_ge(p2T_ready, i + 1)
                        pe.wait_ge(vsel_in, 16 * (i + 1))
                        for t in range(HALVES):
                            l = nc.tensor.matmul(M[1][:, t * QUAD * VD:(t + 1) * QUAD * VD], prob2T[:, t, :],
                                                 vsel[:].rearrange("p (h d) -> p h d", d=VW)[:, :, 0:VD], start=True,
                                                 stop=True)
                        l.then_inc(av2_done, 1)
                    if u == 7 and not last:
                        head(q, QUAD - 1)
                        if more(i):
                            window_keys(q + 1, 0)
                    if u >= 1:
                        weigh(i, s, u - 1)
                    elif not (isinstance(i, int) and i == 0):
                        weigh(i - 1, 1 - s, UNITS - 1)

            for t in range(HALVES):
                window_keys(0, t)
                queries(0, t)
            values(0)
            for h in range(QUAD):
                head(0, h)
            window_keys(1, 0)
            scores(0, 0, 0)
            scores(0, 0, 1)
            quads(pe, body)
            weigh(NQ - 1, 1, UNITS - 1)

    tmp.close()


def experts(nc, a, st, ctx):
    def sem(name):
        return ctx.enter_context(nc.semaphore(name))

    tmp = ExitStack()

    def sb(name, shape, dt=F32):
        return tmp.enter_context(nc.sbuf_tensor(name, shape, dt))

    LE = LAYERS * EXPERTS
    W = CHUNK * P
    PER = EXPERTS * FT
    state, logits, mv = st.state, st.logits, st.mv
    w1_raw = sb("mo_w1_raw", [P, EXPERTS, FF])
    w1 = sb("mo_w1", [P, EXPERTS, FF])
    w2 = sb("mo_w2", [P, 2, EXPERTS, FT, C])
    b1_rows = sb("mo_b1_rows", [LE * FT, P])
    gb_rows = sb("mo_gb_rows", [2 * LE, C])
    b1T = sb("mo_b1T", [P, LE * FT])
    gbT = sb("mo_gbT", [P, 2 * LE])
    bias = sb("mo_bias", [P, PER])
    rw = sb("mo_rw", [C, LAYERS, EXPERTS])
    rb = sb("mo_rb", [P, LE])
    b2_in = sb("mo_b2_in", [3 * 32, LE * C])
    b2_rest = sb("mo_b2_rest", [3 * 32, LE * C])
    b2_part = sb("mo_b2_part", [3 * 32, LE * C], BF16)
    ones = sb("mo_ones", [3 * 32, P], BF16)
    xh = sb("mo_xh", [P, CHUNK, C])
    xhT = sb("mo_xhT", [P, W])
    h = sb("mo_h", [P, 2, FT, W])
    fresh = sb("mo_fresh", [P, CHUNK, C])
    freshT = sb("mo_freshT", [P, CHUNK, P])
    stats = sb("mo_stats", [P, CHUNK, 6])
    fresh_mv = sb("mo_fresh_mv", [P, CHUNK, 2])
    vareps = sb("mo_vareps", [P, TILES])
    minus_half = sb("mo_minus_half", [P, TILES])
    rstd = sb("mo_rstd", [P, TILES])
    comb = sb("mo_comb", [P, TILES, EXPERTS])
    lmax = sb("mo_lmax", [P, TILES])
    loff = sb("mo_loff", [P, TILES, EXPERTS])
    lexp = sb("mo_lexp", [P, TILES, EXPERTS])
    lsum = sb("mo_lsum", [P, TILES])
    linv = sb("mo_linv", [P, TILES])
    pr = sb("mo_pr", [P, TILES, EXPERTS])
    ge = sb("mo_ge", [P, 6, TILES])
    ra = sb("mo_ra", [P, EXPERTS, TILES])
    rc = sb("mo_rc", [P, EXPERTS, TILES])
    kept = sb("mo_kept", [P, TILES, EXPERTS])
    ksum = sb("mo_ksum", [P, TILES])
    kinv = sb("mo_kinv", [P, TILES])

    U = st.bank[0:4]
    Y = st.bank[4:6]
    TR = st.bank[6]
    RT = st.bank[7]

    small_in = sem("mo_small_in")
    w_in = sem("mo_w_in")
    b2_cleared = sem("mo_b2_cleared")
    b2_loaded = sem("mo_b2_loaded")
    half_ready = sem("mo_half_ready")
    b2_step = sem("mo_b2_step")
    rows_ps = sem("mo_rows_ps")
    rows_turned = sem("mo_rows_turned")
    w1_ready = sem("mo_w1_ready")
    bias_ps = sem("mo_bias_ps")
    bias_ready = sem("mo_bias_ready")
    step = sem("mo_router_step")
    var_ready = sem("mo_var_ready")
    rstd_ready = sem("mo_rstd_ready")
    loff_ready = sem("mo_loff_ready")
    lexp_ready = sem("mo_lexp_ready")
    xh_ready = sem("mo_xh_ready")
    xh_ps = sem("mo_xh_ps")
    xhT_ready = sem("mo_xhT_ready")
    up_ps = sem("mo_up_ps")
    h_ready = sem("mo_h_ready")
    y_ps = sem("mo_y_ps")
    y_taken = sem("mo_y_taken")
    fresh_kept = sem("mo_fresh_kept")
    fresh_ps = sem("mo_fresh_ps")
    freshT_ready = sem("mo_freshT_ready")
    stats_ready = sem("mo_stats_ready")
    aggr_ready = sem("mo_aggr_ready")
    mv_ready = sem("mo_mv_ready")
    logits_ps = sem("mo_logits_ps")
    logits_ready = sem("mo_logits_ready")
    NSMALL = 6

    def fresh_at(n):
        return EXPERTS * (n + 1) + 2


    with nc.Block() as block:

        @block.sync
        def _(sp):
            sp.dma_start(state[:], st.d_xn.rearrange("t p c -> p t c")).then_inc(small_in, 16)
            sp.dma_start(b1_rows[:], a["b1"].rearrange("l e (f p) -> (l e f) p", p=P)).then_inc(small_in, 16)
            sp.dma_start(gb_rows[0:LE, :], a["ln_g"].rearrange("l e c -> (l e) c")).then_inc(small_in, 16)
            sp.dma_start(gb_rows[LE:2 * LE, :], a["ln_b"].rearrange("l e c -> (l e) c")).then_inc(small_in, 16)
            sp.dma_start(rw[:], a["router_w"].rearrange("l h e -> h l e")).then_inc(small_in, 16)
            sp.dma_start(rb[:], a["router_b"].rearrange("(o l) e -> o (l e)", o=1).to_broadcast([P, LE]))\
                .then_inc(small_in, 16)

            def load_w(l):
                sp.dma_start(w1_raw[:], a["w1"][ds(l, 1)].rearrange("o e h f -> h (o e) f")).then_inc(w_in, 16)
                for e in range(EXPERTS):
                    sp.dma_start(w2[:, ds(l % 2, 1), e].rearrange("p o f c -> p (o f) c"),
                                 a["w2"][ds(l, 1), e].rearrange("o (f p) c -> p (o f) c", p=P))\
                        .then_inc(w_in, 16)

            load_w(0)
            sp.wait_ge(b2_cleared, 1)
            for k in range(3):
                sp.dma_start(b2_in[32 * k:32 * k + 1, :],
                             a["b2"].rearrange("(o l) e c -> o (l e c)", o=1)).then_inc(b2_loaded, 16)
            with sp.Fori(0, LAYERS - 1) as l:
                sp.wait_ge(w1_ready, l + 1)
                sp.wait_ge(bias_ready, l + 1)
                load_w(l + 1)

        @block.gpsimd
        def _(pool):
            nc.gpsimd.memset(minus_half[:], -0.5).then_inc(half_ready, 1)
            pool.wait_ge(half_ready, 1)
            with pool.Fori(0, LAYERS) as l:
                pool.wait_ge(var_ready, l + 1)
                nc.gpsimd.tensor_tensor(rstd[:], vareps[:], minus_half[:], ALU.pow).then_inc(rstd_ready, 1)

        @block.scalar
        def _(act):
            act.sem_inc(fresh_kept, 1)
            act.wait_ge(rows_ps, 1)
            nc.scalar.activation(b1T[:], TR[:, 0:LE * FT], ACT.Copy).then_inc(rows_turned, 1)
            nc.scalar.activation(gbT[:], TR[:, LE * FT:LE * FT + 2 * LE], ACT.Copy).then_inc(rows_turned, 1)

            def turned(n):
                act.wait_ge(xh_ps, n + 1)
                nc.scalar.activation(xhT[:], TR, ACT.Copy).then_inc(xhT_ready, 1)

            def keep(n, c):
                act.wait_ge(y_taken, fresh_at(n))
                nc.scalar.activation(state[:, ds(c * CHUNK, CHUNK), :], fresh[:], ACT.Copy).then_inc(fresh_kept, 1)

            def gelus(n, c, first):
                for e in range(EXPERTS):
                    if e == 1 and not first:
                        keep(n - 1, c - 1)
                    for f in range(FT):
                        act.wait_ge(up_ps, PER * n + e * FT + f + 1)
                        nc.scalar.activation(h[:, e % 2, f, :], U[f], ACT.Gelu,
                                             bias=bias[:, e * FT + f:e * FT + f + 1]).then_inc(h_ready, 1)

            with act.Fori(0, LAYERS) as l:
                act.wait_ge(loff_ready, l + 1)
                nc.scalar.activation(lexp[:], loff[:], ACT.Exp).then_inc(lexp_ready, 1)
                act.wait_ge(bias_ready, l + 1)
                turned(l * NCH)
                gelus(l * NCH, 0, True)
                turned(l * NCH + 1)
                with act.Fori(1, NCH - 1) as c:
                    gelus(l * NCH + c, c, False)
                    turned(l * NCH + c + 1)
                gelus(l * NCH + NCH - 1, NCH - 1, False)
                keep(l * NCH + NCH - 1, NCH - 1)

        @block.vector
        def _(dve):
            nc.vector.memset(b2_in[:], 0.0).then_inc(b2_cleared, 1)
            nc.vector.memset(ones[:], 1.0)
            dve.sem_inc(y_taken, 2)
            dve.wait_ge(b2_loaded, 16 * 3)
            dve.wait_ge(small_in, 16 * NSMALL)
            nc.vector.tensor_copy(b2_part[:], b2_in[:]).then_inc(b2_step, 1)
            dve.wait_ge(b2_step, 1)
            nc.vector.tensor_tensor(b2_rest[:], b2_in[:], b2_part[:], ALU.subtract).then_inc(b2_step, 1)
            dve.wait_ge(b2_step, 2)
            for row in (32, 64):
                nc.vector.tensor_copy(b2_part[row:row + 32, :], b2_rest[row:row + 32, :]).then_inc(b2_step, 1)
            dve.wait_ge(b2_step, 4)
            nc.vector.tensor_tensor(b2_rest[64:96, :], b2_rest[64:96, :], b2_part[64:96, :],
                                    ALU.subtract).then_inc(b2_step, 1)
            dve.wait_ge(b2_step, 5)
            nc.vector.tensor_copy(b2_part[64:96, :], b2_rest[64:96, :]).then_inc(b2_step, 1)

            def norm(n, c):
                for t in range(CHUNK):
                    tile = c * CHUNK + t
                    last = nc.vector.tensor_scalar(xh[:, t, :], state[:, ds(tile, 1), :].rearrange("p o c -> p (o c)"),
                                                   mv[:, ds(tile, 1), 0], rstd[:, ds(tile, 1)], ALU.subtract,
                                                   ALU.mult)
                last.then_inc(xh_ready, 1)

            def turned(n, c):
                dve.wait_ge(stats_ready, n + 1)
                dve.wait_ge(fresh_ps, n + 1)
                nc.vector.tensor_copy(freshT[:].rearrange("p t n -> p (t n)"), TR).then_inc(freshT_ready, 1)
                for t in range(CHUNK):
                    last = nc.vector.bn_aggr(fresh_mv[:, t, :], stats[:, t, :])
                last.then_inc(aggr_ready, 1)
                dve.wait_ge(aggr_ready, n + 1)
                nc.vector.tensor_copy(mv[:, ds(c * CHUNK, CHUNK), :], fresh_mv[:]).then_inc(mv_ready, 1)

            def route(n, c, l):
                dve.wait_ge(logits_ps, n + 1)
                nc.vector.tensor_tensor(logits[:, ds(c * CHUNK, CHUNK), :],
                                        RT[:, 0:CHUNK * EXPERTS].rearrange("p (t e) -> p t e", e=EXPERTS),
                                        rb[:, ds(((l + 1) % LAYERS) * EXPERTS, EXPERTS)].unsqueeze(1)
                                        .to_broadcast([P, CHUNK, EXPERTS]), ALU.add).then_inc(logits_ready, 1)

            def add_expert(n, c, e):
                dve.wait_ge(y_ps, EXPERTS * n + e + 1)
                dve.wait_ge(y_taken, EXPERTS * n + e + 2)
                if e == EXPERTS - 1:
                    dve.wait_ge(fresh_kept, n + 1)
                for t in range(CHUNK):
                    tile = c * CHUNK + t
                    s = state[:, ds(tile, 1), :].rearrange("p o c -> p (o c)")
                    last = nc.vector.scalar_tensor_tensor(
                        fresh[:, t, :] if e == EXPERTS - 1 else s, Y[e % 2][:, t * C:(t + 1) * C],
                        comb[:, ds(tile, 1), e], s, ALU.mult, ALU.add)
                last.then_inc(y_taken, 1)

            def moments(n):
                dve.wait_ge(y_taken, fresh_at(n))
                for t in range(CHUNK):
                    last = nc.vector.bn_stats(stats[:, t, :], fresh[:, t, :])
                last.then_inc(stats_ready, 1)

            def chunk(l, c, first, final):
                n = l * NCH + c
                if not final:
                    dve.wait_ge(xh_ps, n + 1)
                    norm(n + 1, c + 1)
                if not first:
                    turned(n - 1, c - 1)
                add_expert(n, c, 0)
                if not first:
                    route(n - 1, c - 1, l)
                for e in range(1, EXPERTS):
                    add_expert(n, c, e)
                moments(n)

            RSTEPS = 20
            with dve.Fori(0, LAYERS) as l:
                k = 0

                def after(ins):
                    nonlocal k
                    k += 1
                    ins.then_inc(step, 1)
                    dve.wait_ge(step, RSTEPS * l + k)

                dve.wait_ge(fresh_kept, NCH * l + 1)
                dve.wait_ge(rows_turned, 2)
                nc.vector.tensor_scalar(vareps[:], mv[:, :, 1], MOE_EPS, None, ALU.add).then_inc(var_ready, 1)
                after(nc.vector.reduce_max(lmax[:], logits[:], axis=AX.X))
                nc.vector.tensor_tensor(loff[:], logits[:], bcast(lmax[:], EXPERTS),
                                        ALU.subtract).then_inc(loff_ready, 1)
                dve.wait_ge(w_in, 16 * (1 + EXPERTS) * (l + 1))
                for e in range(EXPERTS):
                    last = nc.vector.tensor_scalar(w1[:, e, :], w1_raw[:, e, :], gbT[:, ds(l * EXPERTS + e, 1)],
                                                   None, ALU.mult)
                last.then_inc(w1_ready, 1)
                dve.wait_ge(bias_ps, l + 1)
                nc.vector.tensor_tensor(bias[:], RT[:, 0:PER], b1T[:, ds(l * PER, PER)],
                                        ALU.add).then_inc(bias_ready, 1)
                dve.wait_ge(rstd_ready, l + 1)
                norm(l * NCH, 0)
                dve.wait_ge(lexp_ready, l + 1)
                after(nc.vector.reduce_sum(lsum[:], lexp[:], axis=AX.X))
                after(nc.vector.reciprocal(linv[:], lsum[:]))
                after(nc.vector.tensor_tensor(pr[:], lexp[:], bcast(linv[:], EXPERTS), ALU.mult))
                pair = {}
                for j in range(EXPERTS):
                    for e in range(j + 1, EXPERTS):
                        pair[j, e] = len(pair)
                        last = nc.vector.tensor_tensor(ge[:, pair[j, e], :], pr[:, :, j], pr[:, :, e], ALU.is_ge)
                after(last)

                def g(j, e):
                    return ge[:, pair[j, e], :]
                plan = [(g(0, 1), ALU.add, g(0, 2), ALU.add, g(0, 3), ALU.is_ge, 1.5),
                        (g(0, 1), ALU.subtract, g(1, 2), ALU.subtract, g(1, 3), ALU.is_le, -0.5),
                        (g(0, 2), ALU.add, g(1, 2), ALU.subtract, g(2, 3), ALU.is_le, 0.5),
                        (g(0, 3), ALU.add, g(1, 3), ALU.add, g(2, 3), ALU.is_le, 1.5)]
                for e, (x0, op0, x1, op1, x2, cmp, at) in enumerate(plan):
                    after(nc.vector.tensor_tensor(ra[:, e, :], x0, x1, op0))
                    after(nc.vector.tensor_tensor(rc[:, e, :], ra[:, e, :], x2, op1))
                    after(nc.vector.scalar_tensor_tensor(kept[:, :, e], rc[:, e, :], at, pr[:, :, e], cmp, ALU.mult))
                after(nc.vector.reduce_sum(ksum[:], kept[:], axis=AX.X))
                after(nc.vector.reciprocal(kinv[:], ksum[:]))
                after(nc.vector.tensor_tensor(comb[:], kept[:], bcast(kinv[:], EXPERTS), ALU.mult))
                assert k == RSTEPS, k
                chunk(l, 0, True, False)
                with dve.Fori(1, NCH - 1) as c:
                    chunk(l, c, False, False)
                chunk(l, NCH - 1, False, True)
                turned(l * NCH + NCH - 1, NCH - 1)
                route(l * NCH + NCH - 1, NCH - 1, l)
                dve.wait_ge(logits_ready, NCH * (l + 1))
                dve.wait_ge(mv_ready, NCH * (l + 1))

        @block.tensor
        def _(pe):
            pe.wait_ge(small_in, 16 * NSMALL)
            nc.tensor.transpose(TR[:, 0:LE * FT], b1_rows[:], st.eye[0:LE * FT, 0:LE * FT])
            nc.tensor.transpose(TR[:, LE * FT:LE * FT + 2 * LE], gb_rows[:],
                                st.eye[0:2 * LE, 0:2 * LE]).then_inc(rows_ps, 1)
            pe.wait_ge(rows_turned, 2)
            pe.wait_ge(b2_step, 6)

            def turn(n):
                pe.wait_ge(xh_ready, n + 1)
                for t in range(CHUNK):
                    last = nc.tensor.transpose(TR[:, t * P:(t + 1) * P], xh[:, t, :], st.eye[:])
                last.then_inc(xh_ps, 1)

            def up(n, e):
                for f in range(FT):
                    if e > 0:
                        pe.wait_ge(h_ready, PER * n + (e - 1) * FT + f + 1)
                    nc.tensor.matmul(U[f], w1[:, e, f * P:(f + 1) * P], xhT[:], start=True,
                                     stop=True).then_inc(up_ps, 1)

            def down(n, l, e):
                pe.wait_ge(y_taken, EXPERTS * n + e + 1)
                y = Y[e % 2]
                b2 = b2_part[:, ds((l * EXPERTS + e) * C, C)].unsqueeze(1).to_broadcast([3 * 32, CHUNK, C])
                nc.tensor.matmul(y.rearrange("p (t c) -> p t c", c=C), ones[:], b2, start=True, stop=False,
                                 skip_group_check=True)
                for f in range(FT):
                    pe.wait_ge(h_ready, PER * n + e * FT + f + 1)
                    for t in range(CHUNK):
                        last = nc.tensor.matmul(y[:, t * C:(t + 1) * C], h[:, e % 2, f, t * P:(t + 1) * P],
                                                w2[:, ds(l % 2, 1), e, f, :].rearrange("p o c -> p (o c)"), start=False, stop=(f == FT - 1),
                                                skip_group_check=True)
                last.then_inc(y_ps, 1)

            def turn_fresh(n):
                pe.wait_ge(y_taken, fresh_at(n))
                for t in range(CHUNK):
                    last = nc.tensor.transpose(TR[:, t * P:(t + 1) * P], fresh[:, t, :], st.eye[:])
                last.then_inc(fresh_ps, 1)

            def route(n, l):
                pe.wait_ge(freshT_ready, n + 1)
                for t in range(CHUNK):
                    last = nc.tensor.matmul(RT[:, t * EXPERTS:(t + 1) * EXPERTS], freshT[:, t, :],
                                            rw[:, ds((l + 1) % LAYERS, 1), :].rearrange("p o e -> p (o e)"),
                                            start=True, stop=True)
                last.then_inc(logits_ps, 1)

            def chunk(l, c, first, final):
                n = l * NCH + c
                pe.wait_ge(xhT_ready, n + 1)
                up(n, 0)
                if not first:
                    turn_fresh(n - 1)
                up(n, 1)
                down(n, l, 0)
                if not first:
                    route(n - 1, l)
                up(n, 2)
                down(n, l, 1)
                up(n, 3)
                if not final:
                    turn(n + 1)
                down(n, l, 2)
                down(n, l, 3)

            with pe.Fori(0, LAYERS) as l:
                pe.wait_ge(w_in, 16 * (1 + EXPERTS) * (l + 1))
                pe.wait_ge(loff_ready, l + 1)
                for e in range(EXPERTS):
                    for f in range(FT):
                        last = nc.tensor.matmul(RT[:, e * FT + f:e * FT + f + 1], w1_raw[:, e, f * P:(f + 1) * P],
                                                gbT[:, ds(LE + l * EXPERTS + e, 1)], start=True, stop=True)
                last.then_inc(bias_ps, 1)
                turn(l * NCH)
                pe.wait_ge(w1_ready, l + 1)
                chunk(l, 0, True, False)
                with pe.Fori(1, NCH - 1) as c:
                    chunk(l, c, False, False)
                chunk(l, NCH - 1, False, True)
                turn_fresh(l * NCH + NCH - 1)
                route(l * NCH + NCH - 1, l)

    tmp.close()


def finish(nc, a, st, out, ctx):
    def sem(name):
        return ctx.enter_context(nc.semaphore(name))

    tmp = ExitStack()

    def sb(name, shape, dt=F32):
        return tmp.enter_context(nc.sbuf_tensor(name, shape, dt))

    D = HEADS * VD
    KT = D // P
    N = TILES // CHUNK
    w_p = sb("fi_w_p", [P, KT, C])
    o = sb("fi_o", [P, 2, CHUNK, D])
    oT = sb("fi_oT", [P, 2, KT, P])
    x = sb("fi_x", [P, 2, CHUNK, C])
    part = sb("fi_part", [P, 2, CHUNK, C])
    res = sb("fi_res", [P, 2, CHUNK, C])

    w_in = sem("fi_w_in")
    o_in = [sem(f"fi_o_in{s}") for s in range(2)]
    turned_ps = sem("fi_turned_ps")
    turned = sem("fi_turned")
    y_ps = sem("fi_y_ps")
    added = sem("fi_added")
    res_ready = sem("fi_res_ready")
    stored = [sem(f"fi_stored{s}") for s in range(2)]
    x_dram = a["x"].rearrange("b (h p) c -> p (b h) c", p=P)
    out_dram = out.rearrange("b (h p) c -> p (b h) c", p=P)
    o_dram = st.d_o.rearrange("t p n -> p t n")

    with nc.Block() as block:

        @block.sync
        def _(sp):
            def load(g, s):
                sp.dma_start(o[:, s], o_dram[:, ds(g * CHUNK, CHUNK), :]).then_inc(o_in[s], 16)
                sp.dma_start(x[:, s], x_dram[:, ds(g * CHUNK, CHUNK), :]).then_inc(o_in[s], 16)

            sp.dma_start(w_p[:], a["w_proj"].rearrange("(k p) c -> p k c", p=P)).then_inc(w_in, 16)
            for s in range(2):
                sp.sem_inc(stored[s], 16)
            load(0, 0)
            load(1, 1)
            with sp.Fori(0, N // 2 - 1) as i:
                for s in range(2):
                    g = 2 * i + s
                    sp.wait_ge(res_ready, g + 1)
                    load(g + 2, s)
                    sp.dma_start(out_dram[:, ds(g * CHUNK, CHUNK), :], res[:, s]).then_inc(stored[s], 16)
            for s in range(2):
                g = N - 2 + s
                sp.wait_ge(res_ready, g + 1)
                sp.dma_start(out_dram[:, ds(g * CHUNK, CHUNK), :], res[:, s]).then_inc(stored[s], 16)
            for s in range(2):
                sp.wait_ge(stored[s], 16 * (N // 2 + 1))

        @block.scalar
        def _(act):
            with act.Fori(0, N // 2) as i:
                for s in range(2):
                    for t in range(CHUNK):
                        m = (2 * i + s) * CHUNK + t
                        act.wait_ge(turned_ps, m + 1)
                        nc.scalar.activation(oT[:, t % 2].rearrange("p k n -> p (k n)"), st.bank[t % 2],
                                             ACT.Copy).then_inc(turned, 1)

        @block.vector
        def _(dve):
            with dve.Fori(0, N // 2) as i:
                for s in range(2):
                    g = 2 * i + s
                    dve.wait_ge(y_ps, g + 1)
                    nc.vector.tensor_tensor(part[:, s], st.bank[2 + s].rearrange("p (t c) -> p t c", c=C),
                                            st.state[:, ds(g * CHUNK, CHUNK), :], ALU.add).then_inc(added, 1)
                    dve.wait_ge(added, g + 1)
                    dve.wait_ge(stored[s], 16 * (i + 1))
                    nc.vector.tensor_tensor(res[:, s], part[:, s], x[:, s], ALU.add).then_inc(res_ready, 1)

        @block.tensor
        def _(pe):
            pe.wait_ge(w_in, 16)

            def turn(m, s, t):
                for k in range(KT):
                    last = nc.tensor.transpose(st.bank[t % 2][:, k * P:(k + 1) * P], o[:, s, t, k * P:(k + 1) * P],
                                               st.eye[:])
                last.then_inc(turned_ps, 1)

            with pe.Fori(0, N // 2) as i:
                for s in range(2):
                    g = 2 * i + s
                    pe.wait_ge(o_in[s], 32 * (i + 1))
                    turn(g * CHUNK, s, 0)
                    for t in range(CHUNK):
                        if t + 1 < CHUNK:
                            if t > 0:
                                pe.wait_ge(turned, g * CHUNK + t)
                            turn(g * CHUNK + t + 1, s, t + 1)
                        pe.wait_ge(turned, g * CHUNK + t + 1)
                        for k in range(KT):
                            last = nc.tensor.matmul(st.bank[2 + s][:, t * C:(t + 1) * C], oT[:, t % 2, k, :],
                                                    w_p[:, k, :], start=(k == 0), stop=(k == KT - 1))
                    last.then_inc(y_ps, 1)

    tmp.close()


def program(nc, a, out):
    st = Store()
    with ExitStack() as ctx:
        def sb(stack, name, shape, dt=F32):
            return stack.enter_context(nc.sbuf_tensor(name, shape, dt))

        def dram(name, shape):
            return nc.dram_tensor(f"d_{name}", shape, F32, kind="Internal").ap()

        st.psum = ctx.enter_context(nc.psum_tensor("psum", [P, 8, 512], F32))
        st.bank = [st.psum[:, k, :] for k in range(8)]
        st.eye = sb(ctx, "eye", [P, P])
        st.d_xn = dram("xn", [TILES, P, C])
        st.d_xnT = dram("xnT", [B, P, T])
        st.d_kvT = dram("kvT", [B, P, T])
        st.d_nqT = dram("nqT", [B, QL, T])
        st.d_ks = dram("ks", [NQ, HD, QUAD * KEEP])
        st.d_vs = dram("vs", [NQ, P, QUAD * (VD + 1)])
        st.d_o = dram("o", [TILES, P, HEADS * VD])

        st.logits = sb(ctx, "logits", [P, TILES, EXPERTS])
        st.mv = sb(ctx, "mv", [P, TILES, 2])

        with ExitStack() as att:
            st.eye16 = sb(att, "eye16", [P, P], BF16)
            st.causal = sb(att, "causal", [P, P], BF16)
            st.cos = sb(att, "cos", [P, HALVES, ROPE])
            st.sin = sb(att, "sin", [P, HALVES, ROPE])
            st.w_q = sb(att, "w_q", [QL, HEADS, QW])
            st.w_kw = sb(att, "w_kw", [P, HEADS, HD])
            st.w_vw = sb(att, "w_vw", [P, HEADS * VD])
            st.w_v1 = sb(att, "w_v1", [P, HEADS * VD])
            st.gates = sb(att, "gates", [P, B, 3])
            with ExitStack() as pre:
                st.rb0 = sb(pre, "rb0", [P, EXPERTS])
                st.w_all = sb(pre, "w_all", [P, CALL])
                st.w_ks = sb(pre, "w_ks", [P, HEADS, HD])
                st.w_vs = sb(pre, "w_vs", [P, HEADS * VD])
                st.cos_sel = sb(pre, "cos_sel", [P, ROPE])
                st.sin_sel = sb(pre, "sin_sel", [P, ROPE])
                st.iota = sb(pre, "iota", [P, KEEP])
                st.imp = sb(pre, "imp", [P, HALVES, B])
                st.gl = sb(pre, "gl", [P, HALVES, B, 3])
                st.place = sb(pre, "place", [P, B, HALVES])
                setup(nc, a, st, ctx)
                tokens(nc, a, st, ctx)
                choose(nc, a, st, ctx)
                selected(nc, a, st, ctx)
            attention(nc, a, st, ctx)
        with ExitStack() as late:
            st.state = sb(late, "state", [P, TILES, C])
            experts(nc, a, st, ctx)
            finish(nc, a, st, out, ctx)


_INS = ["x", "w_cq", "g_qnorm", "w_dq_nope", "w_dq_rope", "w_ckv", "g_kvnorm", "w_dk_nope", "w_dv", "w_krope",
        "w_imp", "w_selk", "w_selv", "w_wink", "w_winv", "w_gate", "w_proj"]
_MOE = ["router_w", "router_b", "ln_g", "ln_b", "w1", "b1", "w2", "b2"]


def kernel(**inputs):
    import concourse.bacc as bacc
    from concourse.bass_utils import run_bass_kernel_spmd

    nc = bacc.Bacc("TRN2", target_bir_lowering=False, num_devices=1)
    arrays = {n: np.ascontiguousarray(inputs[f"L0_attn_{n}"]) for n in _INS}
    arrays.update({n: np.ascontiguousarray(inputs[f"L0_ffn_{n}"]) for n in _MOE})
    arrays.update(shape_constants())
    a = {n: nc.dram_tensor(n, v.shape, mybir.dt.from_np(v.dtype), kind="ExternalInput").ap()
         for n, v in arrays.items()}
    out = nc.dram_tensor("out", (B, T, C), F32, kind="ExternalOutput").ap()
    program(nc, a, out)
    r = run_bass_kernel_spmd(nc, [arrays], core_ids=[0])
    return r.results[0]["out"]
```

```python
from contextlib import ExitStack

import numpy as np
import concourse.bass as bass
from concourse import mybir

F32 = mybir.dt.float32
BF16 = mybir.dt.bfloat16
F16 = mybir.dt.float16
F32R = mybir.dt.float32r
ALU = mybir.AluOpType
ACT = mybir.ActivationFunctionType
AX = mybir.AxisListType
ds = bass.ds

P = 128
B, T, C = 32, 256, 128
TILES = B * T // P
HALVES = T // P
HEADS, NOPE, ROPE, VD = 16, 32, 64, 32
HD = NOPE + ROPE
QL, KL = 96, 32
KEEP = 32
QUAD = 4
QUADS = HEADS // QUAD
NQ = B * QUADS
QW = HD + KL
SCALE = float(HD) ** -0.5
LN_EPS, RMS_EPS, MOE_EPS = 1e-5, 1e-6, 1e-5
CQ, CKV, CKR, CIMP, CGATE = 0, 96, 128, 192, 193
CROUT = 196
CALL = 200
GRP = 4
GT = GRP * HALVES
NGRP = B // GRP
LAYERS, EXPERTS, FF = 4, 4, 512
FT = FF // P
CHUNK = 4
NCH = TILES // CHUNK
WEIGHT_SCALE = 2.0 ** 14
GONE = -3.0e38


def shape_constants():
    f = (1.0 / np.float32(10000.0) ** (np.arange(0, ROPE, 2, dtype=np.float32) / np.float32(ROPE))).astype(np.float32)
    a = np.outer(np.arange(T, dtype=np.float32), f).astype(np.float32)
    cos, sin = np.cos(a).astype(np.float32), np.sin(a).astype(np.float32)
    return {
        "c_eye": np.eye(P, dtype=np.float32),
        "c_causal": np.triu(np.full((P, P), -1e30, np.float32), 1),
        "c_cos": np.concatenate([cos, cos], 1),
        "c_sin": np.concatenate([-sin, sin], 1),
        "c_iota": np.tile(np.arange(KEEP, dtype=np.float32), (P, 1)),
    }


def bcast(ap, n):
    return ap.unsqueeze(len(ap.shape)).to_broadcast(list(ap.shape) + [n])


class Store:
    pass


def setup(nc, a, st, ctx):
    def sem(name):
        return ctx.enter_context(nc.semaphore(name))

    tmp = ExitStack()

    def sb(name, shape, dt=F32):
        return tmp.enter_context(nc.sbuf_tensor(name, shape, dt))

    raw_rope = sb("raw_rope", [QL, HEADS * ROPE])
    raw_nope = sb("raw_nope", [QL, HEADS * NOPE])
    raw_dk = sb("raw_dk", [KL, HEADS * NOPE])
    dk_gained = sb("dk_gained", [KL, HEADS * NOPE])
    gq = sb("gq", [QL, 1])
    gq_scaled = sb("gq_scaled", [QL, 1])
    gkv = sb("gkv", [KL, 1])
    gkv_high = sb("gkv_high", [P, 1])
    nope_T = sb("nope_T", [P, QUADS, QL])
    dk_T = sb("dk_T", [P, QUADS, KL])
    causal32 = sb("causal32", [P, P])

    loaded = sem("su_loaded")
    dv_zeroed = sem("su_dv_zeroed")
    gq_ready = sem("su_gq_ready")
    dk_ready = sem("su_dk_ready")
    flipped = sem("su_flipped")
    flip_out = sem("su_flip_out")
    absorbed = sem("su_absorbed")
    wq_parts = sem("su_wq_parts")
    NLOAD = 16 + 17

    with nc.Block() as block:

        @block.sync
        def _(sp):
            def load(dst, src):
                sp.dma_start(dst, src).then_inc(loaded, 16)

            load(raw_rope[:], a["w_dq_rope"])
            load(raw_nope[:], a["w_dq_nope"])
            load(raw_dk[:], a["w_dk_nope"])
            load(gq[:], a["g_qnorm"].rearrange("(k o) -> k o", o=1))
            load(gkv[:], a["g_kvnorm"].rearrange("(k o) -> k o", o=1))
            load(gkv_high[P - KL:P, :], a["g_kvnorm"].rearrange("(k o) -> k o", o=1))
            load(st.eye[:], a["c_eye"])
            load(causal32[:], a["c_causal"])
            load(st.w_all[:, CQ:CQ + QL], a["w_cq"])
            load(st.w_all[:, CKV:CKV + KL], a["w_ckv"])
            load(st.w_all[:, CKR:CKR + ROPE], a["w_krope"])
            load(st.w_all[:, CIMP:CIMP + 1], a["w_imp"])
            load(st.w_all[:, CGATE:CGATE + 3], a["w_gate"])
            load(st.w_all[:, CROUT:CROUT + EXPERTS], a["router_w"][0])
            load(st.rb0[:], a["router_b"][0:1, :].to_broadcast([P, EXPERTS]))
            sp.wait_ge(dv_zeroed, 1)
            load(st.w_v1[P - KL:P, :], a["w_dv"])

        @block.vector
        def _(dve):
            nc.vector.memset(st.w_v1[:], 0.0).then_inc(dv_zeroed, 1)
            dve.wait_ge(loaded, 16 * NLOAD)
            nc.vector.tensor_scalar(gq_scaled[:], gq[:], SCALE, None, ALU.mult).then_inc(gq_ready, 1)
            nc.vector.tensor_scalar(dk_gained[:], raw_dk[:], gkv[:], None, ALU.mult).then_inc(dk_ready, 1)
            nc.vector.tensor_copy(st.causal[:], causal32[:])
            nc.vector.tensor_copy(st.eye16[:], st.eye[:])
            nc.vector.tensor_scalar(st.w_all[:, CKR:CKR + ROPE], st.w_all[:, CKR:CKR + ROPE], 1.0 / HEADS, None,
                                    ALU.mult)
            nc.vector.tensor_scalar(st.w_v1[P - KL:P, :], st.w_v1[P - KL:P, :], gkv_high[P - KL:P, :], None,
                                    ALU.mult)
            dve.wait_ge(gq_ready, 1)
            nc.vector.tensor_scalar(st.w_q[:, :, 0:ROPE], raw_rope[:].rearrange("p (h d) -> p h d", d=ROPE),
                                    gq_scaled[:], None, ALU.mult).then_inc(wq_parts, 1)
            nc.vector.tensor_scalar(st.w_q[:, :, ROPE:HD], raw_nope[:].rearrange("p (h d) -> p h d", d=NOPE),
                                    gq_scaled[:], None, ALU.mult).then_inc(wq_parts, 1)
            for j in range(QUAD):
                dve.wait_ge(absorbed, j + 1)
                nc.vector.tensor_scalar(st.w_q[:, j:HEADS:QUAD, HD:QW],
                                        st.bank[2 + j][0:QL, 0:QUADS * KL].rearrange("p (g d) -> p g d", d=KL),
                                        gq_scaled[:], None, ALU.mult).then_inc(wq_parts, 1)
            dve.wait_ge(wq_parts, 2 + QUAD)
            for n, (w, parts) in enumerate(((st.w_kw, st.w_kw_parts), (st.w_q, st.w_q_parts))):
                nc.vector.tensor_copy(parts[0][:], w[:]).then_inc(wq_parts, 1)
                dve.wait_ge(wq_parts, 2 + QUAD + n + 1)
                nc.vector.tensor_tensor(parts[1][:], w[:], parts[0][:], ALU.subtract)

        @block.scalar
        def _(act):
            def load(dst, src):
                act.dma_start(dst, src).then_inc(loaded, 16)

            load(st.cos[:], a["c_cos"].rearrange("(h p) d -> p h d", p=P))
            load(st.sin[:], a["c_sin"].rearrange("(h p) d -> p h d", p=P))
            for j in range(GRP):
                load(st.cos_sel[KEEP * j:KEEP * (j + 1), :], a["c_cos"][0:KEEP, :])
                load(st.sin_sel[KEEP * j:KEEP * (j + 1), :], a["c_sin"][0:KEEP, :])
            load(st.iota[:], a["c_iota"])
            for dst, src in ((st.w_kw, a["w_wink"]), (st.w_ks, a["w_selk"])):
                v = src.rearrange("c (h d) -> c h d", d=HD)
                load(dst[:, 0:HEADS, 0:ROPE], v[:, :, NOPE:HD])
                load(dst[:, 0:HEADS, ROPE:HD], v[:, :, 0:NOPE])
            load(st.w_vw[:], a["w_winv"])
            load(st.w_vs[:], a["w_selv"])
            act.wait_ge(flipped, 1)
            nc.scalar.activation(nope_T[:], st.bank[0][:, 0:QUADS * QL].rearrange("p (g d) -> p g d", d=QL),
                                 ACT.Copy).then_inc(flip_out, 1)
            act.wait_ge(flipped, 2)
            nc.scalar.activation(dk_T[:], st.bank[1][:, 0:QUADS * KL].rearrange("p (g d) -> p g d", d=KL),
                                 ACT.Copy).then_inc(flip_out, 1)

        @block.tensor
        def _(pe):
            pe.wait_ge(loaded, 16 * NLOAD)
            for g in range(QUADS):
                last = nc.tensor.transpose(st.bank[0][:, g * QL:(g + 1) * QL], raw_nope[:, g * P:(g + 1) * P],
                                           st.eye[0:QL, 0:QL])
            last.then_inc(flipped, 1)
            pe.wait_ge(dk_ready, 1)
            for g in range(QUADS):
                last = nc.tensor.transpose(st.bank[1][:, g * KL:(g + 1) * KL], dk_gained[:, g * P:(g + 1) * P],
                                           st.eye[0:KL, 0:KL])
            last.then_inc(flipped, 1)
            pe.wait_ge(flip_out, 2)
            for j in range(QUAD):
                rows = slice(NOPE * j, NOPE * (j + 1))
                for g in range(QUADS):
                    last = nc.tensor.matmul(st.bank[2 + j][0:QL, g * KL:(g + 1) * KL], nope_T[rows, g, :],
                                            dk_T[rows, g, :], start=True, stop=True)
                last.then_inc(absorbed, 1)

    tmp.close()


def tokens(nc, a, st, ctx):
    def sem(name):
        return ctx.enter_context(nc.semaphore(name))

    tmp = ExitStack()

    def sb(name, shape, dt=F32):
        return tmp.enter_context(nc.sbuf_tensor(name, shape, dt))

    x = sb("tk_x", [P, GT, C])
    xc = sb("tk_xc", [P, GT, C])
    sq = sb("tk_sq", [P, GT, C])
    xn = sb("tk_xn", [P, GT, C])
    xnT = sb("tk_xnT", [P, GT, P])
    mean = sb("tk_mean", [P, GT])
    nmean = sb("tk_nmean", [P, GT])
    vsum = sb("tk_vsum", [P, GT])
    var = sb("tk_var", [P, GT])
    rstd = sb("tk_rstd", [P, GT])
    xsq = sb("tk_xsq", [P, GT, C])
    proj = sb("tk_proj", [P, 2, GT, CALL])
    psq = sb("tk_psq", [P, GT, QL + KL])
    ssum = sb("tk_ssum", [P, 2, GT])
    smean = sb("tk_smean", [P, 2, GT])
    rrms = sb("tk_rrms", [P, 2, GT])
    rot = sb("tk_rot", [P, GT, ROPE])
    key = sb("tk_key", [P, GT, P])
    nq = sb("tk_nq", [P, GT, QL])
    keyT = sb("tk_keyT", [P, GT, P])
    nqT = sb("tk_nqT", [QL, GT, P])
    minus_half = sb("tk_minus_half", [P, 2 * GT])
    mom = sb("tk_mom", [P, 2, GT])
    msq = sb("tk_msq", [P, GT])
    vsq = sb("tk_vsq", [P, GT])

    x_in = sem("tk_x_in")
    mean_step = sem("tk_mean_step")
    centered = sem("tk_centered")
    squared = sem("tk_squared")
    vsummed = sem("tk_vsummed")
    var_ready = sem("tk_var_ready")
    half_ready = sem("tk_half_ready")
    rstd_ready = sem("tk_rstd_ready")
    xn_ready = sem("tk_xn_ready")
    xt_ps = sem("tk_xt_ps")
    xnT_ready = sem("tk_xnT_ready")
    proj_ps = sem("tk_proj_ps")
    proj_ready = sem("tk_proj_ready")
    psq_ready = sem("tk_psq_ready")
    ssummed = sem("tk_ssummed")
    smean_ready = sem("tk_smean_ready")
    rrms_ready = sem("tk_rrms_ready")
    rotated = sem("tk_rotated")
    key_zeroed = sem("tk_key_zeroed")
    lat_ready = sem("tk_lat_ready")
    lat_ps = sem("tk_lat_ps")
    latT_ready = sem("tk_latT_ready")
    xsq_ready = sem("tk_xsq_ready")
    mom_step = sem("tk_mom_step")
    xn_out = sem("tk_xn_out")
    xt_out = sem("tk_xt_out")
    lat_out = sem("tk_lat_out")

    x_dram = a["x"].rearrange("b (h p) c -> p (b h) c", p=P)
    xn_dram = st.d_xn.rearrange("t p c -> p t c")
    bk = st.bank
    hr = ROPE // 2

    def two(ap):
        return ap.rearrange("p t n -> p (t n)")

    def wait(eng, s, n):
        if not isinstance(n, int) or n > 0:
            eng.wait_ge(s, n)

    def groups(eng, body):
        body(0, 0, False)
        body(1, 1, False)
        with eng.Fori(1, NGRP // 2 - 1) as j:
            body(2 * j, 0, False)
            body(2 * j + 1, 1, False)
        body(NGRP - 2, 0, False)
        body(NGRP - 1, 1, True)

    with nc.Block() as block:

        @block.sync
        def _(sp):
            def load(i):
                sp.dma_start(x[:], x_dram[:, ds(i * GT, GT), :]).then_inc(x_in, 16)

            def store_xn(i):
                sp.wait_ge(xn_ready, i + 1)
                sp.dma_start(xn_dram[:, ds(i * GT, GT), :], xn[:]).then_inc(xn_out, 16)
                sp.wait_ge(xnT_ready, 2 * i + 2)
                sp.dma_start(st.d_xnT[ds(i * GRP, GRP)].rearrange("b c n -> c b n"),
                             xnT[:].rearrange("p (b h) n -> p b (h n)", h=HALVES)).then_inc(xt_out, 16)

            def store_latents(i):
                sp.wait_ge(latT_ready, 4 * i + 4)
                sp.dma_start(st.d_kvT[ds(i * GRP, GRP)].rearrange("b c n -> c b n"),
                             keyT[:].rearrange("p (b h) n -> p b (h n)", h=HALVES)).then_inc(lat_out, 16)
                sp.dma_start(st.d_nqT[ds(i * GRP, GRP)].rearrange("b c n -> c b n"),
                             nqT[:].rearrange("p (b h) n -> p b (h n)", h=HALVES)).then_inc(lat_out, 16)

            def body(i, s, last):
                if not last:
                    if not (isinstance(i, int) and i == NGRP - 2):
                        sp.wait_ge(centered, i + 2)
                        load(i + 2)
                    store_xn(i + 1)
                store_latents(i)

            load(0)
            sp.wait_ge(centered, 1)
            load(1)
            store_xn(0)
            groups(sp, body)
            sp.wait_ge(xn_out, 16 * NGRP)
            sp.wait_ge(xt_out, 16 * NGRP)
            sp.wait_ge(lat_out, 32 * NGRP)

        @block.gpsimd
        def _(pool):
            def deviation(i):
                pool.wait_ge(var_ready, i + 1)
                nc.gpsimd.tensor_tensor(rstd[:], var[:], minus_half[:, 0:GT], ALU.pow).then_inc(rstd_ready, 1)

            def body(i, s, last):
                pool.wait_ge(smean_ready, 2 * i + 2)
                nc.gpsimd.tensor_tensor(rrms[:].rearrange("p k t -> p (k t)"), smean[:].rearrange("p k t -> p (k t)"),
                                        minus_half[:], ALU.pow).then_inc(rrms_ready, 1)
                if not last:
                    deviation(i + 1)

            nc.gpsimd.memset(minus_half[:], -0.5).then_inc(half_ready, 1)
            pool.wait_ge(half_ready, 1)
            deviation(0)
            groups(pool, body)

        @block.scalar
        def _(act):
            def square(i):
                act.wait_ge(centered, i + 1)
                wait(act, vsummed, i)
                nc.scalar.activation(sq[:], xc[:], ACT.Square).then_inc(squared, 1)

            def turned(i):
                for k in range(2):
                    act.wait_ge(xt_ps, 2 * i + k + 1)
                    if k == 0:
                        wait(act, xt_out, 16 * i)
                    nc.scalar.activation(two(xnT[:, 4 * k:4 * k + 4, :]), bk[k][:, :], ACT.Copy).then_inc(xnT_ready, 1)

            def projected(i, s, end):
                for k in range(4):
                    act.wait_ge(proj_ps, 4 * i + k + 1)
                    wait(act, lat_ready, 3 * (i - 1))
                    nc.scalar.activation(two(proj[:, s, 2 * k:2 * k + 2, :]), bk[2 + k][:, 0:2 * CALL],
                                         ACT.Copy).then_inc(proj_ready, 1)
                act.wait_ge(proj_ready, 4 * i + 4)
                wait(act, smean_ready, 2 * i)
                nc.scalar.activation(psq[:], proj[:, s, :, 0:QL + KL], ACT.Square).then_inc(psq_ready, 1)
                if not end:
                    square(i + 1)
                wait(act, mom_step, 5 * i)
                nc.scalar.activation(xsq[:], xn[:], ACT.Square).then_inc(xsq_ready, 1)

            def latents(i):
                for k in range(4):
                    act.wait_ge(lat_ps, 4 * i + k + 1)
                    if k == 0:
                        wait(act, lat_out, 32 * i)
                    out = keyT[:, 4 * k:4 * k + 4, :] if k < 2 else nqT[:, 4 * k - 8:4 * k - 4, :]
                    nc.scalar.activation(two(out), bk[6 + k % 2][0:P if k < 2 else QL, :],
                                         ACT.Copy).then_inc(latT_ready, 1)

            def body(i, s, last):
                if not last:
                    turned(i + 1)
                    projected(i + 1, 1 - s, isinstance(i, int) and i == NGRP - 2)
                latents(i)

            square(0)
            turned(0)
            projected(0, 0, False)
            groups(act, body)

        @block.vector
        def _(dve):
            def center(i):
                dve.wait_ge(x_in, 16 * i + 16)
                nc.vector.reduce_sum(mean[:], x[:], axis=AX.X).then_inc(mean_step, 1)
                dve.wait_ge(mean_step, 2 * i + 1)
                nc.vector.tensor_scalar(nmean[:], mean[:], 1.0 / C, None, ALU.mult).then_inc(mean_step, 1)
                dve.wait_ge(mean_step, 2 * i + 2)
                wait(dve, xn_ready, i)
                nc.vector.tensor_tensor(xc[:], x[:], bcast(nmean[:], C), ALU.subtract).then_inc(centered, 1)

            def variance(i):
                dve.wait_ge(squared, i + 1)
                nc.vector.reduce_sum(vsum[:], sq[:], axis=AX.X).then_inc(vsummed, 1)
                dve.wait_ge(vsummed, i + 1)
                nc.vector.tensor_scalar(var[:], vsum[:], 1.0 / C, LN_EPS, ALU.mult, ALU.add).then_inc(var_ready, 1)

            def norm(i):
                dve.wait_ge(rstd_ready, i + 1)
                wait(dve, xn_out, 16 * i)
                nc.vector.tensor_tensor(xn[:], xc[:], bcast(rstd[:], C), ALU.mult).then_inc(xn_ready, 1)

            def keep(i, s):
                pj = proj[:, s]
                dve.wait_ge(proj_ready, 4 * i + 4)
                nc.vector.tensor_copy(st.imp[:, :, ds(i * GRP, GRP)], pj[:, :, CIMP].rearrange("p (b h) -> p h b", h=HALVES))
                for h in range(HALVES):
                    nc.vector.tensor_copy(st.gl[:, h, ds(i * GRP, GRP), :], pj[:, h:GT:HALVES, CGATE:CGATE + 3])
                nc.vector.tensor_tensor(st.logits[:, ds(i * GT, GT), :], pj[:, :, CROUT:CROUT + EXPERTS],
                                        st.rb0[:].unsqueeze(1).to_broadcast([P, GT, EXPERTS]), ALU.add)
                dve.wait_ge(psq_ready, i + 1)
                nc.vector.reduce_sum(ssum[:, 0, :], psq[:, :, 0:QL], axis=AX.X).then_inc(ssummed, 1)
                nc.vector.reduce_sum(ssum[:, 1, :], psq[:, :, QL:QL + KL], axis=AX.X).then_inc(ssummed, 1)
                for k, width in enumerate((QL, KL)):
                    dve.wait_ge(ssummed, 2 * i + k + 1)
                    wait(dve, rrms_ready, i)
                    nc.vector.tensor_scalar(smean[:, k, :], ssum[:, k, :], 1.0 / width, RMS_EPS, ALU.mult,
                                            ALU.add).then_inc(smean_ready, 1)

            def rope(i, s):
                wait(dve, lat_ps, 4 * i)
                halves = proj[:, s, :, CKR:CKR + ROPE].rearrange("p (b h) d -> p b h d", h=HALVES)
                rk = rot[:].rearrange("p (b h) d -> p b h d", h=HALVES)
                for h in range(HALVES):
                    def tab(t, lo, hi):
                        return t[:, h:h + 1, lo:hi].to_broadcast([P, GRP, hi - lo])
                    nc.vector.tensor_tensor(rk[:, :, h, 0:hr], halves[:, :, h, hr:ROPE], tab(st.sin, 0, hr),
                                            ALU.mult).then_inc(rotated, 1)
                    nc.vector.tensor_tensor(rk[:, :, h, hr:ROPE], halves[:, :, h, 0:hr], tab(st.sin, hr, ROPE),
                                            ALU.mult).then_inc(rotated, 1)
                    nc.vector.tensor_tensor(key[:, h:GT:HALVES, 0:ROPE], halves[:, :, h, :], tab(st.cos, 0, ROPE),
                                            ALU.mult).then_inc(rotated, 1)
                dve.wait_ge(rotated, 6 * i + 6)
                nc.vector.tensor_tensor(key[:, :, 0:ROPE], key[:, :, 0:ROPE], rot[:], ALU.add).then_inc(lat_ready, 1)

            def moments(i):
                nc.vector.reduce_sum(mom[:, 0, :], xn[:], axis=AX.X).then_inc(mom_step, 1)
                dve.wait_ge(xsq_ready, i + 1)
                nc.vector.reduce_sum(mom[:, 1, :], xsq[:], axis=AX.X).then_inc(mom_step, 1)
                dve.wait_ge(mom_step, 5 * i + 2)
                nc.vector.tensor_scalar(st.mv[:, ds(i * GT, GT), 0], mom[:, 0, :], 1.0 / C, None,
                                        ALU.mult).then_inc(mom_step, 1)
                nc.vector.tensor_tensor(msq[:], mom[:, 0, :], mom[:, 0, :], ALU.mult).then_inc(mom_step, 1)
                dve.wait_ge(mom_step, 5 * i + 4)
                nc.vector.scalar_tensor_tensor(vsq[:], msq[:], -1.0 / C, mom[:, 1, :], ALU.mult,
                                               ALU.add).then_inc(mom_step, 1)
                dve.wait_ge(mom_step, 5 * i + 5)
                nc.vector.tensor_scalar(st.mv[:, ds(i * GT, GT), 1], vsq[:], 1.0 / C, None, ALU.mult)

            def scale(i, s):
                dve.wait_ge(rrms_ready, i + 1)
                nc.vector.tensor_tensor(key[:, :, P - KL:P], proj[:, s, :, CKV:CKV + KL], bcast(rrms[:, 1, :], KL),
                                        ALU.mult).then_inc(lat_ready, 1)
                nc.vector.tensor_tensor(nq[:], proj[:, s, :, CQ:CQ + QL], bcast(rrms[:, 0, :], QL),
                                        ALU.mult).then_inc(lat_ready, 1)

            def body(i, s, last):
                if not last:
                    center(i + 1)
                keep(i, s)
                if not last:
                    variance(i + 1)
                moments(i)
                rope(i, s)
                if not last:
                    norm(i + 1)
                scale(i, s)

            nc.vector.memset(key[:], 0.0).then_inc(key_zeroed, 1)
            dve.wait_ge(key_zeroed, 1)
            center(0)
            variance(0)
            norm(0)
            groups(dve, body)

        @block.tensor
        def _(pe):
            def turn(i):
                pe.wait_ge(xn_ready, i + 1)
                for t in range(GT):
                    last = nc.tensor.transpose(bk[t // 4][:, (t % 4) * P:(t % 4 + 1) * P], xn[:, t, :], st.eye[:])
                    if t % 4 == 3:
                        last.then_inc(xt_ps, 1)

            def project(i):
                for t in range(GT):
                    if t % 4 == 0:
                        pe.wait_ge(xnT_ready, 2 * i + t // 4 + 1)
                    last = nc.tensor.matmul(bk[2 + t // 2][:, (t % 2) * CALL:(t % 2 + 1) * CALL], xnT[:, t, :],
                                            st.w_all[:], start=True, stop=True)
                    if t % 2 == 1:
                        last.then_inc(proj_ps, 1)

            def latents(i):
                pe.wait_ge(lat_ready, 3 * i + 3)
                for k in range(4):
                    wait(pe, latT_ready, 4 * i + k - 1)
                    for j in range(4):
                        t = 4 * (k % 2) + j
                        out = bk[6 + k % 2][:, j * P:(j + 1) * P]
                        if k < 2:
                            last = nc.tensor.transpose(out, key[:, t, :], st.eye[:])
                        else:
                            last = nc.tensor.transpose(out[0:QL, :], nq[:, t, :], st.eye[:])
                    last.then_inc(lat_ps, 1)

            def body(i, s, last):
                if not last:
                    turn(i + 1)
                    project(i + 1)
                latents(i)

            turn(0)
            project(0)
            groups(pe, body)

    tmp.close()


def choose(nc, a, st, ctx):
    def sem(name):
        return ctx.enter_context(nc.semaphore(name))

    tmp = ExitStack()

    def sb(name, shape, dt=F32):
        return tmp.enter_context(nc.sbuf_tensor(name, shape, dt))

    left = sb("ch_left", [B, 2, T])
    top = sb("ch_top", [B, 8])
    taken = sb("ch_taken", [B, T])
    rank = sb("ch_rank", [B, T])
    place = sb("ch_place", [B, T])
    place1 = sb("ch_place1", [B, T])
    ones = sb("ch_ones", [B, T])
    mean_w = sb("ch_mean_w", [P, P])
    gm = sb("ch_gm", [P, B])
    gd = sb("ch_gd", [P, B, 3])
    ge = sb("ch_ge", [P, B, 3])
    gs = sb("ch_gs", [P, B])
    gr = sb("ch_gr", [P, B])
    bk = st.bank

    imp_T = sem("ch_imp_T")
    step = sem("ch_vector_step")
    mean_ready = sem("ch_mean_ready")
    place_ready = sem("ch_place_ready")
    place_T = sem("ch_place_T")
    gate_ps = sem("ch_gate_ps")
    gate_off = sem("ch_gate_off")
    gate_exp = sem("ch_gate_exp")

    with nc.Block() as block:

        @block.tensor
        def _(pe):
            for h in range(HALVES):
                last = nc.tensor.transpose(bk[0][0:B, h * P:(h + 1) * P], st.imp[:, h, :], st.eye[:])
            last.then_inc(imp_T, 1)
            pe.wait_ge(mean_ready, 1)
            for h in range(HALVES):
                last = nc.tensor.matmul(bk[1][:, 0:B * 3], mean_w[:], st.gl[:, h].rearrange("p b k -> p (b k)"),
                                        start=(h == 0), stop=(h == HALVES - 1))
            last.then_inc(gate_ps, 1)
            pe.wait_ge(place_ready, 1)
            for h in range(HALVES):
                last = nc.tensor.transpose(bk[2][:, h * B:(h + 1) * B], place1[:, h * P:(h + 1) * P],
                                           st.eye[0:B, 0:B])
            last.then_inc(place_T, 1)

        @block.vector
        def _(dve):
            n = 0

            def after(ins):
                nonlocal n
                n += 1
                ins.then_inc(step, 1)
                dve.wait_ge(step, n)

            nc.vector.memset(mean_w[:], 1.0 / T).then_inc(mean_ready, 1)
            after(nc.vector.memset(ones[:], 1.0))
            dve.wait_ge(imp_T, 1)
            after(nc.vector.tensor_copy(left[:, 0, :], bk[0][0:B, 0:T]))
            for r in range(KEEP // 8):
                after(nc.vector.max(top[:], left[:, r % 2, :]))
                after(nc.vector.match_replace(left[:, (r + 1) % 2, :], top[:], left[:, r % 2, :], GONE))
            after(nc.vector.tensor_scalar(taken[:], left[:, 0, :], GONE, None, ALU.is_equal))
            after(nc.vector.tensor_tensor_scan(rank[:], ones[:], taken[:], 0.0, ALU.mult, ALU.add))
            after(nc.vector.tensor_tensor(place[:], rank[:], taken[:], ALU.mult))
            nc.vector.tensor_scalar(place1[:], place[:], -1.0, None, ALU.add).then_inc(place_ready, 1)
            dve.wait_ge(gate_ps, 1)
            gl = bk[1][:, 0:B * 3].rearrange("p (b k) -> p b k", k=3)
            after(nc.vector.reduce_max(gm[:], gl, axis=AX.X))
            nc.vector.tensor_tensor(gd[:], gl, bcast(gm[:], 3), ALU.subtract).then_inc(gate_off, 1)
            dve.wait_ge(gate_exp, 1)
            after(nc.vector.reduce_sum(gs[:], ge[:], axis=AX.X))
            after(nc.vector.reciprocal(gr[:], gs[:]))
            after(nc.vector.tensor_tensor(gd[:], ge[:], bcast(gr[:], 3), ALU.mult))
            after(nc.vector.tensor_scalar(st.gates[:, :, 0:3:2], gd[:, :, 0:3:2], 1.0 / WEIGHT_SCALE, None, ALU.mult))
            after(nc.vector.tensor_copy(st.gates[:, :, 1:2], gd[:, :, 1:2]))
            dve.wait_ge(place_T, 1)
            after(nc.vector.tensor_copy(st.place[:].rearrange("p b h -> p h b"),
                                        bk[2][:, 0:HALVES * B].rearrange("p (h b) -> p h b", b=B)))

        @block.scalar
        def _(act):
            act.wait_ge(gate_off, 1)
            nc.scalar.activation(ge[:], gd[:], ACT.Exp).then_inc(gate_exp, 1)

    tmp.close()


def selected(nc, a, st, ctx):
    def sem(name):
        return ctx.enter_context(nc.semaphore(name))

    tmp = ExitStack()

    def sb(name, shape, dt=F32):
        return tmp.enter_context(nc.sbuf_tensor(name, shape, dt))

    xn = sb("se_xn", [P, GT, C])
    pick = sb("se_pick", [P, GT, KEEP])
    selT = sb("se_selT", [P, P])
    keys = sb("se_keys", [P, HEADS, HD])
    rot = sb("se_rot", [P, HEADS, ROPE])
    keysT = sb("se_keysT", [HD, GRP, HEADS, KEEP])
    vals = sb("se_vals", [P, GRP, QUADS, QUAD * (VD + 1)])
    bk = st.bank

    xn_in = sem("se_xn_in")
    picked = sem("se_picked")
    sel_ps = sem("se_sel_ps")
    selT_ready = sem("se_selT_ready")
    keys_ps = sem("se_keys_ps")
    rot_ready = sem("se_rot_ready")
    keys_ready = sem("se_keys_ready")
    keysT_ps = sem("se_keysT_ps")
    keysT_ready = sem("se_keysT_ready")
    vals_ps = sem("se_vals_ps")
    vals_init = sem("se_vals_init")
    vals_ready = sem("se_vals_ready")
    keys_out = sem("se_keys_out")
    vals_out = sem("se_vals_out")
    xn_dram = st.d_xn.rearrange("t p c -> p t c")
    hr = ROPE // 2

    with nc.Block() as block:

        @block.sync
        def _(sp):
            def load(i):
                sp.dma_start(xn[:], xn_dram[:, ds(i * GT, GT), :]).then_inc(xn_in, 16)

            def store(i):
                sp.wait_ge(vals_ready, QUAD * GRP * (i + 2))
                quads = ds(i * GRP * QUADS, GRP * QUADS)
                sp.dma_start(st.d_vs[quads].rearrange("q p n -> p q n"),
                             vals[:].rearrange("p b g n -> p (b g) n")).then_inc(vals_out, 16)
                sp.wait_ge(keysT_ready, QUADS * (i + 2))
                sp.dma_start(st.d_ks[quads].rearrange("q p n -> p q n"),
                             keysT[:].rearrange("p b (g h) n -> p (b g) (h n)", g=QUADS)).then_inc(keys_out, 16)

            sp.sem_inc(keys_out, 16)
            sp.sem_inc(vals_out, 16)
            load(0)
            with sp.Fori(0, NGRP - 1) as i:
                sp.wait_ge(sel_ps, i + 1)
                load(i + 1)
                store(i)
            store(NGRP - 1)
            sp.wait_ge(keys_out, 16 * NGRP + 16)
            sp.wait_ge(vals_out, 16 * NGRP + 16)

        @block.vector
        def _(dve):
            nc.vector.memset(vals[:], 0.0).then_inc(vals_init, 1)
            dve.wait_ge(vals_init, 1)
            for j in range(QUAD):
                nc.vector.memset(vals[KEEP * j:KEEP * (j + 1), :, :, j * (VD + 1) + VD:(j + 1) * (VD + 1)],
                                 1.0).then_inc(vals_init, 1)
            dve.wait_ge(vals_init, 1 + QUAD)
            with dve.Fori(0, NGRP) as i:
                nc.vector.tensor_tensor(pick[:], st.iota[:].unsqueeze(1).to_broadcast([P, GT, KEEP]),
                                        bcast(st.place[:, ds(i * GRP, GRP), :].rearrange("p b h -> p (b h)"), KEEP),
                                        ALU.is_equal).then_inc(picked, 1)
                dve.wait_ge(sel_ps, i + 1)
                nc.vector.tensor_copy(selT[:], bk[0][:, 0:P]).then_inc(selT_ready, 1)
                for g in range(QUADS):
                    dve.wait_ge(keys_ps, QUADS * i + g + 1)
                    k = bk[1 + g][:, 0:QUAD * HD].rearrange("p (h d) -> p h d", d=HD)
                    hs = slice(QUAD * g, QUAD * (g + 1))

                    def tab(t, lo, hi):
                        return t[:, lo:hi].unsqueeze(1).to_broadcast([P, QUAD, hi - lo])
                    nc.vector.tensor_tensor(rot[:, hs, 0:hr], k[:, :, hr:ROPE], tab(st.sin_sel, 0, hr),
                                            ALU.mult).then_inc(rot_ready, 1)
                    nc.vector.tensor_tensor(rot[:, hs, hr:ROPE], k[:, :, 0:hr], tab(st.sin_sel, hr, ROPE),
                                            ALU.mult).then_inc(rot_ready, 1)
                    nc.vector.tensor_tensor(keys[:, hs, 0:ROPE], k[:, :, 0:ROPE], tab(st.cos_sel, 0, ROPE),
                                            ALU.mult).then_inc(rot_ready, 1)
                    nc.vector.tensor_copy(keys[:, hs, ROPE:HD], k[:, :, ROPE:HD])
                    dve.wait_ge(rot_ready, 3 * (QUADS * i + g + 1))
                    nc.vector.tensor_tensor(keys[:, hs, 0:ROPE], keys[:, hs, 0:ROPE], rot[:, hs, :],
                                            ALU.add).then_inc(keys_ready, 1)

        @block.scalar
        def _(act):
            act.sem_inc(vals_ready, QUAD * GRP)
            act.sem_inc(keysT_ready, QUADS)
            act.wait_ge(vals_init, 1 + QUAD)
            with act.Fori(0, NGRP) as i:
                act.wait_ge(vals_ps, i + 1)
                act.wait_ge(vals_out, 16 * i + 16)
                pv = bk[5][:, :].rearrange("p (g h d) -> p g h d", g=QUADS, h=QUAD)
                for b in range(GRP):
                    for j in range(QUAD):
                        nc.scalar.activation(vals[KEEP * j:KEEP * (j + 1), b, :, j * (VD + 1):j * (VD + 1) + VD],
                                             pv[KEEP * b:KEEP * (b + 1), :, j, :], ACT.Copy).then_inc(vals_ready, 1)
                act.wait_ge(keys_out, 16 * i + 16)
                for g in range(QUADS):
                    act.wait_ge(keysT_ps, QUADS * i + g + 1)
                    nc.scalar.activation(keysT[:, :, QUAD * g:QUAD * (g + 1), :].rearrange("p b h j -> p h b j"),
                                         bk[1 + g][0:HD, :].rearrange("p (h b j) -> p h b j", h=QUAD, b=GRP),
                                         ACT.Copy).then_inc(keysT_ready, 1)

        @block.tensor
        def _(pe):
            with pe.Fori(0, NGRP) as i:
                pe.wait_ge(xn_in, 16 * i + 16)
                pe.wait_ge(picked, i + 1)
                for b in range(GRP):
                    for h in range(HALVES):
                        last = nc.tensor.matmul(bk[0][:, b * KEEP:(b + 1) * KEEP], xn[:, b * HALVES + h, :],
                                                pick[:, b * HALVES + h, :], start=(h == 0), stop=(h == HALVES - 1))
                last.then_inc(sel_ps, 1)
                pe.wait_ge(selT_ready, i + 1)
                pe.wait_ge(vals_ready, QUAD * GRP * (i + 1))
                nc.tensor.matmul(bk[5][:, :], selT[:], st.w_vs[:], start=True, stop=True).then_inc(vals_ps, 1)
                for g in range(QUADS):
                    pe.wait_ge(keysT_ready, QUADS * i + g + 1)
                    nc.tensor.matmul(bk[1 + g][:, 0:QUAD * HD], selT[:],
                                     st.w_ks[:, QUAD * g:QUAD * (g + 1), :].rearrange("p h d -> p (h d)"),
                                     start=True, stop=True).then_inc(keys_ps, 1)
                for g in range(QUADS):
                    pe.wait_ge(keys_ready, QUADS * i + g + 1)
                    for j in range(QUAD):
                        last = nc.tensor.transpose(bk[1 + g][0:HD, j * P:(j + 1) * P], keys[:, QUAD * g + j, :],
                                                   st.eye[:])
                    last.then_inc(keysT_ps, 1)

    tmp.close()


def load_expert_weights(sp, a, st, l, loaded):
    sp.dma_start(st.w1_raw[:], a["w1"][ds(l, 1)].rearrange("o e h f -> h (o e) f")).then_inc(loaded, 16)
    for e in range(EXPERTS):
        sp.dma_start(st.w2_raw[:, e], a["w2"][ds(l, 1), e].rearrange("o (f p) c -> p (o f) c", p=P))\
            .then_inc(loaded, 16)


def attention(nc, a, st, ctx):
    def sem(name):
        return ctx.enter_context(nc.semaphore(name))

    tmp = ExitStack()

    def sb(name, shape, dt=F32):
        return tmp.enter_context(nc.sbuf_tensor(name, shape, dt))

    UNITS = QUAD * HALVES
    VW = VD + 1
    UW = 2 * 3 * VD
    hr = ROPE // 2
    nqT = sb("at_nqT", [QL, T])
    xnT = sb("at_xnT", [P, T])
    latT = sb("at_latT", [P, T])
    nq_parts = [sb(f"at_nq_{k}", [QL, T], F32R) for k in ("high", "low")]
    xn_parts = [sb(f"at_xn_{k}", [P, T], F32R) for k in ("high", "low")]
    keys = sb("at_keys", [P, 2, 1 + QUAD, T])
    qT = sb("at_qT", [P, QUAD, T])
    ksel = sb("at_ksel", [HD, QUAD * KEEP])
    vsel = sb("at_vsel", [P, QUAD * VW])
    vals = sb("at_vals", [P, 2, HALVES * 2 * QUAD, 3, VD], BF16)
    v_rest = sb("at_v_rest", [P, HALVES * 2 * QUAD, VD])
    q_tok = sb("at_q_tok", [P, HALVES, QUAD, QW])
    k_tok = sb("at_k_tok", [P, HALVES, QUAD, HD])
    q_sin = sb("at_q_sin", [P, HALVES, QUAD, ROPE])
    q_cos = sb("at_q_cos", [P, HALVES, QUAD, ROPE])
    k_sin = sb("at_k_sin", [P, HALVES, QUAD, ROPE])
    k_cos = sb("at_k_cos", [P, HALVES, QUAD, ROPE])
    prob = sb("at_prob", [P, 2, 2 * T])
    high = sb("at_high", [P, 2, 2 * T], F16)
    low = sb("at_low", [P, 2, 2 * T], F16)
    nmax = sb("at_nmax", [P, UNITS, 2])
    max2 = sb("at_max2", [P, HALVES * QUAD])
    off2 = sb("at_off2", [P, HALVES * QUAD, KEEP])
    prob2 = sb("at_prob2", [P, HALVES, QUAD * KEEP])
    prob2T = sb("at_prob2T", [P, HALVES, P])
    sums = sb("at_sums", [P, 2, HALVES, 3, QUAD])
    inv = sb("at_inv", [P, HALVES, 3, QUAD])
    share = sb("at_share", [P, 2, HALVES, 3, QUAD])
    osum = sb("at_osum", [P, 2, HALVES, 3, QUAD, VD])
    part = sb("at_part", [P, HALVES, 3, QUAD, VD])
    part13 = sb("at_part13", [P, HALVES, QUAD * VD])
    o = sb("at_o", [P, HALVES, QUAD * VD])

    S = st.bank[0:2]
    PT = st.bank[2:4]
    O = st.bank[4:6]
    M = st.bank[6:8]
    HM = [M[0], M[0], M[0], M[1]]

    nq_in = sem("at_nq_in")
    tok_in = sem("at_tok_in")
    shared_in = [sem(f"at_shared_in{s}") for s in range(2)]
    in_split = sem("at_in_split")
    ksel_in = sem("at_ksel_in")
    vsel_in = sem("at_vsel_in")
    s_ps = sem("at_s_ps")
    s2_ps = sem("at_s2_ps")
    q_ps = sem("at_q_ps")
    k_ps = sem("at_k_ps")
    heads_ps = sem("at_heads_ps")
    v_ps = sem("at_v_ps")
    pT_ps = sem("at_pT_ps")
    p2T_ps = sem("at_p2T_ps")
    av2_done = sem("at_av2_done")
    av_done = sem("at_av_done")
    q_taken = sem("at_q_taken")
    k_taken = sem("at_k_taken")
    q_turned = sem("at_q_rotated")
    k_turned = sem("at_k_rotated")
    q_roped = sem("at_q_roped")
    k_roped = sem("at_k_roped")
    heads_ready = sem("at_heads_ready")
    v_high = sem("at_v_high")
    v_rested = sem("at_v_rested")
    v_mid = sem("at_v_mid")
    v_ready = sem("at_v_ready")
    nmax_ready = sem("at_nmax_ready")
    max2_ready = sem("at_max2_ready")
    s2_taken = sem("at_s2_taken")
    p_ready = sem("at_p_ready")
    p2_ready = sem("at_p2_ready")
    high_ready = sem("at_high_ready")
    low_ready = sem("at_low_ready")
    p2T_ready = sem("at_p2T_ready")
    sum2_ready = sem("at_sum2_ready")
    inv_ready = sem("at_inv_ready")
    share_ready = sem("at_share_ready")
    osum_ready = sem("at_osum_ready")
    o2_taken = sem("at_o2_taken")
    combined = sem("at_combined")
    o_ready = sem("at_o_ready")
    o_out = sem("at_o_out")
    init = sem("at_init")
    state_in = sem("at_state_in")

    def unit_keys(u):
        return P * (u % HALVES + 1)

    def wait(eng, s, n):
        if not isinstance(n, int) or n > 0:
            eng.wait_ge(s, n)

    def following(b, g, n):
        return b + 1 if g + n >= QUADS else b

    def more(i):
        return not (isinstance(i, int) and i >= NQ - 2)

    def quads(eng, body):
        for g in range(QUADS):
            body(g, 0, g, False)
        with eng.Fori(1, B - 1) as b:
            for g in range(QUADS):
                body(b * QUADS + g, b, g, False)
        for g in range(QUADS):
            body(NQ - QUADS + g, B - 1, g, g == QUADS - 1)

    def ahead(i, s, u, last):
        if u < UNITS:
            return i, s, u
        return None if last else (i + 1, 1 - s, u - UNITS)

    with nc.Block() as block:

        @block.sync
        def _(sp):
            def load_inputs(b):
                sp.dma_start(nqT[:], st.d_nqT[ds(b, 1)].rearrange("b c n -> c (b n)")).then_inc(nq_in, 16)
                sp.dma_start(xnT[:], st.d_xnT[ds(b, 1)].rearrange("b c n -> c (b n)")).then_inc(tok_in, 16)
                sp.dma_start(latT[:], st.d_kvT[ds(b, 1)].rearrange("b c n -> c (b n)")).then_inc(tok_in, 16)

            def load_shared(b, s):
                sp.dma_start(keys[:, s, 0, :], st.d_kvT[ds(b, 1)].rearrange("b c n -> c (b n)"))\
                    .then_inc(shared_in[s], 16)

            def load_ksel(q):
                sp.dma_start(ksel[:], st.d_ks[ds(q, 1)].rearrange("o p n -> p (o n)")).then_inc(ksel_in, 16)

            def load_vsel(q):
                sp.dma_start(vsel[:], st.d_vs[ds(q, 1)].rearrange("o p n -> p (o n)")).then_inc(vsel_in, 16)

            def store(q):
                sp.wait_ge(o_ready, q + 1)
                sp.dma_start(st.d_o[ds((q // QUADS) * HALVES, HALVES), :, ds((q % QUADS) * QUAD * VD, QUAD * VD)]
                             .rearrange("h p n -> p h n"), o[:]).then_inc(o_out, 16)

            def body(i, b, g, last):
                renew = g >= 2 and more(i)
                if not last:
                    sp.wait_ge(s2_ps, i + 1)
                    load_ksel(i + 1)
                if g == 2 and renew:
                    sp.wait_ge(q_ps, HALVES * (i + 2))
                    sp.wait_ge(v_ps, i + 2)
                    load_inputs(b + 1)
                if not last:
                    sp.wait_ge(av2_done, i + 1)
                    load_vsel(i + 1)
                if renew:
                    sp.wait_ge(s_ps, UNITS * (i + 1))
                    load_shared(b + 1, g % 2)
                if not (isinstance(i, int) and i == 0):
                    store(i - 1)

            load_inputs(0)
            load_shared(0, 0)
            load_shared(0, 1)
            load_ksel(0)
            load_vsel(0)
            sp.dma_start(st.state[:], st.d_xn.rearrange("t p c -> p t c")).then_inc(state_in, 16)
            load_expert_weights(sp, a, st, 0, state_in)
            quads(sp, body)
            store(NQ - 1)
            sp.wait_ge(o_out, 16 * NQ)
            sp.wait_ge(state_in, 16 * (1 + 1 + EXPERTS))

        @block.gpsimd
        def _(pool):
            def rope(q, t, tok, sin, cos, taken, turned, roped):
                def tab(x, lo, hi):
                    return x[:, t, lo:hi].unsqueeze(1).to_broadcast([P, QUAD, hi - lo])
                pool.wait_ge(taken, HALVES * q + t + 1)
                nc.gpsimd.tensor_tensor(sin[:, t, :, 0:hr], tok[:, t, :, hr:ROPE], tab(st.sin, 0, hr), ALU.mult)
                nc.gpsimd.tensor_tensor(sin[:, t, :, hr:ROPE], tok[:, t, :, 0:hr], tab(st.sin, hr, ROPE), ALU.mult)
                nc.gpsimd.tensor_tensor(cos[:, t], tok[:, t, :, 0:ROPE], tab(st.cos, 0, ROPE),
                                        ALU.mult).then_inc(turned, 1)
                pool.wait_ge(turned, HALVES * q + t + 1)
                nc.gpsimd.tensor_tensor(tok[:, t, :, 0:ROPE], cos[:, t], sin[:, t], ALU.add).then_inc(roped, 1)

            def rope_k(q, t):
                rope(q, t, k_tok, k_sin, k_cos, k_taken, k_turned, k_roped)

            def rope_q(q, t):
                rope(q, t, q_tok, q_sin, q_cos, q_taken, q_turned, q_roped)

            def values(q, s):
                pool.wait_ge(v_mid, q + 1)
                nc.gpsimd.tensor_tensor(vals[:, s, :, 2, :], v_rest[:], vals[:, s, :, 1, :],
                                        ALU.subtract).then_inc(v_ready, 1)

            def combine(q, s):
                pool.wait_ge(share_ready, HALVES * (q + 1))
                pool.wait_ge(osum_ready, UNITS * (q + 1))
                pool.wait_ge(o2_taken, q + 1)
                wait(pool, o_ready, q)
                for t in range(HALVES):
                    nc.gpsimd.tensor_tensor(part[:, t], osum[:, s, t], bcast(share[:, s, t], VD),
                                            ALU.mult).then_inc(combined, 1)
                pool.wait_ge(combined, 3 * q + 2)
                pv = part[:].rearrange("p t k h d -> p t k (h d)")
                nc.gpsimd.tensor_tensor(part13[:], pv[:, :, 0, :], pv[:, :, 2, :], ALU.add).then_inc(combined, 1)
                wait(pool, o_out, 16 * q)
                pool.wait_ge(combined, 3 * q + 3)
                nc.gpsimd.tensor_tensor(o[:], part13[:], pv[:, :, 1, :], ALU.add).then_inc(o_ready, 1)

            def body(i, b, g, last):
                s = g % 2
                if not last:
                    rope_k(i + 1, 1)
                    rope_q(i + 1, 0)
                    rope_q(i + 1, 1)
                if not (isinstance(i, int) and i == 0):
                    combine(i - 1, 1 - s)
                if not last:
                    values(i + 1, 1 - s)
                if more(i):
                    rope_k(i + 2, 0)

            for t in range(HALVES):
                rope_k(0, t)
                rope_q(0, t)
            values(0, 0)
            rope_k(1, 0)
            quads(pool, body)
            combine(NQ - 1, 1)

        @block.vector
        def _(dve):
            def unit_max(i, s, u):
                dve.wait_ge(s_ps, UNITS * i + u + 1)
                nc.vector.tensor_reduce(nmax[:, u, :],
                                        S[u % 2][:, 0:2 * unit_keys(u)].rearrange("p (a k) -> p a k", a=2),
                                        AX.X, ALU.max, negate=True).then_inc(nmax_ready, 1)

            def unit_low(i, u):
                dve.wait_ge(high_ready, UNITS * i + u + 1)
                n = 2 * unit_keys(u)
                nc.vector.scalar_tensor_tensor(low[:, u % 2, 0:n], PT[u % 2][:, 0:n], WEIGHT_SCALE,
                                               high[:, u % 2, 0:n], ALU.mult, ALU.subtract).then_inc(low_ready, 1)

            def unit_sum(i, s, u):
                h, t = divmod(u, HALVES)
                dve.wait_ge(av_done, UNITS * i + u + 1)
                if u < HALVES:
                    wait(dve, combined, 3 * (i - 1))
                nc.vector.reduce_sum(osum[:, s, t, 0:3:2, h, :],
                                     O[t][:, 0:UW].rearrange("p (k j d) -> p k d j", k=2, j=3),
                                     axis=AX.X).then_inc(osum_ready, 1)

            def rest(q, s):
                dve.wait_ge(v_high, q + 1)
                wait(dve, v_ready, q)
                nc.vector.tensor_tensor(v_rest[:], M[0].rearrange("p (n d) -> p n d", d=VD), vals[:, s, :, 0, :],
                                        ALU.subtract).then_inc(v_rested, 1)

            def split_xn(b):
                dve.wait_ge(tok_in, 32 * (b + 1))
                wait(dve, k_ps, HALVES * QUADS * b)
                nc.vector.tensor_copy(xn_parts[0][:], xnT[:]).then_inc(in_split, 1)
                dve.wait_ge(in_split, 4 * b + 1)
                nc.vector.tensor_tensor(xn_parts[1][:], xnT[:], xn_parts[0][:], ALU.subtract).then_inc(in_split, 1)

            def split_nq(b):
                dve.wait_ge(nq_in, 16 * (b + 1))
                wait(dve, q_ps, HALVES * QUADS * b)
                nc.vector.tensor_copy(nq_parts[0][:], nqT[:]).then_inc(in_split, 1)
                dve.wait_ge(in_split, 4 * b + 3)
                nc.vector.tensor_tensor(nq_parts[1][:], nqT[:], nq_parts[0][:], ALU.subtract).then_inc(in_split, 1)

            def chosen_off(i):
                dve.wait_ge(s2_ps, i + 1)
                s2 = M[1][:, 0:HALVES * QUAD * KEEP].rearrange("p (n k) -> p n k", k=KEEP)
                nc.vector.reduce_max(max2[:], s2, axis=AX.X).then_inc(max2_ready, 1)
                dve.wait_ge(max2_ready, i + 1)
                nc.vector.tensor_tensor(off2[:], s2, bcast(max2[:], KEEP), ALU.subtract).then_inc(s2_taken, 1)

            def body(i, b, g, last):
                s = g % 2
                for u in range(UNITS):
                    if n := ahead(i, s, u + 2, last):
                        unit_max(*n)
                    if u >= 2:
                        unit_sum(i, s, u - 2)
                    elif not (isinstance(i, int) and i == 0):
                        unit_sum(i - 1, 1 - s, UNITS - 2 + u)
                    unit_low(i, u)
                    if g == 2 and more(i) and u == 5:
                        split_xn(b + 1)
                    if g == 2 and more(i) and u == 6:
                        split_nq(b + 1)
                    if u == 3:
                        chosen_off(i)
                    if u == 2 and not last:
                        rest(i + 1, 1 - s)
                    if u == 5:
                        dve.wait_ge(p2_ready, i + 1)
                        nc.vector.reduce_sum(sums[:, s, :, 1, :], prob2[:].rearrange("p t (h k) -> p t h k", h=QUAD),
                                             axis=AX.X).then_inc(sum2_ready, 1)
                    if u == 7:
                        dve.wait_ge(p_ready, UNITS * (i + 1))
                        dve.wait_ge(sum2_ready, i + 1)
                        nc.vector.reciprocal(inv[:], sums[:, s]).then_inc(inv_ready, 1)
                        dve.wait_ge(inv_ready, i + 1)
                        gate = st.gates[:, ds(i // QUADS, 1), :]
                        for t in range(HALVES):
                            nc.vector.tensor_tensor(share[:, s, t], inv[:, t],
                                                    gate.rearrange("p o k -> p (o k)").unsqueeze(2)
                                                    .to_broadcast([P, 3, QUAD]), ALU.mult).then_inc(share_ready, 1)

            for s in range(2):
                nc.vector.memset(keys[:, s, 1:1 + QUAD, :], 0.0).then_inc(init, 1)
            split_xn(0)
            split_nq(0)
            rest(0, 0)
            unit_max(0, 0, 0)
            unit_max(0, 0, 1)
            quads(dve, body)
            for u in (UNITS - 2, UNITS - 1):
                unit_sum(NQ - 1, 1, u)

        @block.scalar
        def _(act):
            def unit_exp(i, s, u):
                act.wait_ge(nmax_ready, UNITS * i + u + 1)
                if u == 0:
                    wait(act, inv_ready, i - 1)
                h, t = divmod(u, HALVES)
                n = unit_keys(u)
                for k in range(2):
                    last = nc.scalar.activation(prob[:, u % 2, k * n:(k + 1) * n], S[u % 2][:, k * n:(k + 1) * n],
                                                ACT.Exp, bias=nmax[:, u, k:k + 1],
                                                accum_out=sums[:, s, t, 2 * k, h:h + 1])
                last.then_inc(p_ready, 1)

            def unit_high(i, u):
                act.wait_ge(pT_ps, UNITS * i + u + 1)
                wait(act, av_done, UNITS * i + u - 1)
                n = 2 * unit_keys(u)
                nc.scalar.activation(high[:, u % 2, 0:n], PT[u % 2][:, 0:n], ACT.Copy,
                                     scale=WEIGHT_SCALE).then_inc(high_ready, 1)

            def take_k(q, t):
                act.wait_ge(k_ps, HALVES * q + t + 1)
                nc.scalar.activation(k_tok[:, t].rearrange("p h d -> p (h d)"), M[0][:, 0:QUAD * HD],
                                     ACT.Copy).then_inc(k_taken, 1)

            def take_q(q, t):
                act.wait_ge(q_ps, HALVES * q + t + 1)
                nc.scalar.activation(q_tok[:, t].rearrange("p h d -> p (h d)"), M[1][:, 0:QUAD * QW],
                                     ACT.Copy).then_inc(q_taken, 1)

            def head(q, s, h):
                act.wait_ge(heads_ps, QUAD * q + h + 1)
                nc.scalar.activation(qT[:, h, :], HM[h][:, 0:T], ACT.Copy)
                nc.scalar.activation(keys[0:HD, s, 1 + h, :], HM[h][0:HD, T:2 * T],
                                     ACT.Copy).then_inc(heads_ready, 1)

            def values(q, s):
                act.wait_ge(v_ps, q + 1)
                wait(act, av_done, UNITS * (q - 1))
                nc.scalar.activation(vals[:, s, :, 0, :], M[0].rearrange("p (n d) -> p n d", d=VD),
                                     ACT.Copy).then_inc(v_high, 1)

            def middle(q, s):
                act.wait_ge(v_rested, q + 1)
                nc.scalar.activation(vals[:, s, :, 1, :], v_rest[:], ACT.Copy).then_inc(v_mid, 1)

            def body(i, b, g, last):
                s = g % 2
                q, r = i + 1, 1 - s
                for u in range(UNITS):
                    if n := ahead(i, s, u + 1, last):
                        unit_exp(*n)
                    unit_high(i, u)
                    if u == 4:
                        act.wait_ge(s2_taken, i + 1)
                        wait(act, sum2_ready, i)
                        nc.scalar.activation(prob2[:].rearrange("p q n -> p (q n)"),
                                             off2[:].rearrange("p n k -> p (n k)"), ACT.Exp).then_inc(p2_ready, 1)
                    if u >= 4 and not last and u < 7:
                        head(q, r, u - 4)
                    if u == 5:
                        act.wait_ge(p2T_ps, i + 1)
                        nc.scalar.activation(prob2T[:].rearrange("p q n -> p (q n)"), M[1][:, 0:HALVES * P],
                                             ACT.Copy).then_inc(p2T_ready, 1)
                    if u == 6:
                        act.wait_ge(av2_done, i + 1)
                        nc.scalar.activation(osum[:, s, :, 1].rearrange("p t h d -> p t (h d)"),
                                             M[1][:, 0:HALVES * QUAD * VD].rearrange("p (t n) -> p t n", t=HALVES),
                                             ACT.Copy).then_inc(o2_taken, 1)
                    if last:
                        continue
                    if u == 0:
                        take_k(q, 1)
                        take_q(q, 0)
                    if u == 1:
                        take_q(q, 1)
                        values(q, r)
                    if u == 3:
                        middle(q, r)
                    if u == 7:
                        head(q, r, QUAD - 1)
                        if more(i):
                            take_k(q + 1, 0)

            act.wait_ge(init, 2)
            for t in range(HALVES):
                take_k(0, t)
                take_q(0, t)
            values(0, 0)
            middle(0, 0)
            for h in range(QUAD):
                head(0, 0, h)
            take_k(1, 0)
            unit_exp(0, 0, 0)
            quads(act, body)

        @block.tensor
        def _(pe):
            def parted(out, x, w, t, c):
                for n, (j, k) in enumerate(((0, 0), (1, 0), (0, 1))):
                    last = nc.tensor.matmul(out, x[j][:, t * P:(t + 1) * P],
                                            w[k][:, c * QUAD:(c + 1) * QUAD, :].rearrange("p h d -> p (h d)"),
                                            start=(n == 0), stop=(n == 2))
                return last

            def queries(q, t, b, c):
                if t == 0:
                    wait(pe, heads_ready, QUAD * q)
                    pe.wait_ge(in_split, 4 * b + 4)
                else:
                    pe.wait_ge(q_taken, HALVES * q + 1)
                parted(M[1][:, 0:QUAD * QW], nq_parts, st.w_q_parts, t, c).then_inc(q_ps, 1)

            def window_keys(q, t, b, c):
                if t == 0:
                    wait(pe, heads_ready, QUAD * q - 1)
                    pe.wait_ge(in_split, 4 * b + 2)
                else:
                    pe.wait_ge(k_taken, HALVES * q + 1)
                parted(M[0][:, 0:QUAD * HD], xn_parts, st.w_kw_parts, t, c).then_inc(k_ps, 1)

            def values(q, c):
                pe.wait_ge(k_taken, HALVES * (q + 1))
                n = QUAD * VD
                cols = slice(c * n, (c + 1) * n)
                for t in range(HALVES):
                    nc.tensor.matmul(M[0][:, 2 * t * n:(2 * t + 1) * n], latT[:, t * P:(t + 1) * P],
                                     st.w_v1[:, cols], start=True, stop=True)
                    last = nc.tensor.matmul(M[0][:, (2 * t + 1) * n:(2 * t + 2) * n], xnT[:, t * P:(t + 1) * P],
                                            st.w_vw[:, cols], start=True, stop=True)
                last.then_inc(v_ps, 1)

            def head(q, h):
                if h == 0:
                    pe.wait_ge(q_roped, HALVES * (q + 1))
                    pe.wait_ge(k_roped, HALVES * (q + 1))
                    pe.wait_ge(v_rested, q + 1)
                elif h == QUAD - 1:
                    wait(pe, o2_taken, q)
                else:
                    pe.wait_ge(heads_ready, QUAD * q + h)
                for t in range(HALVES):
                    nc.tensor.transpose(HM[h][:, t * P:(t + 1) * P], q_tok[:, t, h, :], st.eye[:])
                    last = nc.tensor.transpose(HM[h][0:HD, T + t * P:T + (t + 1) * P], k_tok[:, t, h, :],
                                               st.eye[:])
                last.then_inc(heads_ps, 1)

            def scores(i, s, u):
                h, t = divmod(u, HALVES)
                n = unit_keys(u)
                if t == 0:
                    pe.wait_ge(heads_ready, QUAD * i + h + 1)
                if u == 0:
                    pe.wait_ge(shared_in[s], 16 * (i // QUADS + 1))
                wait(pe, p_ready, UNITS * i + u - 1)
                out = S[u % 2][:, 0:2 * n].rearrange("p (a k) -> p a k", a=2)
                nc.tensor.matmul(out, qT[:, h, t * P:(t + 1) * P], keys[:, s, 0:h + 2:h + 1, 0:n], start=True,
                                 stop=False)
                nc.tensor.matmul(out[:, :, n - P:n], st.eye16[:],
                                 st.causal[:].unsqueeze(1).to_broadcast([P, 2, P]), start=False,
                                 stop=True).then_inc(s_ps, 1)

            def chosen(t):
                for h in range(QUAD):
                    c = (t * QUAD + h) * KEEP
                    last = nc.tensor.matmul(M[1][:, c:c + KEEP], qT[0:HD, h, t * P:(t + 1) * P],
                                            ksel[:, h * KEEP:(h + 1) * KEEP], start=True, stop=True)
                return last

            def turn(i, u):
                pe.wait_ge(p_ready, UNITS * i + u + 1)
                wait(pe, low_ready, UNITS * i + u - 1)
                for k in range(2 * (u % HALVES + 1)):
                    last = nc.tensor.transpose(PT[u % 2][:, k * P:(k + 1) * P], prob[:, u % 2, k * P:(k + 1) * P],
                                               st.eye[:])
                last.then_inc(pT_ps, 1)

            def weigh(i, s, u):
                h, t = divmod(u, HALVES)
                pe.wait_ge(low_ready, UNITS * i + u + 1)
                if u == 0:
                    pe.wait_ge(v_ready, i + 1)
                wait(pe, osum_ready, UNITS * i + u - 1)
                for k in range(2):
                    o0 = k * 3 * VD
                    for kt in range(t + 1):
                        blk = slice((k * (t + 1) + kt) * P, (k * (t + 1) + kt + 1) * P)
                        v = vals[:, s, (kt * 2 + k) * QUAD + h].rearrange("p j d -> p (j d)")
                        nc.tensor.matmul(O[t][:, o0:o0 + 3 * VD], high[:, u % 2, blk], v, start=(kt == 0),
                                         stop=False, skip_group_check=True)
                        last = nc.tensor.matmul(O[t][:, o0:o0 + 2 * VD], low[:, u % 2, blk], v[:, 0:2 * VD],
                                                start=False, stop=(kt == t), skip_group_check=True)
                last.then_inc(av_done, 1)

            def body(i, b, g, last):
                s = g % 2
                q, c = i + 1, (g + 1) % QUADS
                for u in range(UNITS):
                    if n := ahead(i, s, u + 2, last):
                        scores(*n)
                    turn(i, u)
                    if u == 0 and not last:
                        window_keys(q, 1, following(b, g, 1), c)
                        queries(q, 0, following(b, g, 1), c)
                    if u == 1 and not last:
                        queries(q, 1, following(b, g, 1), c)
                        values(q, c)
                    if u == 2:
                        pe.wait_ge(ksel_in, 16 * (i + 1))
                        if last:
                            pe.wait_ge(heads_ready, QUAD * (i + 1))
                        else:
                            pe.wait_ge(q_taken, HALVES * (q + 1))
                        chosen(0)
                        chosen(1).then_inc(s2_ps, 1)
                    if 4 <= u <= 6 and not last:
                        head(q, u - 4)
                    if u == 5:
                        pe.wait_ge(p2_ready, i + 1)
                        for t in range(HALVES):
                            l = nc.tensor.transpose(M[1][:, t * P:(t + 1) * P], prob2[:, t, :], st.eye[:])
                        l.then_inc(p2T_ps, 1)
                    if u == 6:
                        pe.wait_ge(p2T_ready, i + 1)
                        pe.wait_ge(vsel_in, 16 * (i + 1))
                        for t in range(HALVES):
                            l = nc.tensor.matmul(M[1][:, t * QUAD * VD:(t + 1) * QUAD * VD], prob2T[:, t, :],
                                                 vsel[:].rearrange("p (h d) -> p h d", d=VW)[:, :, 0:VD], start=True,
                                                 stop=True)
                        l.then_inc(av2_done, 1)
                    if u == 7 and not last:
                        head(q, QUAD - 1)
                        if more(i):
                            window_keys(q + 1, 0, following(b, g, 2), (g + 2) % QUADS)
                    if u >= 1:
                        weigh(i, s, u - 1)
                    elif not (isinstance(i, int) and i == 0):
                        weigh(i - 1, 1 - s, UNITS - 1)

            for t in range(HALVES):
                window_keys(0, t, 0, 0)
                queries(0, t, 0, 0)
            values(0, 0)
            for h in range(QUAD):
                head(0, h)
            window_keys(1, 0, 0, 1)
            scores(0, 0, 0)
            scores(0, 0, 1)
            quads(pe, body)
            weigh(NQ - 1, 1, UNITS - 1)

    tmp.close()


def experts(nc, a, st, ctx):
    def sem(name):
        return ctx.enter_context(nc.semaphore(name))

    tmp = ExitStack()

    def sb(name, shape, dt=F32):
        return tmp.enter_context(nc.sbuf_tensor(name, shape, dt))

    LE = LAYERS * EXPERTS
    W = CHUNK * P
    PER = EXPERTS * FT
    HALF = FT // 2
    SPLITS = EXPERTS * 2
    state, logits, mv = st.state, st.logits, st.mv
    w1_raw, w2_raw = st.w1_raw, st.w2_raw
    w1 = [sb(f"mo_w1_{k}", [P, EXPERTS, FF], F32R) for k in ("high", "low")]
    w2 = [sb(f"mo_w2_{k}", [P, EXPERTS, FT, C], F32R) for k in ("high", "low")]
    b1_rows = sb("mo_b1_rows", [LE * FT, P])
    gb_rows = sb("mo_gb_rows", [3 * LE, C])
    b1T = sb("mo_b1T", [P, LE * FT])
    gbT = sb("mo_gbT", [P, 3 * LE])
    bias = sb("mo_bias", [P, PER])
    b2 = sb("mo_b2", [P, EXPERTS])
    rw = sb("mo_rw", [C, LAYERS, EXPERTS])
    rb = sb("mo_rb", [P, LE])
    xh = sb("mo_xh", [P, CHUNK, C])
    xhT = [sb(f"mo_xhT_{k}", [P, W], F32R) for k in ("high", "low")]
    h = sb("mo_h", [P, FT, W])
    hs = [sb(f"mo_h_{k}", [P, 2, FT, W], F32R) for k in ("high", "low")]
    yT = sb("mo_yT", [P, 2, W])
    cur = sb("mo_cur", [P, 2, CHUNK, C])
    freshT = sb("mo_freshT", [P, CHUNK, P])
    stats = sb("mo_stats", [P, CHUNK, 6])
    fresh_mv = sb("mo_fresh_mv", [P, CHUNK, 2])
    fresh_var = sb("mo_fresh_var", [P, CHUNK])
    cur_mv = sb("mo_cur_mv", [P, CHUNK, 2])
    cur_comb = sb("mo_cur_comb", [P, CHUNK, EXPERTS])
    vareps = sb("mo_vareps", [P, TILES])
    minus_half = sb("mo_minus_half", [P, TILES])
    comb = sb("mo_comb", [P, TILES, EXPERTS])
    lmax = sb("mo_lmax", [P, TILES])
    loff = sb("mo_loff", [P, TILES, EXPERTS])
    lexp = sb("mo_lexp", [P, TILES, EXPERTS])
    lsum = sb("mo_lsum", [P, TILES])
    linv = sb("mo_linv", [P, TILES])
    pr = sb("mo_pr", [P, TILES, EXPERTS])
    ge = sb("mo_ge", [P, 6, TILES])
    ra = sb("mo_ra", [P, EXPERTS, TILES])
    rc = sb("mo_rc", [P, EXPERTS, TILES])
    kept = sb("mo_kept", [P, TILES, EXPERTS])
    ksum = sb("mo_ksum", [P, TILES])
    kinv = sb("mo_kinv", [P, TILES])

    U = st.bank[0:4]
    YT = st.bank[4]
    Y = st.bank[5]
    TR = st.bank[6]
    RT = st.bank[7]

    small_in = sem("mo_small_in")
    w_in = sem("mo_w_in")
    rows_ps = sem("mo_rows_ps")
    rows_turned = sem("mo_rows_turned")
    w1_high = sem("mo_w1_high")
    w1_ready = sem("mo_w1_ready")
    w2_high = sem("mo_w2_high")
    w2_ready = sem("mo_w2_ready")
    bias_ps = sem("mo_bias_ps")
    bias_ready = sem("mo_bias_ready")
    step = sem("mo_router_step")
    half_ready = sem("mo_half_ready")
    var_ready = sem("mo_var_ready")
    rstd_ready = sem("mo_rstd_ready")
    loff_ready = sem("mo_loff_ready")
    lexp_ready = sem("mo_lexp_ready")
    xh_ready = sem("mo_xh_ready")
    xh_ps = sem("mo_xh_ps")
    xhT_high = sem("mo_xhT_high")
    xhT_ready = sem("mo_xhT_ready")
    up_ps = sem("mo_up_ps")
    h_ready = sem("mo_h_ready")
    h_high = sem("mo_h_high")
    h_low = [sem("mo_h_low_pool"), sem("mo_h_low_vector")]
    yT_ps = sem("mo_yT_ps")
    yT_ready = sem("mo_yT_ready")
    y_ps = sem("mo_y_ps")
    y_taken = sem("mo_y_taken")
    fresh_kept = sem("mo_fresh_kept")
    fresh_ps = sem("mo_fresh_ps")
    freshT_ready = sem("mo_freshT_ready")
    stats_ready = sem("mo_stats_ready")
    aggr_ready = sem("mo_aggr_ready")
    mv_ready = sem("mo_mv_ready")
    fvar_ready = sem("mo_fresh_var_ready")
    frstd_ready = sem("mo_fresh_rstd_ready")
    fetched = sem("mo_fetched")
    cur_mv_ready = sem("mo_cur_mv_ready")
    cur_comb_ready = sem("mo_cur_comb_ready")
    logits_ps = sem("mo_logits_ps")
    logits_ready = sem("mo_logits_ready")
    NSMALL = 6
    LOADS = 16 * (1 + EXPERTS)


    def wait(eng, s, n):
        if not isinstance(n, int) or n > 0:
            eng.wait_ge(s, n)

    def layers(eng, layer):
        layer(0)
        with eng.Fori(1, LAYERS - 1) as l:
            layer(l)
        layer(LAYERS - 1)

    def chunks(eng, l, chunk):
        chunk(l, 0, l * NCH, 0)
        with eng.Fori(0, NCH // 2 - 1) as j:
            for s in (1, 0):
                chunk(l, 2 * j + 2 - s, l * NCH + 2 * j + 2 - s, s)
        chunk(l, NCH - 1, l * NCH + NCH - 1, 1)

    def opens(c):
        return isinstance(c, int) and c == 0

    def closes(c):
        return isinstance(c, int) and c == NCH - 1

    def ends(l, c):
        return isinstance(l, int) and l == LAYERS - 1 and closes(c)

    def begins(n):
        return isinstance(n, int) and n == 0

    def following(c):
        return 0 if closes(c) else c + 1

    def before(c):
        return NCH - 1 if opens(c) else c - 1

    with nc.Block() as block:

        @block.sync
        def _(sp):
            sp.dma_start(b1_rows[:], a["b1"].rearrange("l e (f p) -> (l e f) p", p=P)).then_inc(small_in, 16)
            for k, name in enumerate(("ln_g", "ln_b", "b2")):
                sp.dma_start(gb_rows[k * LE:(k + 1) * LE, :],
                             a[name].rearrange("l e c -> (l e) c")).then_inc(small_in, 16)
            sp.dma_start(rw[:], a["router_w"].rearrange("l h e -> h l e")).then_inc(small_in, 16)
            sp.dma_start(rb[:], a["router_b"].rearrange("(o l) e -> o (l e)", o=1).to_broadcast([P, LE]))\
                .then_inc(small_in, 16)

            with sp.Fori(0, LAYERS - 1) as l:
                sp.wait_ge(w1_ready, EXPERTS * (l + 1))
                sp.wait_ge(w2_ready, EXPERTS * (l + 1))
                sp.wait_ge(bias_ready, l + 1)
                load_expert_weights(sp, a, st, l + 1, w_in)

        @block.gpsimd
        def _(pool):
            nc.gpsimd.memset(minus_half[:], -0.5).then_inc(half_ready, 1)
            pool.wait_ge(half_ready, 1)
            pool.wait_ge(var_ready, 1)
            nc.gpsimd.tensor_tensor(mv[:, :, 1], vareps[:], minus_half[:], ALU.pow).then_inc(rstd_ready, 1)

            def split_w2(l, e):
                pool.wait_ge(w2_high, EXPERTS * l + e + 1)
                nc.gpsimd.tensor_tensor(w2[1][:, e], w2_raw[:, e], w2[0][:, e], ALU.subtract).then_inc(w2_ready, 1)

            def chunk(l, c, n, s):
                for e in range(EXPERTS):
                    pool.wait_ge(h_high, SPLITS * n + 2 * e + 1)
                    nc.gpsimd.tensor_tensor(hs[1][:, e % 2, 0:HALF], h[:, 0:HALF], hs[0][:, e % 2, 0:HALF],
                                            ALU.subtract).then_inc(h_low[0], 1)
                    if closes(c) and not ends(l, c) and e > 0:
                        split_w2(l + 1, e - 1)
                    if opens(c) and not begins(n) and e == 0:
                        split_w2(l, EXPERTS - 1)
                    if e == 1 and not begins(n):
                        pool.wait_ge(fvar_ready, n)
                        nc.gpsimd.tensor_tensor(fresh_mv[:, :, 1], fresh_var[:], minus_half[:, 0:CHUNK],
                                                ALU.pow).then_inc(frstd_ready, 1)

            for e in range(EXPERTS):
                split_w2(0, e)
            layers(pool, lambda l: chunks(pool, l, chunk))

        @block.scalar
        def _(act):
            act.wait_ge(rows_ps, 1)
            nc.scalar.activation(b1T[:], TR[:, 0:LE * FT], ACT.Copy).then_inc(rows_turned, 1)
            nc.scalar.activation(gbT[:], TR[:, LE * FT:LE * FT + 3 * LE], ACT.Copy).then_inc(rows_turned, 1)

            def turned(n):
                act.wait_ge(xh_ps, n + 1)
                wait(act, up_ps, PER * n)
                nc.scalar.activation(xhT[0][:], TR, ACT.Copy).then_inc(xhT_high, 1)

            def gelus(n, e):
                for f in range(FT):
                    act.wait_ge(up_ps, PER * n + e * FT + f + 1)
                    if f == 0:
                        wait(act, h_low[0], EXPERTS * n + e)
                    if f == HALF:
                        wait(act, h_low[1], EXPERTS * n + e)
                    nc.scalar.activation(h[:, f, :], U[f], ACT.Gelu,
                                         bias=bias[:, e * FT + f:e * FT + f + 1]).then_inc(h_ready, 1)

            def output(n, e):
                act.wait_ge(yT_ps, EXPERTS * n + e + 1)
                nc.scalar.activation(yT[:, e % 2], YT, ACT.Identity, bias=b2[:, e:e + 1]).then_inc(yT_ready, 1)

            def keep(n, c, s):
                act.wait_ge(y_taken, EXPERTS * (n + 1))
                nc.scalar.activation(state[:, ds(c * CHUNK, CHUNK), :], cur[:, s], ACT.Copy).then_inc(fresh_kept, 1)

            def fetch(n, c, s):
                wait(act, fresh_ps, n - 1)
                wait(act, stats_ready, n - 1)
                wait(act, fresh_kept, n - 1)
                nc.scalar.activation(cur[:, s], state[:, ds(c * CHUNK, CHUNK), :], ACT.Copy).then_inc(fetched, 1)

            def split_w2(e):
                nc.scalar.activation(w2[0][:, e], w2_raw[:, e], ACT.Copy).then_inc(w2_high, 1)

            def chunk(l, c, n, s):
                if opens(c):
                    act.wait_ge(bias_ready, l + 1)
                gelus(n, 0)
                gelus(n, 1)
                if not begins(n):
                    keep(n - 1, before(c), 1 - s)
                renew = closes(c) and not ends(l, c)
                output(n, 0)
                if renew:
                    act.wait_ge(w_in, LOADS * (l + 1))
                    split_w2(0)
                if not ends(l, c):
                    fetch(n + 1, following(c), 1 - s)
                gelus(n, 2)
                if opens(c):
                    act.wait_ge(loff_ready, l + 1)
                    nc.scalar.activation(lexp[:], loff[:], ACT.Exp).then_inc(lexp_ready, 1)
                output(n, 1)
                if renew:
                    split_w2(1)
                gelus(n, 3)
                output(n, 2)
                if renew:
                    split_w2(2)
                if not ends(l, c):
                    turned(n + 1)
                output(n, 3)
                if renew:
                    split_w2(3)

            for e in range(EXPERTS):
                split_w2(e)
            act.wait_ge(small_in, 16 * NSMALL)
            fetch(0, 0, 0)
            turned(0)
            layers(act, lambda l: chunks(act, l, chunk))
            keep(LAYERS * NCH - 1, NCH - 1, 1)

        @block.vector
        def _(dve):
            def norm(n, c, s):
                nc.vector.tensor_copy(cur_mv[:], mv[:, ds(c * CHUNK, CHUNK), :]).then_inc(cur_mv_ready, 1)
                wait(dve, xh_ps, n)
                dve.wait_ge(fetched, n + 1)
                dve.wait_ge(cur_mv_ready, n + 1)
                for t in range(CHUNK):
                    last = nc.vector.tensor_scalar(xh[:, t, :], cur[:, s, t, :], cur_mv[:, t, 0:1], cur_mv[:, t, 1:2],
                                                   ALU.subtract, ALU.mult)
                last.then_inc(xh_ready, 1)

            def turned_low(n):
                dve.wait_ge(xhT_high, n + 1)
                nc.vector.tensor_tensor(xhT[1][:], TR, xhT[0][:], ALU.subtract).then_inc(xhT_ready, 1)

            def splits(n, e):
                for k in range(2):
                    tiles = slice(k * HALF, (k + 1) * HALF)
                    dve.wait_ge(h_ready, PER * n + e * FT + (k + 1) * HALF)
                    wait(dve, yT_ps, EXPERTS * n + e - 1)
                    nc.vector.tensor_copy(hs[0][:, e % 2, tiles], h[:, tiles]).then_inc(h_high, 1)
                dve.wait_ge(h_high, SPLITS * n + 2 * e + 2)
                nc.vector.tensor_tensor(hs[1][:, e % 2, tiles], h[:, tiles], hs[0][:, e % 2, tiles],
                                        ALU.subtract).then_inc(h_low[1], 1)

            def split_w1(l, e):
                gain = gbT[:, ds(l * EXPERTS + e, 1)]
                nc.vector.tensor_scalar(w1[0][:, e, :], w1_raw[:, e, :], gain, None, ALU.mult).then_inc(w1_high, 1)
                dve.wait_ge(w1_high, EXPERTS * l + e + 1)
                nc.vector.scalar_tensor_tensor(w1[1][:, e, :], w1_raw[:, e, :], gain, w1[0][:, e, :], ALU.mult,
                                               ALU.subtract).then_inc(w1_ready, 1)

            def biases(l):
                dve.wait_ge(bias_ps, l + 1)
                nc.vector.tensor_copy(b2[:], gbT[:, ds(2 * LE + l * EXPERTS, EXPERTS)])
                nc.vector.tensor_tensor(bias[:], RT[:, 0:PER], b1T[:, ds(l * PER, PER)],
                                        ALU.add).then_inc(bias_ready, 1)

            def take_weights(n, c):
                wait(dve, y_taken, EXPERTS * n)
                nc.vector.tensor_copy(cur_comb[:], comb[:, ds(c * CHUNK, CHUNK), :]).then_inc(cur_comb_ready, 1)
                dve.wait_ge(cur_comb_ready, n + 1)

            def add_expert(n, e, s):
                dve.wait_ge(y_ps, EXPERTS * n + e + 1)
                wait(dve, y_taken, EXPERTS * n + e)
                for t in range(CHUNK):
                    last = nc.vector.scalar_tensor_tensor(cur[:, s, t, :], Y[:, t * C:(t + 1) * C],
                                                          cur_comb[:, t, e:e + 1], cur[:, s, t, :], ALU.mult, ALU.add)
                last.then_inc(y_taken, 1)

            def statistics(n, s):
                dve.wait_ge(y_taken, EXPERTS * (n + 1))
                for t in range(CHUNK):
                    last = nc.vector.bn_stats(stats[:, t, :], cur[:, s, t, :])
                last.then_inc(stats_ready, 1)

            def moments(n):
                dve.wait_ge(stats_ready, n + 1)
                wait(dve, mv_ready, n)
                dve.wait_ge(fresh_ps, n + 1)
                nc.vector.tensor_copy(freshT[:].rearrange("p t n -> p (t n)"), TR).then_inc(freshT_ready, 1)
                for t in range(CHUNK):
                    last = nc.vector.bn_aggr(fresh_mv[:, t, :], stats[:, t, :])
                last.then_inc(aggr_ready, 1)
                dve.wait_ge(aggr_ready, n + 1)
                wait(dve, frstd_ready, n)
                nc.vector.tensor_scalar(fresh_var[:], fresh_mv[:, :, 1], MOE_EPS, None, ALU.add).then_inc(fvar_ready, 1)

            def keep_moments(n, c):
                dve.wait_ge(frstd_ready, n + 1)
                nc.vector.tensor_copy(mv[:, ds(c * CHUNK, CHUNK), :], fresh_mv[:]).then_inc(mv_ready, 1)

            def route(n, c, l):
                dve.wait_ge(logits_ps, n + 1)
                nc.vector.tensor_tensor(logits[:, ds(c * CHUNK, CHUNK), :],
                                        RT[:, 0:CHUNK * EXPERTS].rearrange("p (t e) -> p t e", e=EXPERTS),
                                        rb[:, ds(l * EXPERTS, EXPERTS)].unsqueeze(1)
                                        .to_broadcast([P, CHUNK, EXPERTS]), ALU.add).then_inc(logits_ready, 1)

            RSTEPS = 11

            def weights(l):
                k = 0

                def after(ins):
                    nonlocal k
                    k += 1
                    ins.then_inc(step, 1)
                    dve.wait_ge(step, RSTEPS * l + k)

                if not begins(l):
                    dve.wait_ge(logits_ready, NCH * l)
                after(nc.vector.reduce_max(lmax[:], logits[:], axis=AX.X))
                nc.vector.tensor_tensor(loff[:], logits[:], bcast(lmax[:], EXPERTS),
                                        ALU.subtract).then_inc(loff_ready, 1)
                dve.wait_ge(lexp_ready, l + 1)
                after(nc.vector.reduce_sum(lsum[:], lexp[:], axis=AX.X))
                after(nc.vector.reciprocal(linv[:], lsum[:]))
                after(nc.vector.tensor_tensor(pr[:], lexp[:], bcast(linv[:], EXPERTS), ALU.mult))
                pair = {}
                for j in range(EXPERTS):
                    for e in range(j + 1, EXPERTS):
                        pair[j, e] = len(pair)
                        last = nc.vector.tensor_tensor(ge[:, pair[j, e], :], pr[:, :, j], pr[:, :, e], ALU.is_ge)
                after(last)

                def g(j, e):
                    return ge[:, pair[j, e], :]
                plan = [(g(0, 1), ALU.add, g(0, 2), ALU.add, g(0, 3), ALU.is_ge, 1.5),
                        (g(0, 1), ALU.subtract, g(1, 2), ALU.subtract, g(1, 3), ALU.is_le, -0.5),
                        (g(0, 2), ALU.add, g(1, 2), ALU.subtract, g(2, 3), ALU.is_le, 0.5),
                        (g(0, 3), ALU.add, g(1, 3), ALU.add, g(2, 3), ALU.is_le, 1.5)]
                for e, (x0, op0, x1, op1, x2, cmp, at) in enumerate(plan):
                    last = nc.vector.tensor_tensor(ra[:, e, :], x0, x1, op0)
                after(last)
                for e, (x0, op0, x1, op1, x2, cmp, at) in enumerate(plan):
                    last = nc.vector.tensor_tensor(rc[:, e, :], ra[:, e, :], x2, op1)
                after(last)
                for e, (x0, op0, x1, op1, x2, cmp, at) in enumerate(plan):
                    last = nc.vector.scalar_tensor_tensor(kept[:, :, e], rc[:, e, :], at, pr[:, :, e], cmp, ALU.mult)
                after(last)
                after(nc.vector.reduce_sum(ksum[:], kept[:], axis=AX.X))
                after(nc.vector.reciprocal(kinv[:], ksum[:]))
                after(nc.vector.tensor_tensor(comb[:], kept[:], bcast(kinv[:], EXPERTS), ALU.mult))
                assert k == RSTEPS, k

            def chunk(l, c, n, s):
                renew = closes(c) and not ends(l, c)
                splits(n, 0)
                if not begins(n):
                    add_expert(n - 1, EXPERTS - 1, 1 - s)
                    statistics(n - 1, 1 - s)
                splits(n, 1)
                if not begins(n):
                    moments(n - 1)
                    route(n - 1, before(c), l if opens(c) else (l + 1) % LAYERS)
                splits(n, 2)
                if opens(c):
                    weights(l)
                take_weights(n, c)
                if not ends(l, c):
                    norm(n + 1, following(c), 1 - s)
                add_expert(n, 0, s)
                if not begins(n):
                    keep_moments(n - 1, before(c))
                splits(n, 3)
                if not ends(l, c):
                    turned_low(n + 1)
                add_expert(n, 1, s)
                if renew:
                    dve.wait_ge(w_in, LOADS * (l + 1))
                    for e in range(EXPERTS):
                        split_w1(l + 1, e)
                add_expert(n, 2, s)
                if renew:
                    dve.wait_ge(yT_ready, EXPERTS * (n + 1))
                    biases(l + 1)

            dve.wait_ge(small_in, 16 * NSMALL)
            nc.vector.tensor_scalar(vareps[:], mv[:, :, 1], MOE_EPS, None, ALU.add).then_inc(var_ready, 1)
            dve.wait_ge(rows_turned, 2)
            dve.wait_ge(rstd_ready, 1)
            norm(0, 0, 0)
            turned_low(0)
            for e in range(EXPERTS):
                split_w1(0, e)
            biases(0)
            layers(dve, lambda l: chunks(dve, l, chunk))
            add_expert(LAYERS * NCH - 1, EXPERTS - 1, 1)

        @block.tensor
        def _(pe):
            def turn(n):
                pe.wait_ge(xh_ready, n + 1)
                wait(pe, freshT_ready, n - 1)
                for t in range(CHUNK):
                    last = nc.tensor.transpose(TR[:, t * P:(t + 1) * P], xh[:, t, :], st.eye[:])
                last.then_inc(xh_ps, 1)

            def up(n, e):
                for f in range(FT):
                    wait(pe, h_ready, PER * n + (e - 1) * FT + f + 1)
                    cols = slice(f * P, (f + 1) * P)
                    nc.tensor.matmul(U[f], w1[0][:, e, cols], xhT[0][:], start=True, stop=False)
                    nc.tensor.matmul(U[f], w1[0][:, e, cols], xhT[1][:], start=False, stop=False)
                    nc.tensor.matmul(U[f], w1[1][:, e, cols], xhT[0][:], start=False, stop=True).then_inc(up_ps, 1)

            def down(n, e):
                wait(pe, yT_ready, EXPERTS * n + e)
                for f in range(FT):
                    pe.wait_ge(h_low[f // HALF], EXPERTS * n + e + 1)
                    high, low = (x[:, e % 2, f, :] for x in hs)
                    nc.tensor.matmul(YT, w2[0][:, e, f, :], high, start=(f == 0), stop=False)
                    nc.tensor.matmul(YT, w2[0][:, e, f, :], low, start=False, stop=False)
                    last = nc.tensor.matmul(YT, w2[1][:, e, f, :], high, start=False, stop=(f == FT - 1))
                last.then_inc(yT_ps, 1)

            def back(n, e):
                pe.wait_ge(yT_ready, EXPERTS * n + e + 1)
                wait(pe, y_taken, EXPERTS * n + e)
                for t in range(CHUNK):
                    last = nc.tensor.transpose(Y[:, t * P:(t + 1) * P], yT[:, e % 2, t * P:(t + 1) * P], st.eye[:])
                last.then_inc(y_ps, 1)

            def turn_fresh(n, s):
                pe.wait_ge(y_taken, EXPERTS * (n + 1))
                pe.wait_ge(xhT_ready, n + 2)
                for t in range(CHUNK):
                    last = nc.tensor.transpose(TR[:, t * P:(t + 1) * P], cur[:, s, t, :], st.eye[:])
                last.then_inc(fresh_ps, 1)

            def route(n, l):
                pe.wait_ge(freshT_ready, n + 1)
                for t in range(CHUNK):
                    last = nc.tensor.matmul(RT[:, t * EXPERTS:(t + 1) * EXPERTS], freshT[:, t, :],
                                            rw[:, ds(l, 1), :].rearrange("p o e -> p (o e)"), start=True, stop=True)
                last.then_inc(logits_ps, 1)

            def offsets(l):
                for e in range(EXPERTS):
                    for f in range(FT):
                        last = nc.tensor.matmul(RT[:, e * FT + f:e * FT + f + 1], w1_raw[:, e, f * P:(f + 1) * P],
                                                gbT[:, ds(LE + l * EXPERTS + e, 1)], start=True, stop=True)
                last.then_inc(bias_ps, 1)

            def chunk(l, c, n, s):
                pe.wait_ge(xhT_ready, n + 1)
                if opens(c):
                    pe.wait_ge(w1_ready, EXPERTS * (l + 1))
                up(n, 0)
                if not begins(n):
                    back(n - 1, EXPERTS - 1)
                up(n, 1)
                if opens(c):
                    pe.wait_ge(w2_ready, EXPERTS * (l + 1))
                    pe.wait_ge(bias_ready, l + 1)
                down(n, 0)
                if not begins(n):
                    turn_fresh(n - 1, 1 - s)
                up(n, 2)
                if not begins(n):
                    route(n - 1, l if opens(c) else (l + 1) % LAYERS)
                back(n, 0)
                down(n, 1)
                up(n, 3)
                down(n, 2)
                back(n, 1)
                if not ends(l, c):
                    turn(n + 1)
                down(n, 3)
                back(n, 2)
                if closes(c) and not ends(l, c):
                    pe.wait_ge(w_in, LOADS * (l + 1))
                    pe.wait_ge(logits_ready, n)
                    offsets(l + 1)

            pe.wait_ge(small_in, 16 * NSMALL)
            nc.tensor.transpose(TR[:, 0:LE * FT], b1_rows[:], st.eye[0:LE * FT, 0:LE * FT])
            nc.tensor.transpose(TR[:, LE * FT:LE * FT + 3 * LE], gb_rows[:],
                                st.eye[0:3 * LE, 0:3 * LE]).then_inc(rows_ps, 1)
            pe.wait_ge(rows_turned, 2)
            turn(0)
            offsets(0)
            layers(pe, lambda l: chunks(pe, l, chunk))
            back(LAYERS * NCH - 1, EXPERTS - 1)

    tmp.close()


def finish(nc, a, st, out, ctx):
    def sem(name):
        return ctx.enter_context(nc.semaphore(name))

    tmp = ExitStack()

    def sb(name, shape, dt=F32):
        return tmp.enter_context(nc.sbuf_tensor(name, shape, dt))

    D = HEADS * VD
    KT = D // P
    N = TILES // CHUNK
    w_p = sb("fi_w_p", [P, KT, C])
    o = sb("fi_o", [P, 2, CHUNK, D])
    oT = sb("fi_oT", [P, 2, KT, P])
    x = sb("fi_x", [P, 2, CHUNK, C])
    part = sb("fi_part", [P, 2, CHUNK, C])
    res = sb("fi_res", [P, 2, CHUNK, C])

    w_in = sem("fi_w_in")
    o_in = [sem(f"fi_o_in{s}") for s in range(2)]
    turned_ps = sem("fi_turned_ps")
    turned = sem("fi_turned")
    y_ps = sem("fi_y_ps")
    added = sem("fi_added")
    res_ready = sem("fi_res_ready")
    stored = [sem(f"fi_stored{s}") for s in range(2)]
    x_dram = a["x"].rearrange("b (h p) c -> p (b h) c", p=P)
    out_dram = out.rearrange("b (h p) c -> p (b h) c", p=P)
    o_dram = st.d_o.rearrange("t p n -> p t n")

    with nc.Block() as block:

        @block.sync
        def _(sp):
            def load(g, s):
                sp.dma_start(o[:, s], o_dram[:, ds(g * CHUNK, CHUNK), :]).then_inc(o_in[s], 16)
                sp.dma_start(x[:, s], x_dram[:, ds(g * CHUNK, CHUNK), :]).then_inc(o_in[s], 16)

            sp.dma_start(w_p[:], a["w_proj"].rearrange("(k p) c -> p k c", p=P)).then_inc(w_in, 16)
            for s in range(2):
                sp.sem_inc(stored[s], 16)
            load(0, 0)
            load(1, 1)
            with sp.Fori(0, N // 2 - 1) as i:
                for s in range(2):
                    g = 2 * i + s
                    sp.wait_ge(res_ready, g + 1)
                    load(g + 2, s)
                    sp.dma_start(out_dram[:, ds(g * CHUNK, CHUNK), :], res[:, s]).then_inc(stored[s], 16)
            for s in range(2):
                g = N - 2 + s
                sp.wait_ge(res_ready, g + 1)
                sp.dma_start(out_dram[:, ds(g * CHUNK, CHUNK), :], res[:, s]).then_inc(stored[s], 16)
            for s in range(2):
                sp.wait_ge(stored[s], 16 * (N // 2 + 1))

        @block.scalar
        def _(act):
            with act.Fori(0, N // 2) as i:
                for s in range(2):
                    for t in range(CHUNK):
                        m = (2 * i + s) * CHUNK + t
                        act.wait_ge(turned_ps, m + 1)
                        nc.scalar.activation(oT[:, t % 2].rearrange("p k n -> p (k n)"), st.bank[t % 2],
                                             ACT.Copy).then_inc(turned, 1)

        @block.vector
        def _(dve):
            with dve.Fori(0, N // 2) as i:
                for s in range(2):
                    g = 2 * i + s
                    dve.wait_ge(y_ps, g + 1)
                    nc.vector.tensor_tensor(part[:, s], st.bank[2 + s].rearrange("p (t c) -> p t c", c=C),
                                            st.state[:, ds(g * CHUNK, CHUNK), :], ALU.add).then_inc(added, 1)
                    dve.wait_ge(added, g + 1)
                    dve.wait_ge(stored[s], 16 * (i + 1))
                    nc.vector.tensor_tensor(res[:, s], part[:, s], x[:, s], ALU.add).then_inc(res_ready, 1)

        @block.tensor
        def _(pe):
            pe.wait_ge(w_in, 16)

            def turn(m, s, t):
                for k in range(KT):
                    last = nc.tensor.transpose(st.bank[t % 2][:, k * P:(k + 1) * P], o[:, s, t, k * P:(k + 1) * P],
                                               st.eye[:])
                last.then_inc(turned_ps, 1)

            with pe.Fori(0, N // 2) as i:
                for s in range(2):
                    g = 2 * i + s
                    pe.wait_ge(o_in[s], 32 * (i + 1))
                    turn(g * CHUNK, s, 0)
                    for t in range(CHUNK):
                        if t + 1 < CHUNK:
                            if t > 0:
                                pe.wait_ge(turned, g * CHUNK + t)
                            turn(g * CHUNK + t + 1, s, t + 1)
                        pe.wait_ge(turned, g * CHUNK + t + 1)
                        for k in range(KT):
                            last = nc.tensor.matmul(st.bank[2 + s][:, t * C:(t + 1) * C], oT[:, t % 2, k, :],
                                                    w_p[:, k, :], start=(k == 0), stop=(k == KT - 1))
                    last.then_inc(y_ps, 1)

    tmp.close()


def program(nc, a, out):
    st = Store()
    with ExitStack() as ctx:
        def sb(stack, name, shape, dt=F32):
            return stack.enter_context(nc.sbuf_tensor(name, shape, dt))

        def dram(name, shape):
            return nc.dram_tensor(f"d_{name}", shape, F32, kind="Internal").ap()

        st.psum = ctx.enter_context(nc.psum_tensor("psum", [P, 8, 512], F32))
        st.bank = [st.psum[:, k, :] for k in range(8)]
        st.eye = sb(ctx, "eye", [P, P])
        st.d_xn = dram("xn", [TILES, P, C])
        st.d_xnT = dram("xnT", [B, P, T])
        st.d_kvT = dram("kvT", [B, P, T])
        st.d_nqT = dram("nqT", [B, QL, T])
        st.d_ks = dram("ks", [NQ, HD, QUAD * KEEP])
        st.d_vs = dram("vs", [NQ, P, QUAD * (VD + 1)])
        st.d_o = dram("o", [TILES, P, HEADS * VD])

        st.logits = sb(ctx, "logits", [P, TILES, EXPERTS])
        st.mv = sb(ctx, "mv", [P, TILES, 2])
        st.state = sb(ctx, "state", [P, TILES, C])
        st.w1_raw = sb(ctx, "w1_raw", [P, EXPERTS, FF])
        st.w2_raw = sb(ctx, "w2_raw", [P, EXPERTS, FT, C])

        with ExitStack() as att:
            st.eye16 = sb(att, "eye16", [P, P], BF16)
            st.causal = sb(att, "causal", [P, P], BF16)
            st.cos = sb(att, "cos", [P, HALVES, ROPE])
            st.sin = sb(att, "sin", [P, HALVES, ROPE])
            st.w_q_parts = [sb(att, f"w_q_{k}", [QL, HEADS, QW], F32R) for k in ("high", "low")]
            st.w_kw_parts = [sb(att, f"w_kw_{k}", [P, HEADS, HD], F32R) for k in ("high", "low")]
            st.w_vw = sb(att, "w_vw", [P, HEADS * VD])
            st.w_v1 = sb(att, "w_v1", [P, HEADS * VD])
            st.gates = sb(att, "gates", [P, B, 3])
            with ExitStack() as pre:
                st.rb0 = sb(pre, "rb0", [P, EXPERTS])
                st.w_all = sb(pre, "w_all", [P, CALL])
                st.w_q = sb(pre, "w_q", [QL, HEADS, QW])
                st.w_kw = sb(pre, "w_kw", [P, HEADS, HD])
                st.w_ks = sb(pre, "w_ks", [P, HEADS, HD])
                st.w_vs = sb(pre, "w_vs", [P, HEADS * VD])
                st.cos_sel = sb(pre, "cos_sel", [P, ROPE])
                st.sin_sel = sb(pre, "sin_sel", [P, ROPE])
                st.iota = sb(pre, "iota", [P, KEEP])
                st.imp = sb(pre, "imp", [P, HALVES, B])
                st.gl = sb(pre, "gl", [P, HALVES, B, 3])
                st.place = sb(pre, "place", [P, B, HALVES])
                setup(nc, a, st, ctx)
                tokens(nc, a, st, ctx)
                choose(nc, a, st, ctx)
                selected(nc, a, st, ctx)
            attention(nc, a, st, ctx)
        experts(nc, a, st, ctx)
        finish(nc, a, st, out, ctx)


_INS = ["x", "w_cq", "g_qnorm", "w_dq_nope", "w_dq_rope", "w_ckv", "g_kvnorm", "w_dk_nope", "w_dv", "w_krope",
        "w_imp", "w_selk", "w_selv", "w_wink", "w_winv", "w_gate", "w_proj"]
_MOE = ["router_w", "router_b", "ln_g", "ln_b", "w1", "b1", "w2", "b2"]


def kernel(**inputs):
    import concourse.bacc as bacc
    from concourse.bass_utils import run_bass_kernel_spmd

    nc = bacc.Bacc("TRN2", target_bir_lowering=False, num_devices=1)
    arrays = {n: np.ascontiguousarray(inputs[f"L0_attn_{n}"]) for n in _INS}
    arrays.update({n: np.ascontiguousarray(inputs[f"L0_ffn_{n}"]) for n in _MOE})
    arrays.update(shape_constants())
    a = {n: nc.dram_tensor(n, v.shape, mybir.dt.from_np(v.dtype), kind="ExternalInput").ap()
         for n, v in arrays.items()}
    out = nc.dram_tensor("out", (B, T, C), F32, kind="ExternalOutput").ap()
    program(nc, a, out)
    r = run_bass_kernel_spmd(nc, [arrays], core_ids=[0])
    return r.results[0]["out"]
```
